# Optimizing a Trainium2 kernel written in Bass

```python
import numpy as np
import jax
import jax.numpy as jnp

def _softmax(x, axis=-1):
    return jax.nn.softmax(x, axis=axis)

def _gelu(x):
    return jax.nn.gelu(x, approximate=True)

def _silu(x):
    return jax.nn.silu(x)

def _sigmoid(x):
    return jax.nn.sigmoid(x)

def _layernorm(x, axis=-1, eps=1e-05):
    m = jnp.mean(x, axis=axis, keepdims=True)
    v = jnp.var(x, axis=axis, keepdims=True)
    return (x - m) / jnp.sqrt(v + eps)

def _scatter_add(tgt, idx, src, axis=0):
    return tgt.at[idx].add(src)

def _segment_sum(src, seg, n):
    return jax.ops.segment_sum(src, seg, n)
kernel_name = 'mk_adaln_d2_jaxref_r8_fb59f9'

def setup_inputs(seed: int=0):
    np.random.seed(seed)
    _w = jnp.asarray

    def _L0_attn_setup():
        import jax, jax.numpy as jnp
        import numpy as np
        B, T, D = (2, 256, 128)
        H = 16
        DH = D // H
        C = 128
        ROPE_BASE = 10000.0

        def _rope_cos_sin(t_len, d_head, dtype):
            inv_freq = 1.0 / ROPE_BASE ** (jnp.arange(0, d_head, 2, dtype=jnp.float32) / d_head)
            freqs = jnp.arange(t_len, dtype=jnp.float32)[:, None] * inv_freq[None, :]
            emb = jnp.concatenate([freqs, freqs], axis=-1)
            return (jnp.cos(emb).astype(dtype), jnp.sin(emb).astype(dtype))

        def _rotate_half(x):
            x1, x2 = jnp.split(x, 2, axis=-1)
            return jnp.concatenate([-x2, x1], axis=-1)

        def _apply_rope(x, cos, sin):
            return x * cos[None, None] + _rotate_half(x) * sin[None, None]
        key = jax.random.key(seed)
        ks = jax.random.split(key, 12)
        s = 0.02
        return {'x': jax.random.normal(ks[0], (B, T, D), dtype=jnp.float32), 'w_dk': jax.random.normal(ks[1], (D, C), dtype=jnp.float32) * s, 'b_dk': jnp.zeros((C,), dtype=jnp.float32), 'w_dv': jax.random.normal(ks[2], (D, C), dtype=jnp.float32) * s, 'b_dv': jnp.zeros((C,), dtype=jnp.float32), 'w_uk': jax.random.normal(ks[3], (C, D), dtype=jnp.float32) * s, 'b_uk': jnp.zeros((D,), dtype=jnp.float32), 'w_uv': jax.random.normal(ks[4], (C, D), dtype=jnp.float32) * s, 'b_uv': jnp.zeros((D,), dtype=jnp.float32), 'w_o': jax.random.normal(ks[5], (D, D), dtype=jnp.float32) * s, 'b_o': jnp.zeros((D,), dtype=jnp.float32)}
    _L0_attn_in = _L0_attn_setup()

    def _L0_ffn_setup():
        import jax, jax.numpy as jnp
        import numpy as np
        E = 8
        JITTER = 0.01

        def _sparse_mixer_routing(logits):
            top_vals, top_idx = jax.lax.top_k(logits, 2)
            eidx = jnp.arange(logits.shape[-1])

            def _multiplier(thr, base_logits, idx):
                factor = jnp.maximum(jnp.abs(logits), thr)
                mask = (thr - logits) / factor > 2.0 * JITTER
                probs = jax.nn.softmax(jnp.where(mask, -jnp.inf, base_logits), axis=-1)
                return jnp.take_along_axis(probs, idx, axis=-1)
            mult1 = _multiplier(top_vals[:, :1], logits, top_idx[:, :1])
            scat = jnp.where(eidx[None, :] == top_idx[:, :1], -jnp.inf, logits)
            mult2 = _multiplier(top_vals[:, 1:2], scat, top_idx[:, 1:2])
            return (jnp.concatenate([mult1, mult2], axis=-1), top_idx)
        key = jax.random.key(seed)
        ks = jax.random.split(key, 5)
        H, F = (128, 512)
        scale = 0.02
        return {'hidden_states': jax.random.normal(ks[0], (1, 256, H), jnp.float32), 'gate_w': jax.random.normal(ks[1], (H, E), jnp.float32) * scale, 'w1': jax.random.normal(ks[2], (E, H, F), jnp.float32) * scale, 'w2': jax.random.normal(ks[3], (E, F, H), jnp.float32) * scale, 'w3': jax.random.normal(ks[4], (E, H, F), jnp.float32) * scale}
    _L0_ffn_in = _L0_ffn_setup()
    _L0_c = _w((lambda *s: np.random.randn(*s).astype(np.float32) * 0.05)(32, 128))
    _L0_wmod = _w((lambda *s: np.random.randn(*s).astype(np.float32) * 0.05)(128, 6 * 128) * 128 ** (-0.5))

    def _L1_attn_setup():
        import jax, jax.numpy as jnp
        import numpy as np
        EMB, DS, DC, EXP, GRID = (128, 16, 4, 2, 8)
        DI = EXP * EMB
        DTR = EMB // 16
        B, L = (2, 128)
        EPS = 1e-12

        def _silu(v):
            return v * jax.nn.sigmoid(v)

        def _layernorm(v, g, b):
            mu = jnp.mean(v, axis=-1, keepdims=True)
            var = jnp.mean(jnp.square(v - mu), axis=-1, keepdims=True)
            return (v - mu) * jax.lax.rsqrt(var + EPS) * g + b

        def _mamba(x, in_w, conv_w, conv_b, xproj_w, dt_w, dt_b, A_log, D, out_w):
            xz = jnp.einsum('ble,ie->bli', x, in_w)
            xc, z = jnp.split(xz, 2, axis=-1)
            xt = jnp.transpose(xc, (0, 2, 1))
            xt = jax.lax.conv_general_dilated(xt, conv_w[:, None, :], (1,), [(DC - 1, 0)], feature_group_count=DI)
            xc = _silu(jnp.transpose(xt, (0, 2, 1)) + conv_b)
            x_dbl = jnp.einsum('bld,rd->blr', xc, xproj_w)
            dt, Bm, Cm = jnp.split(x_dbl, [DTR, DTR + DS], axis=-1)
            dt = jax.nn.softplus(jnp.einsum('blr,dr->bld', dt, dt_w) + dt_b)
            A = -jnp.exp(A_log)
            dA = jnp.exp(dt[..., None] * A)
            dBx = dt[..., None] * Bm[:, :, None, :] * xc[..., None]

            def step(h, inp):
                dA_t, dBx_t, C_t = inp
                h = dA_t * h + dBx_t
                y = jnp.einsum('bds,bs->bd', h, C_t)
                return (h, y)
            h0 = jnp.zeros((x.shape[0], DI, DS), x.dtype)
            _, ys = jax.lax.scan(step, h0, (jnp.transpose(dA, (1, 0, 2, 3)), jnp.transpose(dBx, (1, 0, 2, 3)), jnp.transpose(Cm, (1, 0, 2))))
            y = jnp.transpose(ys, (1, 0, 2)) + xc * D
            y = y * _silu(z)
            return jnp.einsum('bld,ed->ble', y, out_w)

        def _fourier_kan(v, coef):
            shp = v.shape
            vf = v.reshape(-1, shp[-1])
            k = jnp.arange(1, GRID + 1, dtype=v.dtype)
            arg = vf[:, :, None] * k
            y = jnp.einsum('nik,jik->nj', jnp.cos(arg), coef[0]) + jnp.einsum('nik,jik->nj', jnp.sin(arg), coef[1])
            return y.reshape(shp[:-1] + (coef.shape[1],))
        key = jax.random.key(seed)
        ks = jax.random.split(key, 16)
        n = lambda k, shp, s=0.02: jax.random.normal(k, shp, jnp.float32) * s
        A_log = jnp.tile(jnp.log(jnp.arange(1, DS + 1, dtype=jnp.float32))[None, :], (DI, 1))
        return {'x': jax.random.normal(ks[0], (B, L, EMB), jnp.float32), 'in_proj_w': n(ks[1], (2 * DI, EMB)), 'out_proj_w': n(ks[2], (EMB, DI)), 'conv_w_f': n(ks[3], (DI, DC), 0.1), 'conv_b_f': jnp.zeros((DI,), jnp.float32), 'x_proj_w_f': n(ks[4], (DTR + 2 * DS, DI)), 'dt_w_f': n(ks[5], (DI, DTR), 0.1), 'dt_b_f': jax.random.uniform(ks[6], (DI,), jnp.float32, -4.0, -2.0), 'A_log_f': A_log, 'D_f': jnp.ones((DI,), jnp.float32), 'conv_w_b': n(ks[7], (DI, DC), 0.1), 'conv_b_b': jnp.zeros((DI,), jnp.float32), 'x_proj_w_b': n(ks[8], (DTR + 2 * DS, DI)), 'dt_w_b': n(ks[9], (DI, DTR), 0.1), 'dt_b_b': jax.random.uniform(ks[10], (DI,), jnp.float32, -4.0, -2.0), 'A_log_b': A_log, 'D_b': jnp.ones((DI,), jnp.float32), 'ln1_g': jnp.ones((EMB,), jnp.float32), 'ln1_b': jnp.zeros((EMB,), jnp.float32), 'ln_g': jnp.ones((EMB,), jnp.float32), 'ln_b': jnp.zeros((EMB,), jnp.float32), 'kan_coef': jax.random.normal(ks[11], (2, EMB, EMB, GRID), jnp.float32) / (np.sqrt(EMB) * np.sqrt(GRID))}
    _L1_attn_in = _L1_attn_setup()

    def _L1_ffn_setup():
        import jax, jax.numpy as jnp
        import numpy as np
        NUM_EXPERTS = 8
        CAPACITY = 80
        key = jax.random.key(seed)
        ks = jax.random.split(key, 5)
        D, E, F = (128, NUM_EXPERTS, 512)
        inputs = jax.random.normal(ks[0], (2, 256, D), dtype=jnp.float32)
        gate_w = jax.random.normal(ks[1], (D, E), dtype=jnp.float32) * 0.02
        gate_b = jnp.zeros((E,), dtype=jnp.float32)
        w1 = jax.random.normal(ks[2], (E, D, F), dtype=jnp.float32) * 0.02
        b1 = jnp.zeros((E, F), dtype=jnp.float32)
        w2 = jax.random.normal(ks[3], (E, F, D), dtype=jnp.float32) * 0.02
        b2 = jnp.zeros((E, D), dtype=jnp.float32)
        return {'inputs': inputs, 'gate_w': gate_w, 'gate_b': gate_b, 'w1': w1, 'b1': b1, 'w2': w2, 'b2': b2}
    _L1_ffn_in = _L1_ffn_setup()
    _L1_c = _w((lambda *s: np.random.randn(*s).astype(np.float32) * 0.05)(32, 128))
    _L1_wmod = _w((lambda *s: np.random.randn(*s).astype(np.float32) * 0.05)(128, 6 * 128) * 128 ** (-0.5))
    _d = {'L0_attn_x': _L0_attn_in['x'], 'L0_attn_w_dk': _L0_attn_in['w_dk'], 'L0_attn_b_dk': _L0_attn_in['b_dk'], 'L0_attn_w_dv': _L0_attn_in['w_dv'], 'L0_attn_b_dv': _L0_attn_in['b_dv'], 'L0_attn_w_uk': _L0_attn_in['w_uk'], 'L0_attn_b_uk': _L0_attn_in['b_uk'], 'L0_attn_w_uv': _L0_attn_in['w_uv'], 'L0_attn_b_uv': _L0_attn_in['b_uv'], 'L0_attn_w_o': _L0_attn_in['w_o'], 'L0_attn_b_o': _L0_attn_in['b_o'], 'L0_ffn_gate_w': _L0_ffn_in['gate_w'], 'L0_ffn_w1': _L0_ffn_in['w1'], 'L0_ffn_w2': _L0_ffn_in['w2'], 'L0_ffn_w3': _L0_ffn_in['w3'], 'L0_c': _L0_c, 'L0_wmod': _L0_wmod, 'L1_attn_in_proj_w': _L1_attn_in['in_proj_w'], 'L1_attn_out_proj_w': _L1_attn_in['out_proj_w'], 'L1_attn_conv_w_f': _L1_attn_in['conv_w_f'], 'L1_attn_conv_b_f': _L1_attn_in['conv_b_f'], 'L1_attn_x_proj_w_f': _L1_attn_in['x_proj_w_f'], 'L1_attn_dt_w_f': _L1_attn_in['dt_w_f'], 'L1_attn_dt_b_f': _L1_attn_in['dt_b_f'], 'L1_attn_A_log_f': _L1_attn_in['A_log_f'], 'L1_attn_D_f': _L1_attn_in['D_f'], 'L1_attn_conv_w_b': _L1_attn_in['conv_w_b'], 'L1_attn_conv_b_b': _L1_attn_in['conv_b_b'], 'L1_attn_x_proj_w_b': _L1_attn_in['x_proj_w_b'], 'L1_attn_dt_w_b': _L1_attn_in['dt_w_b'], 'L1_attn_dt_b_b': _L1_attn_in['dt_b_b'], 'L1_attn_A_log_b': _L1_attn_in['A_log_b'], 'L1_attn_D_b': _L1_attn_in['D_b'], 'L1_attn_ln1_g': _L1_attn_in['ln1_g'], 'L1_attn_ln1_b': _L1_attn_in['ln1_b'], 'L1_attn_ln_g': _L1_attn_in['ln_g'], 'L1_attn_ln_b': _L1_attn_in['ln_b'], 'L1_attn_kan_coef': _L1_attn_in['kan_coef'], 'L1_ffn_gate_w': _L1_ffn_in['gate_w'], 'L1_ffn_gate_b': _L1_ffn_in['gate_b'], 'L1_ffn_w1': _L1_ffn_in['w1'], 'L1_ffn_b1': _L1_ffn_in['b1'], 'L1_ffn_w2': _L1_ffn_in['w2'], 'L1_ffn_b2': _L1_ffn_in['b2'], 'L1_c': _L1_c, 'L1_wmod': _L1_wmod}
    _x0 = _d['L0_attn_x']
    _d['L0_attn_x'] = jax.random.normal(jax.random.fold_in(jax.random.key(seed), 1), (32, 256, 128), dtype=_x0.dtype)
    del _x0
    return _d

def reference(L0_attn_x, L0_attn_w_dk, L0_attn_b_dk, L0_attn_w_dv, L0_attn_b_dv, L0_attn_w_uk, L0_attn_b_uk, L0_attn_w_uv, L0_attn_b_uv, L0_attn_w_o, L0_attn_b_o, L0_ffn_gate_w, L0_ffn_w1, L0_ffn_w2, L0_ffn_w3, L0_c, L0_wmod, L1_attn_in_proj_w, L1_attn_out_proj_w, L1_attn_conv_w_f, L1_attn_conv_b_f, L1_attn_x_proj_w_f, L1_attn_dt_w_f, L1_attn_dt_b_f, L1_attn_A_log_f, L1_attn_D_f, L1_attn_conv_w_b, L1_attn_conv_b_b, L1_attn_x_proj_w_b, L1_attn_dt_w_b, L1_attn_dt_b_b, L1_attn_A_log_b, L1_attn_D_b, L1_attn_ln1_g, L1_attn_ln1_b, L1_attn_ln_g, L1_attn_ln_b, L1_attn_kan_coef, L1_ffn_gate_w, L1_ffn_gate_b, L1_ffn_w1, L1_ffn_b1, L1_ffn_w2, L1_ffn_b2, L1_c, L1_wmod):

    def _L0_attn_ref(x, w_dk, b_dk, w_dv, b_dv, w_uk, b_uk, w_uv, b_uv, w_o, b_o):
        import jax, jax.numpy as jnp
        import numpy as np
        B, T, D = (2, 256, 128)
        H = 16
        DH = D // H
        C = 128
        ROPE_BASE = 10000.0

        def _rope_cos_sin(t_len, d_head, dtype):
            inv_freq = 1.0 / ROPE_BASE ** (jnp.arange(0, d_head, 2, dtype=jnp.float32) / d_head)
            freqs = jnp.arange(t_len, dtype=jnp.float32)[:, None] * inv_freq[None, :]
            emb = jnp.concatenate([freqs, freqs], axis=-1)
            return (jnp.cos(emb).astype(dtype), jnp.sin(emb).astype(dtype))

        def _rotate_half(x):
            x1, x2 = jnp.split(x, 2, axis=-1)
            return jnp.concatenate([-x2, x1], axis=-1)

        def _apply_rope(x, cos, sin):
            return x * cos[None, None] + _rotate_half(x) * sin[None, None]
        Bx, Tx, Dx = x.shape
        c_k = x @ w_dk + b_dk
        c_v = x @ w_dv + b_dv
        k = c_k @ w_uk + b_uk
        v = c_v @ w_uv + b_uv

        def split_heads(t):
            return t.reshape(Bx, Tx, H, DH).transpose(0, 2, 1, 3)
        q = split_heads(x)
        k = split_heads(k)
        v = split_heads(v)
        cos, sin = _rope_cos_sin(Tx, DH, x.dtype)
        q = _apply_rope(q, cos, sin)
        k = _apply_rope(k, cos, sin)
        scale = 1.0 / np.sqrt(DH)
        attn = jnp.einsum('bhid,bhjd->bhij', q, k) * scale
        attn = jax.nn.softmax(attn, axis=-1)
        out = jnp.einsum('bhij,bhjd->bhid', attn, v)
        out = out.transpose(0, 2, 1, 3).reshape(Bx, Tx, Dx)
        return out @ w_o + b_o

    def _L0_ffn_ref(hidden_states, gate_w, w1, w2, w3):
        import jax, jax.numpy as jnp
        import numpy as np
        E = 8
        JITTER = 0.01

        def _sparse_mixer_routing(logits):
            top_vals, top_idx = jax.lax.top_k(logits, 2)
            eidx = jnp.arange(logits.shape[-1])

            def _multiplier(thr, base_logits, idx):
                factor = jnp.maximum(jnp.abs(logits), thr)
                mask = (thr - logits) / factor > 2.0 * JITTER
                probs = jax.nn.softmax(jnp.where(mask, -jnp.inf, base_logits), axis=-1)
                return jnp.take_along_axis(probs, idx, axis=-1)
            mult1 = _multiplier(top_vals[:, :1], logits, top_idx[:, :1])
            scat = jnp.where(eidx[None, :] == top_idx[:, :1], -jnp.inf, logits)
            mult2 = _multiplier(top_vals[:, 1:2], scat, top_idx[:, 1:2])
            return (jnp.concatenate([mult1, mult2], axis=-1), top_idx)
        B, S, H = hidden_states.shape
        x = hidden_states.reshape(-1, H)
        logits = x @ gate_w
        mult, sel = _sparse_mixer_routing(logits)
        w = jnp.sum(mult[:, :, None] * (sel[:, :, None] == jnp.arange(E)[None, None, :]), axis=1)
        h = jax.nn.silu(jnp.einsum('th,ehf->etf', x, w1)) * jnp.einsum('th,ehf->etf', x, w3)
        out = jnp.einsum('etf,efh,te->th', h, w2, w)
        return out.reshape(B, S, H)

    def _L1_attn_ref(x, in_proj_w, out_proj_w, conv_w_f, conv_b_f, x_proj_w_f, dt_w_f, dt_b_f, A_log_f, D_f, conv_w_b, conv_b_b, x_proj_w_b, dt_w_b, dt_b_b, A_log_b, D_b, ln1_g, ln1_b, ln_g, ln_b, kan_coef):
        import jax, jax.numpy as jnp
        import numpy as np
        EMB, DS, DC, EXP, GRID = (128, 16, 4, 2, 8)
        DI = EXP * EMB
        DTR = EMB // 16
        B, L = (2, 128)
        EPS = 1e-12

        def _silu(v):
            return v * jax.nn.sigmoid(v)

        def _layernorm(v, g, b):
            mu = jnp.mean(v, axis=-1, keepdims=True)
            var = jnp.mean(jnp.square(v - mu), axis=-1, keepdims=True)
            return (v - mu) * jax.lax.rsqrt(var + EPS) * g + b

        def _mamba(x, in_w, conv_w, conv_b, xproj_w, dt_w, dt_b, A_log, D, out_w):
            xz = jnp.einsum('ble,ie->bli', x, in_w)
            xc, z = jnp.split(xz, 2, axis=-1)
            xt = jnp.transpose(xc, (0, 2, 1))
            xt = jax.lax.conv_general_dilated(xt, conv_w[:, None, :], (1,), [(DC - 1, 0)], feature_group_count=DI)
            xc = _silu(jnp.transpose(xt, (0, 2, 1)) + conv_b)
            x_dbl = jnp.einsum('bld,rd->blr', xc, xproj_w)
            dt, Bm, Cm = jnp.split(x_dbl, [DTR, DTR + DS], axis=-1)
            dt = jax.nn.softplus(jnp.einsum('blr,dr->bld', dt, dt_w) + dt_b)
            A = -jnp.exp(A_log)
            dA = jnp.exp(dt[..., None] * A)
            dBx = dt[..., None] * Bm[:, :, None, :] * xc[..., None]

            def step(h, inp):
                dA_t, dBx_t, C_t = inp
                h = dA_t * h + dBx_t
                y = jnp.einsum('bds,bs->bd', h, C_t)
                return (h, y)
            h0 = jnp.zeros((x.shape[0], DI, DS), x.dtype)
            _, ys = jax.lax.scan(step, h0, (jnp.transpose(dA, (1, 0, 2, 3)), jnp.transpose(dBx, (1, 0, 2, 3)), jnp.transpose(Cm, (1, 0, 2))))
            y = jnp.transpose(ys, (1, 0, 2)) + xc * D
            y = y * _silu(z)
            return jnp.einsum('bld,ed->ble', y, out_w)

        def _fourier_kan(v, coef):
            shp = v.shape
            vf = v.reshape(-1, shp[-1])
            k = jnp.arange(1, GRID + 1, dtype=v.dtype)
            arg = vf[:, :, None] * k
            y = jnp.einsum('nik,jik->nj', jnp.cos(arg), coef[0]) + jnp.einsum('nik,jik->nj', jnp.sin(arg), coef[1])
            return y.reshape(shp[:-1] + (coef.shape[1],))
        out = _layernorm(x, ln1_g, ln1_b)
        out_f = _mamba(out, in_proj_w, conv_w_f, conv_b_f, x_proj_w_f, dt_w_f, dt_b_f, A_log_f, D_f, out_proj_w)
        out_b = _mamba(out[:, ::-1], in_proj_w, conv_w_b, conv_b_b, x_proj_w_b, dt_w_b, dt_b_b, A_log_b, D_b, out_proj_w)[:, ::-1]
        out = _layernorm(out_f + out_b, ln_g, ln_b)
        out = _fourier_kan(out, kan_coef)
        return out + x

    def _L1_ffn_ref(inputs, gate_w, gate_b, w1, b1, w2, b2):
        import jax, jax.numpy as jnp
        import numpy as np
        NUM_EXPERTS = 8
        CAPACITY = 80
        D = inputs.shape[-1]
        tokens = inputs.reshape(-1, D)
        logits = tokens @ gate_w + gate_b
        probs = jax.nn.softmax(logits, axis=-1)
        expert_idx = jnp.argmax(probs, axis=-1)
        mask1 = jax.nn.one_hot(expert_idx, NUM_EXPERTS, dtype=jnp.float32)
        pos = jnp.sum(jnp.cumsum(mask1, axis=0) * mask1, axis=-1) - 1.0
        pos = pos.astype(jnp.int32)
        keep = (pos < CAPACITY).astype(jnp.float32)
        gate_prob = jnp.sum(probs * mask1, axis=-1)
        pos_oh = jax.nn.one_hot(pos, CAPACITY, dtype=jnp.float32)
        sec_mask = mask1[:, :, None] * pos_oh[:, None, :] * keep[:, None, None]
        combine_weights = sec_mask * gate_prob[:, None, None]
        dispatch = jnp.einsum('nec,nd->ecd', sec_mask, tokens)
        h = jax.nn.gelu(jnp.einsum('ecd,edf->ecf', dispatch, w1) + b1[:, None, :])
        expert_out = jnp.einsum('ecf,efd->ecd', h, w2) + b2[:, None, :]
        out = jnp.einsum('nec,ecd->nd', combine_weights, expert_out)
        return out.reshape(inputs.shape)
    x = L0_attn_x
    mod = (_silu(L0_c) @ L0_wmod).reshape(L0_c.shape[0], 6, 1, -1)
    sa, ca, ga, sb, cb, gb = (mod[:, 0], mod[:, 1], mod[:, 2], mod[:, 3], mod[:, 4], mod[:, 5])
    ga = (2 * (ga >= 0) - 1) * jnp.maximum(jnp.abs(ga), 0.25)
    gb = (2 * (gb >= 0) - 1) * jnp.maximum(jnp.abs(gb), 0.25)
    h = _layernorm(x, axis=-1) * (1 + ca) + sa
    x = x + ga * _L0_attn_ref(h, L0_attn_w_dk, L0_attn_b_dk, L0_attn_w_dv, L0_attn_b_dv, L0_attn_w_uk, L0_attn_b_uk, L0_attn_w_uv, L0_attn_b_uv, L0_attn_w_o, L0_attn_b_o)
    h = _layernorm(x, axis=-1) * (1 + cb) + sb
    x = x + gb * _L0_ffn_ref(h, L0_ffn_gate_w, L0_ffn_w1, L0_ffn_w2, L0_ffn_w3)
    mod = (_silu(L1_c) @ L1_wmod).reshape(L1_c.shape[0], 6, 1, -1)
    sa, ca, ga, sb, cb, gb = (mod[:, 0], mod[:, 1], mod[:, 2], mod[:, 3], mod[:, 4], mod[:, 5])
    ga = (2 * (ga >= 0) - 1) * jnp.maximum(jnp.abs(ga), 0.25)
    gb = (2 * (gb >= 0) - 1) * jnp.maximum(jnp.abs(gb), 0.25)
    h = _layernorm(x, axis=-1) * (1 + ca) + sa
    x = x + ga * _L1_attn_ref(h, L1_attn_in_proj_w, L1_attn_out_proj_w, L1_attn_conv_w_f, L1_attn_conv_b_f, L1_attn_x_proj_w_f, L1_attn_dt_w_f, L1_attn_dt_b_f, L1_attn_A_log_f, L1_attn_D_f, L1_attn_conv_w_b, L1_attn_conv_b_b, L1_attn_x_proj_w_b, L1_attn_dt_w_b, L1_attn_dt_b_b, L1_attn_A_log_b, L1_attn_D_b, L1_attn_ln1_g, L1_attn_ln1_b, L1_attn_ln_g, L1_attn_ln_b, L1_attn_kan_coef)
    h = _layernorm(x, axis=-1) * (1 + cb) + sb
    x = x + gb * _L1_ffn_ref(h, L1_ffn_gate_w, L1_ffn_gate_b, L1_ffn_w1, L1_ffn_b1, L1_ffn_w2, L1_ffn_b2)
    return x

_drawn_inputs = setup_inputs


def setup_inputs(seed=0):
    import zlib

    import numpy as np

    out = dict(_drawn_inputs(seed))
    spreads = {'L0_attn_b_dk': (0.0, 0.8),
     'L0_attn_b_dv': (0.0, 0.8),
     'L0_attn_b_uk': (0.0, 0.8),
     'L0_attn_b_uv': (0.0, 0.763),
     'L0_attn_b_o': (0.0, 0.1),
     'L1_attn_conv_b_f': (0.0, 0.1),
     'L1_attn_D_f': (1.0, 0.2),
     'L1_attn_conv_b_b': (0.0, 0.1),
     'L1_attn_D_b': (1.0, 0.2),
     'L1_attn_ln1_g': (1.0, 0.2),
     'L1_attn_ln1_b': (0.0, 0.1),
     'L1_attn_ln_g': (1.0, 0.2),
     'L1_attn_ln_b': (0.0, 0.1),
     'L1_ffn_gate_b': (0.0, 0.8),
     'L1_ffn_b1': (0.0, 0.8),
     'L1_ffn_b2': (0.0, 0.8)}
    factors = {'L0_attn_w_dk': 8.0,
     'L0_attn_w_dv': 8.0,
     'L0_attn_w_uk': 8.0,
     'L0_attn_w_uv': 8.0,
     'L0_attn_w_o': 6.162,
     'L0_ffn_gate_w': 8.0,
     'L0_ffn_w1': 8.0,
     'L0_ffn_w2': 8.0,
     'L0_ffn_w3': 8.0,
     'L1_attn_x_proj_w_f': 8.0,
     'L1_attn_dt_w_f': 8.0,
     'L1_attn_dt_b_f': 8.0,
     'L1_attn_A_log_f': 8.0,
     'L1_attn_x_proj_w_b': 8.0,
     'L1_attn_dt_w_b': 8.0,
     'L1_attn_dt_b_b': 8.0,
     'L1_attn_A_log_b': 8.0,
     'L1_ffn_gate_w': 8.0,
     'L1_ffn_w1': 8.0,
     'L1_ffn_w2': 8.0}
    for name, (base, spread) in spreads.items():
        noise = np.random.default_rng([zlib.crc32(name.encode()), seed]).standard_normal(out[name].shape)
        drawn = base * np.exp(spread * noise) if base else spread * noise
        out[name] = jnp.asarray(drawn.astype(out[name].dtype))
    for name, factor in factors.items():
        out[name] = (out[name] * factor).astype(out[name].dtype)
    return out
```

```python
import numpy as np

import concourse.bass as bass
from concourse import mybir
from contextlib import ExitStack

P = 128
F32 = mybir.dt.float32
BF16 = mybir.dt.bfloat16
U32 = mybir.dt.uint32
I32 = mybir.dt.int32
ALU = mybir.AluOpType
ACT = mybir.ActivationFunctionType
AX = mybir.AxisListType
ds = bass.ds

T, D = 256, 128
TC = T // P
SHIFT_A, SCALE_A, GATE_A, SHIFT_B, SCALE_B, GATE_B = range(6)
LN_EPS = 1e-5


def at(eng, sem, count):
    if isinstance(count, int) and count <= 0:
        return
    eng.wait_ge(sem, count)


def at_alone(eng, sem, count, passed):
    at(eng, sem, count)
    if not isinstance(count, int):
        eng.sem_inc(passed, 1)


class Core:

    def __init__(self, nc, aps, B):
        self.nc, self.aps, self.B = nc, aps, B
        self.NT = B * TC
        self.stack = ExitStack()
        self.sems = []
        self.X = self.sbuf("resid_x", [P, max(self.NT * D, 8192)])
        self.mod = self.sbuf("mod_cols", [P, 2 * 6 * B])
        self.ident = self.sbuf("identity", [P, P])
        self.rstd = self.sbuf("rstd", [P, self.NT])
        self.nmr = self.sbuf("neg_mean_rstd", [P, self.NT])
        self.st = self.sbuf("bn_stats", [P, self.NT, 6])
        self.ln_tmp = [self.sbuf(f"ln_{n}", [P, self.NT]) for n in ("mean", "dmean", "var", "std")]
        self.modrow = nc.dram_tensor("mod_rows", [10, B, D], F32, kind="Internal").ap()

    def sbuf(self, name, shape, dt=F32, on=None):
        return (on or self.stack).enter_context(self.nc.sbuf_tensor(name, shape, dt))

    def psum(self, name, shape, dt=F32, on=None):
        return (on or self.stack).enter_context(self.nc.psum_tensor(name, shape, dt))

    def sem(self, name):
        self.sems.append(self.nc.alloc_semaphore(name=name))
        return self.sems[-1]

    def next_stage(self):
        self.nc.all_engine_barrier()
        self.nc.clear_and_free_semaphores(self.sems)
        self.nc.all_engine_barrier()
        self.sems = []

    def modcol(self, layer, kind, b):
        o = (layer * 6 + kind) * self.B
        return self.mod[:, ds(b + o, 1)]


class Chain:

    def __init__(self, core, eng, name, base=0):
        self.eng, self.sem, self.n = eng, core.sem(name), 0

    def step(self, ins):
        ins.then_inc(self.sem, 1)
        self.n += 1
        self.eng.wait_ge(self.sem, self.n)


def load_and_modulate(core):
    nc, B, aps = core.nc, core.B, core.aps
    on = ExitStack()
    with on:
        c = core.sbuf("c_rows", [2 * B, D], on=on)
        cs = core.sbuf("c_silu", [2 * B, D], on=on)
        cT = core.sbuf("c_silu_T", [P, 2 * B], on=on)
        w = core.sbuf("wmod", [P, 2, 6 * D], on=on)
        rows = core.sbuf("mod_rows_sb", [B, 10, D], on=on)
        sgn = core.sbuf("gate_sign", [P, 4 * D], on=on)
        psT = core.psum("m_psT", [P, 512], on=on)
        psC = core.psum("m_psC", [P, 512], on=on)
        psR = core.psum("m_psR", [P, 3, 512], on=on)
        s_x, s_in, s_silu = core.sem("x_loaded"), core.sem("mod_in_loaded"), core.sem("c_silu_ready")
        s_T, s_cT, s_mm, s_rows, s_out = core.sem("cT_ps"), core.sem("cT_ready"), core.sem("mod_ps"), core.sem("modrows_ready"), core.sem("modrows_stored")
        with nc.Block() as block:
            @block.sync
            def _(sp):
                for l, (cn, wn) in enumerate((("L0_c", "L0_wmod"), ("L1_c", "L1_wmod"))):
                    sp.dma_start(c[l * B:(l + 1) * B, :], aps[cn][0:B]).then_inc(s_in, 16)
                    sp.dma_start(w[:, l, :], aps[wn]).then_inc(s_in, 16)
                sp.dma_start(core.ident[:], aps["ident"]).then_inc(s_in, 16)
                half = core.NT // 2
                for k in range(2):
                    sp.dma_start(core.X[:, k * half * D:(k + 1) * half * D].rearrange("p (n d) -> p n d", d=D),
                                 aps["x_tiles"][k * half:(k + 1) * half].rearrange("n p d -> p n d")).then_inc(s_x, 16)
                sp.wait_ge(s_rows, 1)
                sp.dma_start(core.modrow.rearrange("k b d -> b k d"), rows[:]).then_inc(s_out, 16)
                sp.wait_ge(s_out, 16)
                sp.wait_ge(s_x, 32)

            @block.scalar
            def _(act):
                act.wait_ge(s_in, 80)
                nc.scalar.activation(cs[:], c[:], ACT.Silu).then_inc(s_silu, 1)

            @block.tensor
            def _(pe):
                pe.wait_ge(s_silu, 1)
                nc.tensor.transpose(psT[:, 0:2 * B], cs[:], core.ident[0:2 * B, 0:2 * B]).then_inc(s_T, 1)
                pe.wait_ge(s_cT, 1)
                for l in range(2):
                    for k in range(6):
                        o = (l * 6 + k) * B
                        nc.tensor.matmul(psC[:, o:o + B], w[:, l, k * D:(k + 1) * D], cT[:, l * B:(l + 1) * B],
                                         start=True, stop=True)
                for n, (l, k) in enumerate(((0, GATE_A), (0, GATE_B), (1, GATE_A), (1, GATE_B), (0, SHIFT_B), (0, SCALE_B), (1, SHIFT_B), (1, SCALE_B),
                                             (1, SHIFT_A), (1, SCALE_A))):
                    last = nc.tensor.matmul(psR[0:B, n // 4, (n % 4) * D:(n % 4 + 1) * D], cT[:, l * B:(l + 1) * B],
                                            w[:, l, k * D:(k + 1) * D], start=True, stop=True)
                last.then_inc(s_mm, 1)

            @block.vector
            def _(dve):
                chain = Chain(core, dve, "mod_dve_chain")
                dve.wait_ge(s_T, 1)
                nc.vector.tensor_copy(cT[:], psT[:, 0:2 * B]).then_inc(s_cT, 1)
                dve.wait_ge(s_mm, 1)
                chain.step(nc.vector.tensor_copy(core.mod[:], psC[:, 0:12 * B]))
                for l in range(2):
                    for k in (SCALE_A, SCALE_B):
                        o = (l * 6 + k) * B
                        nc.vector.tensor_scalar(core.mod[:, o:o + B], core.mod[:, o:o + B], 1.0, None, ALU.add)
                chain.step(nc.vector.tensor_scalar(sgn[0:B, :], psR[0:B, 0, :], 0.0, None, ALU.is_ge))
                chain.step(nc.vector.tensor_scalar(sgn[0:B, :], sgn[0:B, :], 2.0, -1.0, ALU.mult, ALU.add))
                for k in range(3):
                    pair = psR[0:B, 1 + k // 2, (k % 2) * 2 * D:(k % 2 + 1) * 2 * D]
                    nc.vector.tensor_copy(rows[:, 4 + 2 * k, :], pair[:, 0:D])
                    nc.vector.tensor_scalar(rows[:, 5 + 2 * k, :], pair[:, D:2 * D], 1.0, None, ALU.add)
                gates = rows[:, 0:4, :].rearrange("b k d -> b (k d)")
                chain.step(nc.vector.tensor_copy(gates, psR[0:B, 0, :]))
                chain.step(nc.vector.scalar_tensor_tensor(out=gates, in0=gates, scalar=-1.0, in1=gates,
                                                          op0=ALU.mult, op1=ALU.max))
                chain.step(nc.vector.tensor_scalar(gates, gates, 0.25, None, ALU.max))
                nc.vector.tensor_tensor(gates, gates, sgn[0:B, :], ALU.mult).then_inc(s_rows, 1)


def ln_finish(core, tag, st, eps, block):
    nc, NT = core.nc, core.NT
    on = core.stack
    m, dm, v, sd = core.ln_tmp
    s_v, s_sd = core.sem(f"{tag}_var_ready"), core.sem(f"{tag}_std_ready")

    @block.vector
    def _(dve):
        chain = Chain(core, dve, f"{tag}_dve_chain")
        chain.step(nc.vector.tensor_tensor(m[:], st[:, :, 1], st[:, :, 4], ALU.add))
        nc.vector.tensor_tensor(dm[:], st[:, :, 1], st[:, :, 4], ALU.subtract)
        chain.step(nc.vector.tensor_tensor(v[:], st[:, :, 2], st[:, :, 5], ALU.add))
        chain.step(nc.vector.tensor_tensor(dm[:], dm[:], dm[:], ALU.mult))
        chain.step(nc.vector.tensor_scalar(dm[:], dm[:], 0.25, eps, ALU.mult, ALU.add))
        nc.vector.scalar_tensor_tensor(out=v[:], in0=v[:], scalar=1.0 / D, in1=dm[:],
                                       op0=ALU.mult, op1=ALU.add).then_inc(s_v, 1)
        dve.wait_ge(s_sd, 1)
        chain.step(nc.vector.reciprocal(core.rstd[:], sd[:]))
        chain.step(nc.vector.scalar_tensor_tensor(out=core.nmr[:], in0=m[:], scalar=-0.5, in1=core.rstd[:],
                                                  op0=ALU.mult, op1=ALU.mult))

    @block.scalar
    def _(act):
        act.wait_ge(s_v, 1)
        nc.scalar.activation(sd[:], v[:], ACT.Sqrt).then_inc(s_sd, 1)


def ln_stats(core, tag, src=None, eps=LN_EPS):
    nc, NT = core.nc, core.NT
    src = core.X if src is None else src
    s_st = core.sem(f"{tag}_bn_ready")
    with nc.Block() as block:
        @block.vector
        def _(dve):
            for t in range(NT):
                last = nc.vector.bn_stats(core.st[:, t, :], src[:, t * D:(t + 1) * D])
            last.then_inc(s_st, 1)
            dve.wait_ge(s_st, 1)
    with nc.Block() as block:
        ln_finish(core, tag, core.st, eps, block)
H, DH = 16, 8
HQ = 4
PARTS = 3
KROWS = PARTS * PARTS * DH
RING = 3
PAIRS = H // 2
MAXHEADS = (0, 2, 3, 3, 3, 3, 2, 0)
MAXFROM = [sum(MAXHEADS[:p]) for p in range(PAIRS)]


def pair_heads(p):
    r, q = p // 2, 2 * (p % 2)
    return [HQ * q + r, HQ * (q + 1) + r]


def rolled(eng, n, lag, first, emit, ring=RING):
    turns = max(0, (n - first) // ring)
    for i in range(first):
        emit(i, i % ring)
    if turns:
        with eng.Fori(0, turns) as turn:
            for u in range(ring):
                emit(turn * ring + (first + u), (first + u) % ring)
    for i in range(first + turns * ring, n + lag):
        emit(i, i % ring)


def attention(core):
    nc, B, X, aps = core.nc, core.B, core.X, core.aps
    SCALE = float(DH) ** -0.5
    live = lambda i, lag: not isinstance(i, int) or 0 <= i - lag < B
    on = ExitStack()
    with on:
        sb = lambda name, shape, dt=F32: core.sbuf("a_" + name, shape, dt, on=on)
        w_dk, w_dv, w_uk, w_uv, w_o, rot = (sb(n, [P, D]) for n in ("w_dk", "w_dv", "w_uk", "w_uv", "w_o", "rot"))
        bias = sb("bias_cols", [P, 4])
        bo = sb("bias_out", [P, TC * D])
        bo_row = sb("bias_out_row", [1, D])
        bo_in = sb("b_o_row", [1, D])
        ones1 = sb("ones_row", [1, P])
        cos, sin = sb("cos", [P, 2 * T]), sb("sin", [P, 2 * T])
        xn = sb("xn", [P, TC, D])
        qk = sb("qk", [P, 2, T])
        ckv = sb("ckv", [P, 2, T])
        qcos, qsin = sb("qk_cos", [P, 2 * T]), sb("qk_sin", [P, 2 * T])
        roped, left = sb("roped", [P, 2 * T]), sb("left", [P, 2 * T])
        parts = sb("parts", [P, PARTS, 2, T], BF16)
        Q9 = [sb(f"Q9_{n}", [KROWS + 2, H, T], BF16) for n in range(RING)]
        K9 = [sb(f"K9_{n}", [KROWS + 2, H, T], BF16) for n in range(RING)]
        V = [sb(f"V_{n}", [P, TC, HQ, HQ, 32]) for n in range(RING)]
        ones = sb("ones_pad", [P, HQ, 32])
        mx = sb("row_max", [P, H, TC])
        mhi, mlo = sb("max_hi", [2 * H, P], BF16), sb("max_lo", [2 * H, P], BF16)
        PT = sb("probs", [P, 4, 2, TC, T])
        rden, oT = sb("rden", [P, T]), sb("oT", [P, T])
        ga = sb("gate_rows", [P, D])
        minus = sb("minus_one", [2, H * T], BF16)
        y1, y2 = sb("y1", [P, TC * D]), sb("y2", [P, TC * D])
        ST = core.psum("a_scores", [P, 2, 2, TC, T], on=on)
        MX = core.psum("a_maxscores", [P, 2, TC, T], on=on)
        O = core.psum("a_out", [P, 2, T], on=on)
        PP = core.psum("a_proj", [P, 512], on=on)
        split = [nc.dram_tensor(f"split_qk_{n}", [P, PARTS, 2, T], BF16, kind="Internal").ap() for n in range(RING)]

        S = {n: core.sem("a_" + n) for n in (
            "w_loaded", "const_ready", "mrow_const", "bo_ps", "bo_row", "bo_ready", "gate_loaded", "xn_ready", "hT_ps", "hT_ready", "ckv_ps",
            "ckv_ready", "kv_ps", "k_ready", "v_ready", "rot_ps", "cos_done", "sin_done", "roped_ready", "part0",
            "left1", "part1", "part2", "stored", "loaded", "max_ps", "max_done", "maxT_ps", "max_hi", "max_lo",
            "max_rows", "scores_ps", "exp_done", "av_done", "rden_ready", "oT_ready", "y_ps", "y_biased",
            "y_gated", "x_updated", "passed")}

        with nc.Block() as block:
            @block.sync
            def _(sp):
                for t, n in ((w_dk, "L0_attn_w_dk"), (w_dv, "L0_attn_w_dv"), (w_uk, "L0_attn_w_uk"), (w_uv, "L0_attn_w_uv"),
                             (w_o, "L0_attn_w_o"), (rot, "rope_rot")):
                    sp.dma_start(t[:], aps[n]).then_inc(S["w_loaded"], 16)
                for k, n in enumerate(("L0_attn_b_dk", "L0_attn_b_dv", "L0_attn_b_uk", "L0_attn_b_uv")):
                    sp.dma_start(bias[:, k:k + 1], aps[n].rearrange("(p n) -> p n", n=1)).then_inc(S["w_loaded"], 16)
                sp.dma_start(bo_in[:], aps["L0_attn_b_o"].rearrange("(n d) -> n d", n=1)).then_inc(S["w_loaded"], 16)
                for t, n in ((cos, "rope_cos"), (sin, "rope_sin")):
                    for k in range(2):
                        sp.dma_start(t[:, k * T:(k + 1) * T], aps[n]).then_inc(S["w_loaded"], 16)
                sp.wait_ge(S["const_ready"], 1)
                for n in range(RING):
                    sp.dma_start(K9[n][KROWS:KROWS + 2, :, :], minus[:].rearrange("p (h t) -> p h t", t=T)).then_inc(S["mrow_const"], 16)

                def emit(i, u):
                    if live(i, 3):
                        at(sp, S["y_gated"], i - 3)
                        sp.dma_start(ga[:], core.modrow[0, ds(i - 3, 1), :].rearrange("n d -> (n d)").partition_broadcast(P)).then_inc(S["gate_loaded"], 16)
                    if live(i, 1):
                        n = (u + 2) % RING
                        at_alone(sp, S["max_lo"], i, S["passed"])
                        at(sp, S["scores_ps"], PAIRS * (i - 3))
                        for k, m in enumerate((mhi, mlo)):
                            sp.dma_start(Q9[n][KROWS + k:KROWS + k + 1, :, :], m[:]).then_inc(S["max_rows"], 16)
                    if live(i, 0):
                        at_alone(sp, S["loaded"], 16 * 2 * PARTS * PARTS * (i - 2), S["passed"])
                        sp.wait_ge(S["part2"], i + 1)
                        sp.dma_start(split[u], parts[:]).then_inc(S["stored"], 16)
                        at_alone(sp, S["stored"], 16 * (i + 1), S["passed"])
                        at(sp, S["scores_ps"], PAIRS * (i - 2))
                        view = split[u].rearrange("(h e) a w t -> a w e h t", e=DH)
                        for a in range(PARTS):
                            for b in range(PARTS):
                                row = (a * PARTS + b) * DH
                                sp.dma_start(Q9[u][row:row + DH, :, :], view[a, 0]).then_inc(S["loaded"], 16)
                                sp.dma_start(K9[u][row:row + DH, :, :], view[b, 1]).then_inc(S["loaded"], 16)
                rolled(sp, B, 3, 5, emit)

            @block.gpsimd
            def _(pool):
                nc.gpsimd.memset(ones[:], 0.0)
                for n in range(RING):
                    last = nc.gpsimd.memset(V[n][:], 0.0)
                last.then_inc(S["bo_row"], 1)
                pool.wait_ge(S["bo_row"], 1)
                for r in range(HQ):
                    nc.gpsimd.memset(ones[:, r, r * DH:(r + 1) * DH], 1.0)
                nc.gpsimd.memset(minus[:], -1.0)
                nc.gpsimd.memset(ones1[:], 1.0).then_inc(S["const_ready"], 1)
                pool.wait_ge(S["w_loaded"], 15 * 16)
                pool.wait_ge(S["bo_ready"], 1)

                def emit(i, u):
                    if live(i, 0):
                        pool.wait_ge(S["k_ready"], i + 1)
                        at(pool, S["roped_ready"], i)
                        nc.gpsimd.tensor_tensor(qcos[:], qk[:].rearrange("p a t -> p (a t)"), cos[:], ALU.mult).then_inc(S["cos_done"], 1)
                    if live(i, 3):
                        pool.wait_ge(S["y_biased"], i - 2)
                        pool.wait_ge(S["gate_loaded"], 16 * (i - 2))
                        at(pool, S["x_updated"], i - 3)
                        g = ga[:].unsqueeze(1).broadcast_to([P, TC, D])
                        nc.gpsimd.tensor_tensor(y2[:].rearrange("p (n d) -> p n d", d=D), y1[:].rearrange("p (n d) -> p n d", d=D), g,
                                                ALU.mult).then_inc(S["y_gated"], 1)
                    if live(i, 3):
                        pool.wait_ge(S["y_gated"], i - 2)
                        x = X[:, ds((i - 3) * (TC * D), TC * D)]
                        nc.gpsimd.tensor_tensor(x, x, y2[:], ALU.add).then_inc(S["x_updated"], 1)
                rolled(pool, B, 3, 5, emit)

            @block.scalar
            def _(act):
                act.wait_ge(S["w_loaded"], 15 * 16)

                def emit(i, u):
                    for p in range(PAIRS):
                        if live(i, 2):
                            act.wait_ge(S["scores_ps"], PAIRS * (i - 2) + p + 1)
                            at(act, S["av_done"], 4 * (i - 2) + p // 2 - 1)
                            nc.scalar.activation(PT[:, p % 4].rearrange("p a b t -> p (a b t)"), ST[:, p % 2].rearrange("p a b t -> p (a b t)"),
                                                 ACT.Exp, scale=SCALE).then_inc(S["exp_done"], 1)
                        if p == 1 and live(i, 0):
                            act.wait_ge(S["hT_ps"], i + 1)
                            at(act, S["rot_ps"], i)
                            at(act, S["cos_done"], i)
                            nc.scalar.activation(qk[:, 0, :], PP[:, 0:T], ACT.Identity, scale=core.modcol(0, SCALE_A, i),
                                                 bias=core.modcol(0, SHIFT_A, i)).then_inc(S["hT_ready"], 1)
                        if p == 2 and live(i, 0):
                            act.wait_ge(S["ckv_ps"], i + 1)
                            at(act, S["kv_ps"], i)
                            for k in range(2):
                                last = nc.scalar.activation(ckv[:, k, :], PP[:, k * T:(k + 1) * T], ACT.Identity, bias=bias[:, k:k + 1])
                            last.then_inc(S["ckv_ready"], 1)
                        if p == 3 and live(i, 0):
                            act.wait_ge(S["v_ready"], i + 1)
                            nc.scalar.activation(qk[:, 1, :], PP[:, 0:T], ACT.Identity, bias=bias[:, 2:3]).then_inc(S["k_ready"], 1)
                        if p == 6 and live(i, 0):
                            act.wait_ge(S["roped_ready"], i + 1)
                            at(act, S["stored"], 16 * i)
                            nc.scalar.activation(parts[:, 0].rearrange("p a t -> p (a t)"), roped[:], ACT.Copy).then_inc(S["part0"], 1)
                            act.wait_ge(S["left1"], i + 1)
                            nc.scalar.activation(parts[:, 1].rearrange("p a t -> p (a t)"), left[:], ACT.Copy).then_inc(S["part1"], 1)
                rolled(act, B, 3, 5, emit)

            @block.vector
            def _(dve):
                dve.wait_ge(S["bo_ps"], 1)
                nc.vector.tensor_tensor(bo_row[:], PP[0:1, 0:D], bo_in[:], ALU.add).then_inc(S["bo_ready"], 1)
                dve.wait_ge(S["bo_ps"], 2)
                for k in range(TC):
                    last = nc.vector.tensor_copy(bo[:, k * D:(k + 1) * D], PP[:, D:2 * D])
                last.then_inc(S["bo_ready"], 1)
                dve.wait_ge(S["bo_ready"], 2)

                def emit(i, u):
                    for p in range(PAIRS):
                        if p == 0 and live(i, 0):
                            at(dve, S["hT_ps"], i)
                            for k in range(TC):
                                c = 2 * i + k
                                last = nc.vector.tensor_scalar(xn[:, k, :], X[:, ds(i * (TC * D) + k * D, D)], core.rstd[:, ds(c, 1)],
                                                               core.nmr[:, ds(c, 1)], ALU.mult, ALU.add)
                            last.then_inc(S["xn_ready"], 1)
                        if p == 2 and live(i, 3):
                            b = i - 3
                            dve.wait_ge(S["av_done"], 4 * (b + 1))
                            nc.vector.reciprocal(rden[:], O[:, 1, :]).then_inc(S["rden_ready"], 1)
                            dve.wait_ge(S["rden_ready"], b + 1)
                            at(dve, S["y_ps"], b)
                            nc.vector.tensor_tensor(oT[:], O[:, 0, :], rden[:], ALU.mult).then_inc(S["oT_ready"], 1)
                        if live(i, 1):
                            b = i - 1
                            for h in range(MAXFROM[p], MAXFROM[p] + MAXHEADS[p]):
                                dve.wait_ge(S["max_ps"], H * b + h + 1)
                                if h == 0:
                                    at(dve, S["maxT_ps"], b)
                                nc.vector.tensor_reduce(mx[:, h, :], MX[:, h % 2], AX.X, ALU.max).then_inc(S["max_done"], 1)
                        if p == 3 and live(i, 0):
                            dve.wait_ge(S["kv_ps"], i + 1)
                            at(dve, S["av_done"], 4 * (i - 2))
                            for k in range(TC):
                                v = V[u][:, k]
                                heads = bass.AP(tensor=v.tensor, offset=v.offset, ap=[list(v.ap[0]), [HQ * 32, HQ], [32 + DH, HQ], [1, DH]])
                                last = nc.vector.tensor_copy(heads, PP[:, T + k * D:T + (k + 1) * D].rearrange("p (q r e) -> p q r e", q=HQ, r=HQ))
                            last.then_inc(S["v_ready"], 1)
                        if p == 5 and live(i, 0):
                            dve.wait_ge(S["rot_ps"], i + 1)
                            nc.vector.tensor_tensor(qsin[:], PP[:], sin[:], ALU.mult).then_inc(S["sin_done"], 1)
                            dve.wait_ge(S["sin_done"], i + 1)
                            dve.wait_ge(S["cos_done"], i + 1)
                            nc.vector.tensor_tensor(roped[:], qcos[:], qsin[:], ALU.add).then_inc(S["roped_ready"], 1)
                        if p == 6 and live(i, 3):
                            b = i - 3
                            dve.wait_ge(S["y_ps"], b + 1)
                            at(dve, S["y_gated"], b)
                            nc.vector.tensor_tensor(y1[:], PP[:, 0:TC * D], bo[:], ALU.add).then_inc(S["y_biased"], 1)
                        if p == 6 and live(i, 0):
                            dve.wait_ge(S["part0"], i + 1)
                            nc.vector.tensor_tensor(left[:], roped[:], parts[:, 0].rearrange("p a t -> p (a t)"), ALU.subtract).then_inc(S["left1"], 1)
                        if p == 7 and live(i, 1):
                            b = i - 1
                            dve.wait_ge(S["maxT_ps"], b + 1)
                            at(dve, S["max_rows"], 32 * b)
                            nc.vector.tensor_copy(mhi[:], PP[0:2 * H, 0:P]).then_inc(S["max_hi"], 1)
                            dve.wait_ge(S["max_hi"], b + 1)
                            nc.vector.tensor_tensor(mlo[:], PP[0:2 * H, 0:P], mhi[:], ALU.subtract).then_inc(S["max_lo"], 1)
                        if p == 7 and live(i, 0):
                            dve.wait_ge(S["part1"], i + 1)
                            nc.vector.tensor_tensor(parts[:, 2].rearrange("p a t -> p (a t)"), left[:], parts[:, 1].rearrange("p a t -> p (a t)"),
                                                    ALU.subtract).then_inc(S["part2"], 1)
                rolled(dve, B, 3, 5, emit)

            @block.tensor
            def _(pe):
                mm = nc.tensor.matmul
                pe.wait_ge(S["w_loaded"], 15 * 16)
                pe.wait_ge(S["const_ready"], 1)
                pe.wait_ge(S["mrow_const"], 16 * RING)
                mm(PP[0:1, 0:D], bias[:, 3:4], w_o[:], start=True, stop=True).then_inc(S["bo_ps"], 1)
                pe.wait_ge(S["bo_ready"], 1)
                mm(PP[:, D:2 * D], ones1[:], bo_row[:], start=True, stop=True).then_inc(S["bo_ps"], 1)
                pe.wait_ge(S["bo_ready"], 2)

                def values(b, u, g):
                    pe.wait_ge(S["exp_done"], PAIRS * b + 2 * g + 2)
                    if g == 0:
                        at(pe, S["oT_ready"], b)
                    for k in range(TC):
                        for kind in range(2):
                            for q in range(HQ):
                                w = V[u][:, k, q, g, :] if kind == 0 else ones[:, g, :]
                                pr = PT[:, (2 * g + q // 2) % 4, q % 2, k, :]
                                last = mm(O[32 * q:32 * q + 32, kind, :], w, pr, start=(g == 0 and k == 0 and kind == 0),
                                          stop=(g == 3 and k == TC - 1 and kind == 1), skip_group_check=True)
                    last.then_inc(S["av_done"], 1)

                def emit(i, u):
                    for p in range(PAIRS):
                        if live(i, 2):
                            b, n = i - 2, (u + 1) % RING
                            if p == 0:
                                pe.wait_ge(S["max_rows"], 32 * (b + 1))
                            at(pe, S["exp_done"], PAIRS * b + p - 1)
                            for j, h in enumerate(pair_heads(p)):
                                for k in range(TC):
                                    last = mm(ST[:, p % 2, j, k, :], K9[n][:, h, k * P:(k + 1) * P], Q9[n][:, h, :], start=True, stop=True)
                            last.then_inc(S["scores_ps"], 1)
                        if p == 1 and live(i, 3):
                            values(i - 3, u, 3)
                        if p % 2 == 1 and p >= 3 and live(i, 2):
                            if p == 3:
                                pe.wait_ge(S["v_ready"], i - 1)
                            values(i - 2, (u + 1) % RING, p // 2 - 1)
                        if p == 1 and live(i, 0):
                            pe.wait_ge(S["xn_ready"], i + 1)
                            at(pe, S["max_lo"], i - 1)
                            at(pe, S["y_biased"], i - 3)
                            for k in range(TC):
                                last = nc.tensor.transpose(PP[:, k * P:(k + 1) * P], xn[:, k, :], core.ident[:])
                            last.then_inc(S["hT_ps"], 1)
                        if p == 2 and live(i, 0):
                            pe.wait_ge(S["hT_ready"], i + 1)
                            mm(PP[:, 0:T], w_dk[:], qk[:, 0, :], start=True, stop=True)
                            mm(PP[:, T:2 * T], w_dv[:], qk[:, 0, :], start=True, stop=True).then_inc(S["ckv_ps"], 1)
                        if live(i, 1):
                            b, n = i - 1, (u + 2) % RING
                            for h in range(MAXFROM[p], MAXFROM[p] + MAXHEADS[p]):
                                if h == 0:
                                    pe.wait_ge(S["loaded"], 16 * 2 * PARTS * PARTS * (b + 1))
                                at(pe, S["max_done"], H * b + h - 1)
                                for k in range(TC):
                                    last = mm(MX[:, h % 2, k, :], Q9[n][0:KROWS, h, k * P:(k + 1) * P], K9[n][0:KROWS, h, :], start=True, stop=True)
                                last.then_inc(S["max_ps"], 1)
                        if p == 3 and live(i, 0):
                            pe.wait_ge(S["ckv_ready"], i + 1)
                            mm(PP[:, 0:T], w_uk[:], ckv[:, 0, :], start=True, stop=True)
                            for k in range(TC):
                                last = mm(PP[:, T + k * D:T + (k + 1) * D], ckv[:, 1, k * P:(k + 1) * P], w_uv[:], start=True, stop=True)
                            last.then_inc(S["kv_ps"], 1)
                        if p == 4 and live(i, 0):
                            pe.wait_ge(S["k_ready"], i + 1)
                            pe.wait_ge(S["v_ready"], i + 1)
                            mm(PP[:], rot[:], qk[:].rearrange("p a t -> p (a t)"), start=True, stop=True).then_inc(S["rot_ps"], 1)
                        if p == 6 and live(i, 3):
                            b = i - 3
                            if live(i, 0):
                                pe.wait_ge(S["sin_done"], i + 1)
                            else:
                                pe.wait_ge(S["max_lo"], min(i - 1, B))
                            pe.wait_ge(S["oT_ready"], b + 1)
                            for k in range(TC):
                                last = mm(PP[:, k * D:(k + 1) * D], oT[:, k * P:(k + 1) * P], w_o[:], start=True, stop=True)
                            last.then_inc(S["y_ps"], 1)
                        if p == 7 and live(i, 1):
                            b = i - 1
                            pe.wait_ge(S["max_done"], H * (b + 1))
                            if live(i, 0):
                                pe.wait_ge(S["sin_done"], i + 1)
                            if live(i, 3):
                                pe.wait_ge(S["y_biased"], i - 2)
                            nc.tensor.transpose(PP[0:2 * H, 0:P], mx[:].rearrange("p h k -> p (h k)"), core.ident[:]).then_inc(S["maxT_ps"], 1)
                rolled(pe, B, 3, 5, emit)
E, F = 8, 512
FC = F // P
STAGES = 4
CAP = 80


def start_counts(core, tag, names):
    S = {n: core.sem(f"{tag}_{n}") for n in names}
    with core.nc.Block() as block:
        @block.sync
        def _(sp):
            for n in names:
                sp.sem_inc(S[n], 1)
    return S


def upto(eng, sem, count):
    if isinstance(count, int) and count < 0:
        return
    eng.wait_ge(sem, count + 1)


def fill_zero(core, tag, table, tiles):
    nc = core.nc
    on = ExitStack()
    with on:
        zero = core.sbuf(f"{tag}_zero", [P, tiles, D // 8], on=on)
        s_zero, s_out = core.sem(f"{tag}_zero_ready"), core.sem(f"{tag}_zeroed")
        with nc.Block() as block:
            @block.vector
            def _(dve):
                nc.vector.memset(zero[:], 0.0).then_inc(s_zero, 1)

            @block.sync
            def _(sp):
                sp.wait_ge(s_zero, 1)
                w = tiles * D // 8
                flat = table.rearrange("r d -> (r d)").rearrange("(k p w) -> k p w", k=8, p=P)
                for k in range(8):
                    sp.dma_start(flat[k], zero[:].rearrange("p n d -> p (n d)")).then_inc(s_out, 16)
                sp.wait_ge(s_out, 128)


def modulated(core, layer, Hr, L, row):
    nc, B, X, aps, tag = core.nc, core.B, core.X, core.aps, f"r{row}"
    on = ExitStack()
    with on:
        sb = lambda name, shape, dt=F32: core.sbuf(f"{tag}_{name}", shape, dt, on=on)
        gw = sb("gate_w", [P, E])
        mod = [sb(f"mod_rows{n}", [P, 2, D]) for n in range(2)]
        xn = [sb(f"xn{n}", [P, TC, D]) for n in range(2)]
        h = [sb(f"h{n}", [P, TC, D]) for n in range(2)]
        hT = [sb(f"hT{n}", [P, TC, P]) for n in range(2)]
        psT = core.psum(f"{tag}_psT", [P, 2, 512], on=on)
        psL = core.psum(f"{tag}_psL", [P, 2, 512], on=on)
        S = start_counts(core, tag, ("w_loaded", "mod_loaded0", "mod_loaded1", "xn_ready", "scaled", "h_ready", "h_kept", "hT_ps", "hT_ready",
                                     "logits_ps", "logits_kept"))

        def loop(eng, emit):
            with eng.Fori(0, B // 2) as t:
                for u in range(2):
                    emit(t * 2 + u, u, t)

        with nc.Block() as block:
            @block.sync
            def _(sp):
                if L is not None:
                    sp.dma_start(gw[:], aps[f"L{layer}_ffn_gate_w"]).then_inc(S["w_loaded"], 16)

                def emit(b, u, turn):
                    upto(sp, S["h_ready"], b)
                    sp.dma_start(mod[u][:], core.modrow[row:row + 2, ds(b, 1), :].rearrange("k n d -> (k n) d").partition_broadcast(P))\
                        .then_inc(S[f"mod_loaded{u}"], 16)
                loop(sp, emit)

            @block.vector
            def _(dve):
                def emit(b, u, turn):
                    upto(dve, S["scaled"], b)
                    for k in range(TC):
                        c = b * TC + k
                        last = nc.vector.tensor_scalar(xn[u][:, k, :], X[:, ds(b * (TC * D) + k * D, D)], core.rstd[:, ds(c, 1)],
                                                       core.nmr[:, ds(c, 1)], ALU.mult, ALU.add)
                    last.then_inc(S["xn_ready"], 1)
                    if L is None:
                        return
                    upto(dve, S["logits_ps"], b + 1)
                    nc.vector.tensor_copy(L[:, ds(b * (TC * E), TC * E)], psL[:, u, 0:TC * E]).then_inc(S["logits_kept"], 1)
                loop(dve, emit)

            @block.gpsimd
            def _(pool):
                def emit(b, u, turn):
                    upto(pool, S["xn_ready"], b + 1)
                    upto(pool, S[f"mod_loaded{u}"], 16 * (turn + 1))
                    upto(pool, S["h_kept"], b)
                    if L is not None:
                        upto(pool, S["hT_ps"], b)
                    nc.gpsimd.tensor_tensor(h[u][:], xn[u][:], mod[u][:, 1, :].unsqueeze(1).broadcast_to([P, TC, D]), ALU.mult).then_inc(S["scaled"], 1)
                    upto(pool, S["scaled"], b + 1)
                    nc.gpsimd.tensor_tensor(h[u][:], h[u][:], mod[u][:, 0, :].unsqueeze(1).broadcast_to([P, TC, D]), ALU.add).then_inc(S["h_ready"], 1)
                loop(pool, emit)

            if L is not None:
                @block.tensor
                def _(pe):
                    upto(pe, S["w_loaded"], 16)

                    def emit(b, u, turn):
                        upto(pe, S["h_ready"], b + 1)
                        upto(pe, S["hT_ready"], b)
                        for k in range(TC):
                            last = nc.tensor.transpose(psT[:, u, k * P:(k + 1) * P], h[u][:, k, :], core.ident[:])
                        last.then_inc(S["hT_ps"], 1)
                        upto(pe, S["hT_ready"], b + 1)
                        upto(pe, S["logits_kept"], b)
                        for k in range(TC):
                            last = nc.tensor.matmul(psL[:, u, k * E:(k + 1) * E], hT[u][:, k, :], gw[:], start=True, stop=True)
                        last.then_inc(S["logits_ps"], 1)
                    loop(pe, emit)

            @block.scalar
            def _(act):
                def emit(b, u, turn):
                    if L is None:
                        upto(act, S["h_ready"], b + 1)
                    else:
                        upto(act, S["hT_ps"], b + 1)
                        upto(act, S["logits_ps"], b)
                        nc.scalar.activation(hT[u][:].rearrange("p k t -> p (k t)"), psT[:, u, 0:TC * P], ACT.Copy).then_inc(S["hT_ready"], 1)
                    nc.scalar.activation(Hr[:, ds(b * (TC * D), TC * D)], h[u][:].rearrange("p k d -> p (k d)"), ACT.Copy).then_inc(S["h_kept"], 1)
                loop(act, emit)


def moe_route(core, layer, L, slots, weights, expert_of_tile=None, tiles=0):
    nc, NT, aps, tag = core.nc, core.NT, core.aps, f"q{layer}"
    K = 2 if layer == 0 else 1
    on = ExitStack()
    with on:
        sb = lambda name, shape, dt=F32: core.sbuf(f"{tag}_{name}", shape, dt, on=on)
        big = lambda name: sb(name, [P, NT, E])
        rev, tri, allone = sb("rev", [P, E]), sb("tri", [P, P]), sb("allone", [P, P])
        gb = sb("gate_b", [P, E])
        m = [big(f"choice{k}") for k in range(K)]
        L2, eq, cand, lim, dist, ex = big("masked_logits"), big("is_max"), big("candidates"), big("limit"), big("distance"), big("expd")
        both, before, within, place = big("chosen"), big("tiles_before"), big("within"), big("place")
        v, r = [sb(f"top{k}", [P, NT]) for k in range(K)], sb("rank", [P, NT])
        total = sb("sum", [P, NT])
        zero = sb("zeros", [P, NT])
        cnt, cnt_i = sb("counts", [P, E]), sb("counts_int", [P, E], I32)
        ends, base = sb("tile_ends", [P, E]), sb("base", [P, E])
        slot_f = sb("slot_f", [P, NT])
        ps = core.psum(f"{tag}_ps", [P, 2, 512], on=on)
        s_in, s_exp, s_exped = core.sem(f"{tag}_loaded"), core.sem(f"{tag}_exp_in"), core.sem(f"{tag}_exp_out")
        s_m, s_cum = core.sem(f"{tag}_chosen"), core.sem(f"{tag}_cum_ps")
        per_token = lambda t: t[:].unsqueeze(2).broadcast_to([P, NT, E])
        per_expert = lambda t: t[:].unsqueeze(1).broadcast_to([P, NT, E])
        flat = lambda t: t[:].rearrange("p n e -> p (n e)")
        with nc.Block() as block:
            @block.sync
            def _(sp):
                sp.dma_start(rev[:], aps["rev_rank"]).then_inc(s_in, 16)
                sp.dma_start(tri[:], aps["tri"]).then_inc(s_in, 16)
                if layer:
                    sp.dma_start(gb[:], aps["L1_ffn_gate_b"].partition_broadcast(P)).then_inc(s_in, 16)

            @block.scalar
            def _(act):
                for k in range(K):
                    act.wait_ge(s_exp, k + 1)
                    nc.scalar.activation(flat(ex), flat(dist), ACT.Exp).then_inc(s_exped, 1)

            @block.tensor
            def _(pe):
                pe.wait_ge(s_m, 1)
                nc.tensor.matmul(ps[:, 0, 0:NT * E], tri[:], flat(both), start=True, stop=True)
                nc.tensor.matmul(ps[:, 1, 0:NT * E], allone[:], flat(both), start=True, stop=True).then_inc(s_cum, 1)

            @block.vector
            def _(dve):
                chain = Chain(core, dve, f"{tag}_dve_chain")
                step = chain.step
                tt, ts, stt, red = nc.vector.tensor_tensor, nc.vector.tensor_scalar, nc.vector.scalar_tensor_tensor, nc.vector.tensor_reduce
                L3 = L[:].rearrange("p (n e) -> p n e", e=E)
                dve.wait_ge(s_in, 32 + 16 * layer)
                nc.vector.memset(allone[:], 1.0)
                step(nc.vector.memset(zero[:], 0.0))
                if layer:
                    step(tt(L3, L3, per_expert(gb), ALU.add))

                def first_max(src, k):
                    step(red(v[k][:], src, AX.X, ALU.max))
                    step(tt(eq[:], src, per_token(v[k]), ALU.is_equal))
                    step(tt(cand[:], eq[:], per_expert(rev), ALU.mult))
                    step(red(r[:], cand[:], AX.X, ALU.max))
                    step(tt(m[k][:], cand[:], per_token(r), ALU.is_equal))

                first_max(L3, 0)
                if K == 2:
                    step(ts(flat(L2), flat(m[0]), -2e38, 1e38, ALU.mult, ALU.add))
                    step(tt(L2[:], L2[:], L3, ALU.min))
                    first_max(L2[:], 1)
                for k in range(K):
                    src = L3 if k == 0 else L2[:]
                    step(tt(dist[:], src, per_token(v[k]), ALU.subtract))
                    dist_ready = nc.vector.tensor_copy(total[:], zero[:])
                    dist_ready.then_inc(s_exp, 1)
                    dve.wait_ge(s_exp, k + 1)
                    if layer == 0:
                        step(stt(out=lim[:], in0=L3, scalar=-1.0, in1=L3, op0=ALU.mult, op1=ALU.max))
                        step(tt(lim[:], lim[:], per_token(v[k]), ALU.max))
                        step(stt(out=flat(lim), in0=flat(lim), scalar=0.02, in1=flat(dist), op0=ALU.mult, op1=ALU.add))
                        step(ts(flat(lim), flat(lim), 0.0, None, ALU.is_ge))
                        dve.wait_ge(s_exped, k + 1)
                        step(tt(flat(ex), flat(ex), flat(lim), ALU.mult))
                    else:
                        dve.wait_ge(s_exped, k + 1)
                    step(red(total[:], ex[:], AX.X, ALU.add))
                    step(nc.vector.reciprocal(weights[k][:], total[:]))
                if K == 2:
                    tt(both[:], m[0][:], m[1][:], ALU.add).then_inc(s_m, 1)
                else:
                    nc.vector.tensor_copy(flat(both), flat(m[0])).then_inc(s_m, 1)
                dve.wait_ge(s_cum, 1)
                tot = ps[:, 1, 0:NT * E].rearrange("p (n e) -> p n e", e=E)
                step(nc.vector.tensor_copy(within[:], tot))
                for e in range(E):
                    last = nc.vector.tensor_tensor_scan(before[:, :, e], within[:, :, e], zero[:], 0.0, ALU.add, ALU.add)
                step(last)
                step(nc.vector.tensor_copy(cnt[:], before[:, NT - 1, :]))
                step(tt(before[:], before[:], within[:], ALU.subtract))
                step(tt(place[:], before[:], ps[:, 0, 0:NT * E].rearrange("p (n e) -> p n e", e=E), ALU.add))
                if layer == 0:
                    step(ts(cnt_i[:], cnt[:], float(P - 1), None, ALU.add))
                    step(ts(cnt_i[:], cnt_i[:], 7, None, ALU.arith_shift_right))
                    step(nc.vector.tensor_copy(cnt[:], cnt_i[:]))
                    step(nc.vector.tensor_tensor_scan(ends[:], cnt[:], zero[:, 0:E], 0.0, ALU.add, ALU.add))
                    step(tt(base[:], ends[:], cnt[:], ALU.subtract))
                    step(ts(base[:], base[:], float(P), -1.0, ALU.mult, ALU.add))
                    step(tt(place[:], place[:], per_expert(base), ALU.add))
                    for k in range(K):
                        step(tt(cand[:], m[k][:], place[:], ALU.mult))
                        step(red(slot_f[:], cand[:], AX.X, ALU.add))
                        step(nc.vector.tensor_copy(slots[k][:], slot_f[:]))
                    tile_no = sb("tile_no", [1, tiles])
                    acc = sb("tile_expert", [1, tiles])
                    step(nc.vector.memset(acc[:], 1.0))
                    step(nc.vector.tensor_tensor_scan(tile_no[:], acc[:], acc[:], -1.0, ALU.mult, ALU.add))
                    step(nc.vector.memset(acc[:], 0.0))
                    for e in range(E - 1):
                        step(stt(out=acc[:], in0=tile_no[:], scalar=ends[0:1, e:e + 1], in1=acc[:], op0=ALU.is_ge, op1=ALU.add))
                    step(nc.vector.tensor_copy(expert_of_tile[:], acc[:]))
                else:
                    step(tt(cand[:], m[0][:], place[:], ALU.mult))
                    step(red(r[:], cand[:], AX.X, ALU.add))
                    step(ts(base[:], rev[:], -float(CAP), float(E * CAP - 1), ALU.mult, ALU.add))
                    step(tt(place[:], place[:], per_expert(base), ALU.add))
                    step(tt(cand[:], m[0][:], place[:], ALU.mult))
                    step(red(slot_f[:], cand[:], AX.X, ALU.add))
                    step(ts(r[:], r[:], float(CAP), None, ALU.is_le))
                    nc.vector.tensor_tensor(weights[0][:], weights[0][:], r[:], ALU.mult)
                    step(ts(slot_f[:], slot_f[:], -float(E * CAP), None, ALU.add))
                    step(tt(slot_f[:], slot_f[:], r[:], ALU.mult))
                    step(ts(slot_f[:], slot_f[:], float(E * CAP), None, ALU.add))
                    step(nc.vector.tensor_copy(slots[0][:], slot_f[:]))


def scatter_rows(core, tag, Hr, slots, table, rows):
    nc, NT, K = core.nc, core.NT, len(slots)
    on = ExitStack()
    with on:
        row = [core.sbuf(f"{tag}_row{n}", [P, D], on=on) for n in range(STAGES)]
        idx = [[core.sbuf(f"{tag}_idx{n}_{k}", [P, 1], U32, on=on) for k in range(K)] for n in range(STAGES)]
        S = start_counts(core, tag, ["row_staged", "slot_staged", "passed"])
        scattered = [core.sem(f"{tag}_scattered{u}") for u in range(STAGES)]

        def loop(eng, emit):
            for u in range(STAGES):
                emit(u, u, 0)
            with eng.Fori(0, NT // STAGES - 1) as t:
                for u in range(STAGES):
                    emit((t + 1) * STAGES + u, u, t + 1)

        with nc.Block() as block:
            @block.scalar
            def _(act):
                def emit(t, u, turn):
                    at(act, scattered[u], turn * (16 * K))
                    nc.scalar.activation(row[u][:], Hr[:, ds(t * D, D)], ACT.Copy).then_inc(S["row_staged"], 1)
                loop(act, emit)

            @block.vector
            def _(dve):
                def emit(t, u, turn):
                    at(dve, scattered[u], turn * (16 * K))
                    for k in range(K):
                        last = nc.vector.tensor_copy(idx[u][k][:], slots[k][:, ds(t, 1)])
                    last.then_inc(S["slot_staged"], 1)
                loop(dve, emit)

            @block.gpsimd
            def _(pool):
                def emit(t, u, turn):
                    upto(pool, S["row_staged"], t + 1)
                    at_alone(pool, S["slot_staged"], t + 2, S["passed"])
                    for k in range(K):
                        nc.gpsimd.indirect_dma_start(out=table, out_offset=bass.IndirectOffsetOnAxis(ap=idx[u][k][:, 0:1], axis=0),
                                                     in_=row[u][:], in_offset=None, bounds_check=rows - 1, oob_is_err=False)\
                            .then_inc(scattered[u], 16)
                loop(pool, emit)
                for u in range(STAGES):
                    pool.wait_ge(scattered[u], 16 * K * (NT // STAGES))


def experts0(core, XS, YS, expert_of_tile, tiles):
    nc, aps = core.nc, core.aps
    U = 3
    assert tiles % U == 0
    on = ExitStack()
    with on:
        sb = lambda name, shape, dt=F32: core.sbuf("e0_" + name, shape, dt, on=on)
        w1, w3, w2 = sb("w1", [P, E, F]), sb("w3", [P, E, F]), sb("w2", [P, E, FC, D])
        x = [sb(f"x{n}", [P, D]) for n in range(U)]
        xT = [sb(f"xT{n}", [P, P]) for n in range(U)]
        act_h = [sb(f"silu{n}", [P, F]) for n in range(U)]
        g = [sb(f"g{n}", [P, FC, P]) for n in range(U)]
        gT = [sb(f"gT{n}", [P, FC, P]) for n in range(U)]
        y = [sb(f"y{n}", [P, D]) for n in range(U)]
        psX, ps1, ps3, psY = (core.psum("e0_ps" + n, [P, 512], on=on) for n in "X13Y")
        psG = core.psum("e0_psG", [P, FC, P], on=on)
        S = start_counts(core, "e0", ["w_loaded", "xT_ps", "xT_ready", "h1_ps", "h3_ps", "silu_ready", "g_ready", "gT_ps", "gT_ready",
                                      "y_ps", "y_ready"] + [f"{n}{u}" for n in ("x_loaded", "y_stored") for u in range(U)])
        turns = tiles // U

        def loop(eng, emit, peel=0):
            with eng.Fori(0, turns - peel) as turn:
                for u in range(U):
                    emit(turn * U + u, u, turn)
            for turn in range(turns - peel, turns):
                for u in range(U):
                    emit(turn * U + u, u, turn)

        with nc.Block() as block:
            @block.sync
            def _(sp):
                for t, n in ((w1, "L0_ffn_w1"), (w3, "L0_ffn_w3")):
                    sp.dma_start(t[:], aps[n].rearrange("e d f -> d e f")).then_inc(S["w_loaded"], 16)
                sp.dma_start(w2[:].rearrange("p e c d -> p (e c) d"), aps["L0_ffn_w2"].rearrange("e (c f) d -> f (e c) d", f=P)).then_inc(S["w_loaded"], 16)
                ahead = U - 1
                for j in range(ahead):
                    sp.dma_start(x[j][:], XS[j * P:(j + 1) * P, :]).then_inc(S[f"x_loaded{j}"], 16)

                def emit(j, u, turn):
                    if not isinstance(j, int) or j + ahead < tiles:
                        n = (u + ahead) % U
                        upto(sp, S["xT_ps"], j)
                        sp.dma_start(x[n][:], XS[ds((j + ahead) * P, P), :]).then_inc(S[f"x_loaded{n}"], 16)
                    upto(sp, S["y_ready"], j + 1)
                    sp.dma_start(YS[ds(j * P, P), :], y[u][:]).then_inc(S[f"y_stored{u}"], 16)
                loop(sp, emit, peel=1)
                for u in range(U):
                    upto(sp, S[f"y_stored{u}"], 16 * turns)

            @block.tensor
            def _(pe):
                mm = nc.tensor.matmul
                upto(pe, S["w_loaded"], 48)
                expert = lambda j: pe.value_load(expert_of_tile[0:1, ds(j, 1)], min_val=0, max_val=E - 1)

                def up(j, u, turn):
                    upto(pe, S[f"x_loaded{u}"], 16 * (turn + 1))
                    nc.tensor.transpose(psX[:, 0:P], x[u][:], core.ident[:]).then_inc(S["xT_ps"], 1)
                    e = expert(j)
                    upto(pe, S["xT_ready"], j + 1)
                    upto(pe, S["silu_ready"], j)
                    mm(ps1[:], xT[u][:], w1[:, ds(e, 1), :].rearrange("p n f -> p (n f)"), start=True, stop=True).then_inc(S["h1_ps"], 1)
                    upto(pe, S["g_ready"], j)
                    mm(ps3[:], xT[u][:], w3[:, ds(e, 1), :].rearrange("p n f -> p (n f)"), start=True, stop=True).then_inc(S["h3_ps"], 1)

                def down(j, u):
                    upto(pe, S["g_ready"], j + 1)
                    for c in range(FC):
                        last = nc.tensor.transpose(psG[:, c, :], g[u][:, c, :], core.ident[:])
                    last.then_inc(S["gT_ps"], 1)
                    e = expert(j)
                    upto(pe, S["gT_ready"], j + 1)
                    upto(pe, S["y_ready"], j)
                    for c in range(FC):
                        last = mm(psY[:, 0:D], gT[u][:, c, :], w2[:, ds(e, 1), c, :].rearrange("p n d -> p (n d)"), start=(c == 0), stop=(c == FC - 1))
                    last.then_inc(S["y_ps"], 1)

                up(0, 0, 0)

                def emit(j, u, turn):
                    if not isinstance(j, int) or j + 1 < tiles:
                        up(j + 1, (u + 1) % U, turn + (u + 1) // U)
                    down(j, u)
                loop(pe, emit, peel=1)

            @block.scalar
            def _(act):
                def emit(j, u, turn):
                    upto(act, S["h1_ps"], j + 1)
                    nc.scalar.activation(act_h[u][:], ps1[:], ACT.Silu).then_inc(S["silu_ready"], 1)
                    upto(act, S["gT_ps"], j + 1)
                    nc.scalar.activation(gT[u][:].rearrange("p c t -> p (c t)"), psG[:].rearrange("p c t -> p (c t)"), ACT.Copy).then_inc(S["gT_ready"], 1)
                loop(act, emit)

            @block.vector
            def _(dve):
                upto(dve, S["xT_ps"], 1)
                nc.vector.tensor_copy(xT[0][:], psX[:, 0:P]).then_inc(S["xT_ready"], 1)

                def emit(j, u, turn):
                    upto(dve, S["silu_ready"], j + 1)
                    upto(dve, S["h3_ps"], j + 1)
                    nc.vector.tensor_tensor(g[u][:].rearrange("p c t -> p (c t)"), act_h[u][:], ps3[:], ALU.mult).then_inc(S["g_ready"], 1)
                    if not isinstance(j, int) or j + 1 < tiles:
                        n = (u + 1) % U
                        upto(dve, S["xT_ps"], j + 2)
                        nc.vector.tensor_copy(xT[n][:], psX[:, 0:P]).then_inc(S["xT_ready"], 1)
                    upto(dve, S["y_ps"], j + 1)
                    upto(dve, S[f"y_stored{u}"], turn * 16)
                    nc.vector.tensor_copy(y[u][:], psY[:, 0:D]).then_inc(S["y_ready"], 1)
                loop(dve, emit, peel=1)


def gather_and_add(core, tag, layer, slots, weights, table):
    nc, NT, B, X, K = core.nc, core.NT, core.B, core.X, len(slots)
    GB = STAGES // TC
    on = ExitStack()
    with on:
        yg = [[core.sbuf(f"{tag}_y{n}_{k}", [P, D], on=on) for k in range(K)] for n in range(STAGES)]
        idx = [[core.sbuf(f"{tag}_idx{n}_{k}", [P, 1], U32, on=on) for k in range(K)] for n in range(STAGES)]
        acc = [core.sbuf(f"{tag}_acc{n}", [P, D], on=on) for n in range(STAGES)]
        gate = [core.sbuf(f"{tag}_gate{n}", [P, D], on=on) for n in range(GB)]
        S = start_counts(core, tag, ["slot_staged", "weighted", "summed", "gated", "x_updated", "passed"] + [f"gate_loaded{u}" for u in range(GB)])
        gathered = [core.sem(f"{tag}_gathered{u}") for u in range(STAGES)]
        turns = NT // STAGES

        with nc.Block() as block:
            @block.sync
            def _(sp):
                with sp.Fori(0, turns) as turn:
                    for n in range(GB):
                        upto(sp, S["gated"], turn * STAGES)
                        sp.dma_start(gate[n][:], core.modrow[1 + 2 * layer, ds(turn * GB + n, 1), :].rearrange("n d -> (n d)").partition_broadcast(P))\
                            .then_inc(S[f"gate_loaded{n}"], 16)

            @block.gpsimd
            def _(pool):
                with pool.Fori(0, turns) as turn:
                    for u in range(STAGES):
                        at_alone(pool, S["slot_staged"], turn * STAGES + (u + 1) + 1, S["passed"])
                        for k in range(K):
                            nc.gpsimd.indirect_dma_start(out=yg[u][k][:], out_offset=None, in_=table,
                                                         in_offset=bass.IndirectOffsetOnAxis(ap=idx[u][k][:, 0:1], axis=0))\
                                .then_inc(gathered[u], 16)

            @block.vector
            def _(dve):
                ahead = STAGES - 1

                def stage(t, u):
                    for k in range(K):
                        last = nc.vector.tensor_copy(idx[u][k][:], slots[k][:, ds(t, 1)])
                    last.then_inc(S["slot_staged"], 1)

                for t in range(ahead):
                    stage(t, t)

                def emit(t, u, turn):
                    if not isinstance(t, int) or t + ahead < NT:
                        stage(t + ahead, (u + ahead) % STAGES)
                    dve.wait_ge(gathered[u], (turn + 1) * (16 * K))
                    nc.vector.tensor_scalar(acc[u][:], yg[u][0][:], weights[0][:, ds(t, 1)], None, ALU.mult).then_inc(S["weighted"], 1)
                    upto(dve, S["weighted"], t + 1)
                    if K == 2:
                        nc.vector.scalar_tensor_tensor(out=acc[u][:], in0=yg[u][1][:], scalar=weights[1][:, ds(t, 1)], in1=acc[u][:],
                                                       op0=ALU.mult, op1=ALU.add).then_inc(S["summed"], 1)
                        upto(dve, S["summed"], t + 1)
                    upto(dve, S[f"gate_loaded{u // TC}"], (turn + 1) * 16)
                    nc.vector.tensor_tensor(acc[u][:], acc[u][:], gate[u // TC][:], ALU.mult).then_inc(S["gated"], 1)
                    upto(dve, S["gated"], t + 1)
                    x = X[:, ds(t * D, D)]
                    nc.vector.tensor_tensor(x, x, acc[u][:], ALU.add).then_inc(S["x_updated"], 1)

                with dve.Fori(0, turns - 1) as turn:
                    for u in range(STAGES):
                        emit(turn * STAGES + u, u, turn)
                for u in range(STAGES):
                    emit((turns - 1) * STAGES + u, u, turns - 1)
                upto(dve, S["x_updated"], NT)


def ffn0(core):
    nc, NT = core.nc, core.NT
    tiles = 2 * NT + E - 1
    tiles += -tiles % 3
    XS = nc.dram_tensor("slot_inputs", [tiles * P, D], F32, kind="Internal").ap()
    YS = nc.dram_tensor("slot_outputs", [tiles * P, D], F32, kind="Internal").ap()
    on = ExitStack()
    with on:
        slots = [core.sbuf(f"slots0_{k}", [P, NT], U32, on=on) for k in range(2)]
        weights = [core.sbuf(f"weights0_{k}", [P, NT], on=on) for k in range(2)]
        expert_of_tile = core.sbuf("expert_of_tile", [1, tiles], I32, on=on)
        scratch = ExitStack()
        with scratch:
            Hr = core.sbuf("h_rows0", [P, NT * D], on=scratch)
            L = core.sbuf("logits0", [P, NT * E], on=scratch)
            fill_zero(core, "xs0", XS, tiles)
            modulated(core, 0, Hr, L, 4)
            moe_route(core, 0, L, slots, weights, expert_of_tile, tiles)
            scatter_rows(core, "sc0", Hr, slots, XS, tiles * P)
        experts0(core, XS, YS, expert_of_tile, tiles)
        gather_and_add(core, "ga0", 0, slots, weights, YS)
DI, DS, DC, DTR = 256, 16, 4, 8
C2 = DI // P
DIRS = 2
G = 2
W = G * T
BC = 2 * DS
USES = 13
BANK_USES = (7, 6)


def mixer_weights(core, Wt, on):
    nc, aps = core.nc, core.aps
    tmp = ExitStack()
    with tmp:
        sb = lambda name, shape, dt=F32: core.sbuf("w_" + name, shape, dt, on=tmp)
        win = sb("in_proj", [P, 4, D])
        taps = sb("conv_w", [P, DIRS, C2, DC])
        scaled = sb("in_taps", [P, DIRS, C2, DC, D])
        wout = sb("out_proj", [P, DI])
        xp = sb("x_proj", [BC + DTR, DIRS, DI])
        xdt = sb("x_proj_dt", [DTR, DIRS, DI])
        dtT = sb("dt_w_T", [DTR, DIRS, DI])
        sel = sb("selector", [PARTS * BC, BC])
        alog = sb("A_log", [P, DIRS, C2, DS])
        ps = core.psum("w_ps", [P, 4, 512], on=tmp)
        S = {n: core.sem("w_" + n) for n in ("loaded", "scaled", "ps", "kept", "exp_done", "done")}
        names = "fb"
        jobs = []
        for d in range(DIRS):
            for c in range(C2):
                for k in range(DC):
                    jobs.append((Wt["taps"][:, d, c, k, :], scaled[:, d, c, k, :], None))
        for c in range(C2):
            jobs.append((Wt["z"][:, c, :], win[:, C2 + c, :], None))
            jobs.append((Wt["out"][:, c, :], wout[:, c * P:(c + 1) * P], None))
        for d in range(DIRS):
            for c in range(C2):
                jobs.append((Wt["bc"][:, d, c, :], xp[0:BC, d, c * P:(c + 1) * P], None))
                for c2 in range(C2):
                    jobs.append((Wt["dt"][:, d, c, c2, :], xdt[:, d, c * P:(c + 1) * P], dtT[:, d, c2 * P:(c2 + 1) * P]))
        with nc.Block() as block:
            @block.sync
            def _(sp):
                n = 0

                def load(dst, src, **how):
                    sp.dma_start(dst, src, **how).then_inc(S["loaded"], 16)
                load(win[:], aps["L1_attn_in_proj_w"].rearrange("(c p) e -> p c e", p=P))
                load(wout[:], aps["L1_attn_out_proj_w"])
                load(sel[:], aps["selector"])
                for d, f in enumerate(names):
                    load(taps[:, d], aps[f"L1_attn_conv_w_{f}"].rearrange("(c p) k -> p c k", p=P))
                    x = aps[f"L1_attn_x_proj_w_{f}"]
                    load(xp[0:BC, d], x[DTR:DTR + BC])
                    load(xdt[:, d], x[0:DTR])
                    load(dtT[:, d], aps[f"L1_attn_dt_w_{f}"].rearrange("d r -> r d"), allow_slow_non_contiguous=True)
                    load(alog[:, d], aps[f"L1_attn_A_log_{f}"].rearrange("(c p) s -> p c s", p=P))
                    for name, key in (("conv_b", "conv_b"), ("dt_b", "dt_b"), ("D", "D")):
                        load(Wt[key][:, d], aps[f"L1_attn_{name}_{f}"].rearrange("(c p n) -> p c n", p=P, n=1), allow_slow_non_contiguous=True)
                load(Wt["ln1"][:, 0:1], aps["L1_attn_ln1_g"].rearrange("(p n) -> p n", n=1))
                load(Wt["ln1"][:, 1:2], aps["L1_attn_ln1_b"].rearrange("(p n) -> p n", n=1))

            loads = 16 * (3 + DIRS * 8 + 2)

            @block.scalar
            def _(act):
                act.wait_ge(S["loaded"], loads)
                nc.scalar.activation(Wt["A"][:].rearrange("p d c s -> p (d c s)"), alog[:].rearrange("p d c s -> p (d c s)"), ACT.Exp).then_inc(S["exp_done"], 1)

            @block.vector
            def _(dve):
                dve.wait_ge(S["loaded"], loads)
                for d in range(DIRS):
                    for c in range(C2):
                        for k in range(DC):
                            last = nc.vector.tensor_scalar(scaled[:, d, c, k, :], win[:, c, :], taps[:, d, c, k:k + 1], None, ALU.mult)
                last.then_inc(S["scaled"], 1)
                nc.vector.tensor_copy(Wt["sel"][:], sel[:].unsqueeze(2).broadcast_to([PARTS * BC, BC, P]))
                nc.vector.memset(Wt["one"][:], 1.0)
                dve.wait_ge(S["exp_done"], 1)
                a = Wt["A"][:].rearrange("p d c s -> p (d c s)")
                nc.vector.tensor_scalar(a, a, -1.0, None, ALU.mult)
                for n, (dst, _, rhs) in enumerate(jobs):
                    dve.wait_ge(S["ps"], n + 1)
                    nc.vector.tensor_copy(dst, ps[:, n % 4, 0:dst.shape[-1]]).then_inc(S["kept"], 1)
                dve.wait_ge(S["kept"], len(jobs))

            @block.tensor
            def _(pe):
                pe.wait_ge(S["scaled"], 1)
                for n, (dst, src, rhs) in enumerate(jobs):
                    at(pe, S["kept"], n - 3)
                    if rhs is None:
                        k = src.shape[0]
                        nc.tensor.transpose(ps[:, n % 4, 0:k], src, core.ident[0:k, 0:k]).then_inc(S["ps"], 1)
                    else:
                        nc.tensor.matmul(ps[:, n % 4, 0:P], src, rhs, start=True, stop=True).then_inc(S["ps"], 1)


def mixer(core, Hr, OD):
    nc, B, aps = core.nc, core.B, core.aps
    NP = B // G
    live = lambda i, lag: not isinstance(i, int) or 0 <= i - lag < NP
    on = ExitStack()
    with on:
        sb = lambda name, shape, dt=F32: core.sbuf("s_" + name, shape, dt, on=on)
        Wt = {"taps": sb("w_taps", [P, DIRS, C2, DC, P]), "z": sb("w_z", [P, C2, P]), "out": sb("w_out", [P, C2, P]),
              "bc": sb("w_bc", [P, DIRS, C2, BC]), "dt": sb("w_dt", [P, DIRS, C2, C2, P]), "sel": sb("w_sel", [PARTS * BC, BC, P], BF16),
              "A": sb("A", [P, DIRS, C2, DS]), "conv_b": sb("conv_b", [P, DIRS, C2, 1]), "dt_b": sb("dt_b", [P, DIRS, C2, 1]),
              "D": sb("D", [P, DIRS, C2, 1]), "ln1": sb("ln1", [P, 2]), "one": sb("one", [P, 1])}
        mixer_weights(core, Wt, on)
        PADW = T + 2 * (DC - 1)
        xn = sb("xn", [P, G * TC, P])
        xT = sb("xT", [P, G, PADW])
        xc = [sb(f"xc{n}", [P, DIRS, C2, W]) for n in range(2)]
        z = [sb(f"z{n}", [P, C2, W]) for n in range(2)]
        dt = [sb(f"dt{n}", [P, DIRS, C2, W]) for n in range(2)]
        ux = [sb(f"ux{n}", [P, DIRS, C2, W]) for n in range(2)]
        bcs = [sb(f"bc_parts{n}", [PARTS * BC, DIRS, W], BF16) for n in range(2)]
        rest, part2 = sb("bc_rest", [BC, W]), sb("bc_part2", [BC, W], BF16)
        e_abs, e_one, e_ln = sb("exp_abs", [P, C2, W]), sb("exp_plus_1", [P, C2, W]), sb("ln", [P, C2, W])
        dA = [sb(f"dA{n}", [P, DIRS, C2, G, T]) for n in range(2)]
        bsb = [sb(f"B_rows{n}", [P, DIRS, W]) for n in range(2)]
        R = core.X[:, 0:8192].rearrange("p (n d c w) -> p n d c w", n=4, d=DIRS, c=C2)
        yg = sb("y_gated", [P, C2, W])
        o = sb("out", [P, G * TC, D])
        YP = core.psum("s_y", [P, C2, W], on=on)
        BP = core.psum("s_B", [P, DIRS, W], on=on)
        CP = core.psum("s_C", [P, DIRS, W], on=on)
        PR = core.psum("s_prep", [P, 2, 512], on=on)
        S = {n: core.sem("s_" + n) for n in (
            "xn_ready", "prep_ps", "prep_read0", "prep_read1", "silu_done", "bc_part1", "bc_rest", "bc_part2", "bc_ready", "abs_done",
            "relu_done", "exp_done", "plus1_done", "ln_done", "corr_done", "ln_corr", "dt_ready", "u_ready", "B_ps", "C_ps",
            "B_ready", "dA_ready", "in_ready", "scanned", "part_ready", "summed", "y_read", "y_skip", "gated", "out_ps", "out_read",
            "stats_done", "out_stored", "pads", "x_saved")}
        flat = lambda t: t.rearrange("p c w -> p (c w)")
        read = lambda u: S[f"prep_read{u % 2}"]

        xsave = nc.dram_tensor("x_saved", [P, core.NT * D], F32, kind="Internal").ap()
        with nc.Block() as block:
            @block.sync
            def _(sp):
                sp.dma_start(xsave, core.X[:, 0:core.NT * D]).then_inc(S["x_saved"], 16)
                sp.wait_ge(S["x_saved"], 16)

            @block.vector
            def _(dve):
                nc.vector.memset(xT[:], 0.0)
                for n in range(2):
                    nc.vector.memset(dA[n][:, 0, :, :, 0:1], 0.0)
                    last = nc.vector.memset(dA[n][:, 1, :, :, T - 1:T], 0.0)
                last.then_inc(S["pads"], 1)
                dve.wait_ge(S["pads"], 1)

        with nc.Block() as block:
            @block.sync
            def _(sp):
                def emit(i, u):
                    if live(i, 2):
                        j = i - 2
                        sp.wait_ge(S["stats_done"], j + 1)
                        sp.dma_start(OD[ds(j * (G * TC), G * TC)].rearrange("n p d -> p n d"), o[:]).then_inc(S["out_stored"], 16)
                rolled(sp, NP, 2, 3, emit, ring=2)
                sp.wait_ge(S["out_stored"], 16 * NP)

            @block.gpsimd
            def _(pool):
                def inputs(j, par, s):
                    pool.wait_ge(S["B_ready"], j * DS + (s + 1))
                    if s == 0:
                        pool.wait_ge(S["u_ready"], DIRS * (j + 1))
                    at(pool, S["summed"], j * DS + (s - 3))
                    nc.gpsimd.tensor_tensor(R[:, s % 4], ux[par][:], bsb[s % 2][:].unsqueeze(2).broadcast_to([P, DIRS, C2, W]),
                                            ALU.mult).then_inc(S["in_ready"], 1)

                def emit(i, u):
                    if live(i, 1):
                        for s in range(1, DS):
                            inputs(i - 1, (u + 1) % 2, s)
                    if live(i, 0):
                        inputs(i, u, 0)
                rolled(pool, NP, 2, 3, emit, ring=2)

            @block.scalar
            def _(act):
                def front(j, par, s):
                    act.wait_ge(S["B_ps"], j * DS + (s + 1))
                    at(act, S["in_ready"], j * DS + (s - 1))
                    nc.scalar.activation(bsb[s % 2][:].rearrange("p d w -> p (d w)"), BP[:].rearrange("p d w -> p (d w)"), ACT.Copy).then_inc(S["B_ready"], 1)
                    if s == 0:
                        act.wait_ge(S["dt_ready"], DIRS * (j + 1))
                    at(act, S["scanned"], DIRS * (j * DS + (s - 1)))
                    for d in range(DIRS):
                        lo = 1 - d
                        for c in range(C2):
                            last = nc.scalar.activation(dA[s % 2][:, d, c, :, lo:lo + T - 1], dt[par][:, d, c, :].rearrange("p (g t) -> p g t", t=T)[:, :, lo:lo + T - 1],
                                                        ACT.Exp, scale=Wt["A"][:, d, c, s:s + 1])
                    last.then_inc(S["dA_ready"], 1)

                def softplus(i, u, d):
                    act.wait_ge(S["abs_done"], 2 * (DIRS * i + d) + 2)
                    nc.scalar.activation(flat(e_abs[:]), flat(e_abs[:]), ACT.Exp, scale=-1.0).then_inc(S["exp_done"], 1)
                    act.wait_ge(S["exp_done"], DIRS * i + (d + 1))
                    nc.scalar.activation(flat(e_one[:]), flat(e_abs[:]), ACT.Identity, bias=Wt["one"][:, 0:1]).then_inc(S["plus1_done"], 1)
                    act.wait_ge(S["plus1_done"], DIRS * i + (d + 1))
                    nc.scalar.activation(flat(e_ln[:]), flat(e_one[:]), ACT.Ln).then_inc(S["ln_done"], 1)

                def emit(i, u):
                    for s in range(DS):
                        if live(i, 1) and s < DS - 1:
                            front(i - 1, (u + 1) % 2, s + 1)
                        if live(i, 0):
                            n = USES * i
                            if s == 0:
                                act.wait_ge(S["prep_ps"], n + 1)
                                nc.scalar.activation(xT[:, :, DC - 1:DC - 1 + T], PR[:, 0, :].rearrange("p (g t) -> p g t", t=T), ACT.Identity,
                                                     scale=Wt["ln1"][:, 0:1], bias=Wt["ln1"][:, 1:2]).then_inc(read(0), 1)
                            if 1 <= s <= 4:
                                d, c = (s - 1) // C2, (s - 1) % C2
                                act.wait_ge(S["prep_ps"], n + s + 1)
                                at(act, S["y_skip"], i - 1)
                                nc.scalar.activation(xc[u][:, d, c, :], PR[:, s % 2, :], ACT.Identity, bias=Wt["conv_b"][:, d, c, :]).then_inc(read(s), 1)
                            if s == 5:
                                at(act, S["gated"], i - 1)
                                for c in range(C2):
                                    act.wait_ge(S["prep_ps"], n + 6 + c)
                                    nc.scalar.activation(z[u][:, c, :], PR[:, (5 + c) % 2, :], ACT.Identity).then_inc(read(5 + c), 1)
                                act.wait_ge(read(5), BANK_USES[1] * i + 3)
                                act.wait_ge(read(6), BANK_USES[0] * i + 4)
                                nc.scalar.activation(xc[u][:].rearrange("p d c w -> p (d c w)"), xc[u][:].rearrange("p d c w -> p (d c w)"), ACT.Silu)
                                nc.scalar.activation(flat(z[u][:]), flat(z[u][:]), ACT.Silu).then_inc(S["silu_done"], 1)
                            if 7 <= s <= 10:
                                d, c = (s - 7) // C2, (s - 7) % C2
                                use = 9 + (s - 7)
                                act.wait_ge(S["prep_ps"], n + use + 1)
                                at(act, S["corr_done"], DIRS * i + d)
                                bias = Wt["dt_b"][:, d, c, :]
                                nc.scalar.activation(e_abs[:, c, :], PR[:, use % 2, :], ACT.Abs, bias=bias).then_inc(S["abs_done"], 1)
                                nc.scalar.activation(dt[u][:, d, c, :], PR[:, use % 2, :], ACT.Relu, bias=bias).then_inc(read(use), 1)
                            if s == 8 or s == 10:
                                at(act, S["dt_ready"], DIRS * i + (s - 8) // 2)
                                softplus(i, u, (s - 8) // 2)
                        if s == 11 and live(i, 2):
                            j = i - 2
                            act.wait_ge(S["out_ps"], j + 1)
                            at(act, S["out_stored"], 16 * j)
                            nc.scalar.activation(o[:].rearrange("p n d -> p (n d)"), PR[:, 1, :], ACT.Copy).then_inc(S["out_read"], 1)
                        if s == DS - 1 and live(i, 0):
                            front(i, u, 0)
                rolled(act, NP, 2, 3, emit, ring=2)

            @block.vector
            def _(dve):
                tt, stt = nc.vector.tensor_tensor, nc.vector.scalar_tensor_tensor

                def scan(j, s):
                    n = j * DS + s
                    dve.wait_ge(S["dA_ready"], n + 1)
                    dve.wait_ge(S["in_ready"], n + 1)
                    for d in range(DIRS):
                        r, a = flat(R[:, s % 4, d]), dA[s % 2][:, d].rearrange("p c g t -> p (c g t)")
                        if d:
                            r, a = r[:, ::-1], a[:, ::-1]
                        nc.vector.tensor_tensor_scan(r, a, r, 0.0, ALU.mult, ALU.add).then_inc(S["scanned"], 1)
                    dve.wait_ge(S["C_ps"], n + 1)
                    for d in range(DIRS):
                        dve.wait_ge(S["scanned"], DIRS * n + (d + 1))
                        r = R[:, s % 4, d]
                        last = tt(r, r, CP[:, d, :].unsqueeze(1).broadcast_to([P, C2, W]), ALU.mult)
                    last.then_inc(S["part_ready"], 1)

                def emit(i, u):
                    for s in range(DS):
                        if s == 0 and live(i, 0):
                            at(dve, S["prep_ps"], USES * (i - 1) + 1)
                            for k in range(G * TC):
                                c = i * (G * TC) + k
                                last = nc.vector.tensor_scalar(xn[:, k, :], Hr[:, ds(c * D, D)], core.rstd[:, ds(c, 1)], core.nmr[:, ds(c, 1)],
                                                               ALU.mult, ALU.add)
                            last.then_inc(S["xn_ready"], 1)
                        if live(i, 1):
                            scan(i - 1, s)
                        if s == 0 and live(i, 2):
                            j, par = i - 2, u
                            dve.wait_ge(S["summed"], DS * (j + 1))
                            at(dve, S["out_ps"], j)
                            for c in range(C2):
                                last = stt(out=yg[:, c, :], in0=xc[par][:, 0, c, :], scalar=Wt["D"][:, 0, c, :], in1=YP[:, c, :], op0=ALU.mult, op1=ALU.add)
                            last.then_inc(S["y_read"], 1)
                            dve.wait_ge(S["y_read"], j + 1)
                            for c in range(C2):
                                last = stt(out=yg[:, c, :], in0=xc[par][:, 1, c, :], scalar=Wt["D"][:, 1, c, :], in1=yg[:, c, :], op0=ALU.mult, op1=ALU.add)
                            last.then_inc(S["y_skip"], 1)
                            dve.wait_ge(S["y_skip"], j + 1)
                            tt(flat(yg[:]), flat(yg[:]), flat(z[par][:]), ALU.mult).then_inc(S["gated"], 1)
                        if s in (6, 7) and live(i, 0):
                            d = s - 6
                            use = 7 + d
                            n = DIRS * i + d
                            dve.wait_ge(S["prep_ps"], USES * i + use + 1)
                            at(dve, S["C_ps"], DS * (i - 1))
                            psb = PR[0:BC, use % 2, :]
                            nc.vector.tensor_copy(bcs[u][0:BC, d, :], psb).then_inc(S["bc_part1"], 1)
                            dve.wait_ge(S["bc_part1"], n + 1)
                            tt(rest[:], psb, bcs[u][0:BC, d, :], ALU.subtract).then_inc(S["bc_rest"], 1)
                            dve.wait_ge(S["bc_rest"], n + 1)
                            nc.vector.tensor_copy(part2[:], rest[:]).then_inc(S["bc_part2"], 1)
                            dve.wait_ge(S["bc_part2"], n + 1)
                            nc.vector.tensor_copy(bcs[u][BC:2 * BC, d, :], part2[:]).then_inc(read(use), 1)
                            tt(bcs[u][2 * BC:3 * BC, d, :], rest[:], part2[:], ALU.subtract).then_inc(S["bc_ready"], 1)
                        if s in (10, 12) and live(i, 0):
                            d = (s - 10) // 2
                            n = DIRS * i + d
                            dve.wait_ge(S["ln_done"], n + 1)
                            stt(out=flat(e_one[:]), in0=flat(e_one[:]), scalar=-1.0, in1=flat(e_abs[:]), op0=ALU.add, op1=ALU.subtract).then_inc(S["corr_done"], 1)
                            dve.wait_ge(S["corr_done"], n + 1)
                            tt(flat(e_ln[:]), flat(e_ln[:]), flat(e_one[:]), ALU.subtract).then_inc(S["ln_corr"], 1)
                            dve.wait_ge(S["ln_corr"], n + 1)
                            tt(flat(dt[u][:, d]), flat(dt[u][:, d]), flat(e_ln[:]), ALU.add).then_inc(S["dt_ready"], 1)
                            dve.wait_ge(S["dt_ready"], n + 1)
                            tt(flat(ux[u][:, d]), flat(dt[u][:, d]), flat(xc[u][:, d]), ALU.mult).then_inc(S["u_ready"], 1)
                        if s == 12 and live(i, 2):
                            j = i - 2
                            dve.wait_ge(S["out_read"], j + 1)
                            for k in range(G * TC):
                                c = j * (G * TC) + k
                                last = nc.vector.bn_stats(core.st[:, ds(c, 1), :].rearrange("p n k -> p (n k)"), o[:, k, :])
                            last.then_inc(S["stats_done"], 1)
                rolled(dve, NP, 2, 3, emit, ring=2)
                dve.wait_ge(S["stats_done"], NP)

            @block.tensor
            def _(pe):
                mm = nc.tensor.matmul

                def b_rows(j, par, s):
                    if s == 0:
                        pe.wait_ge(S["bc_ready"], DIRS * (j + 1))
                    at(pe, S["B_ready"], j * DS + s)
                    for d in range(DIRS):
                        last = mm(BP[:, d, :], Wt["sel"][:, s, :], bcs[par][:, d, :], start=True, stop=True)
                    last.then_inc(S["B_ps"], 1)

                def c_rows(j, par, s):
                    at(pe, S["part_ready"], j * DS + s)
                    for d in range(DIRS):
                        last = mm(CP[:, d, :], Wt["sel"][:, DS + s, :], bcs[par][:, d, :], start=True, stop=True)
                    last.then_inc(S["C_ps"], 1)

                def add_up(j, s):
                    at(pe, S["part_ready"], j * DS + (s + 1))
                    if s == 0:
                        at(pe, S["y_read"], j)
                    for c in range(C2):
                        for d in range(DIRS):
                            last = mm(YP[:, c, :], core.ident[:], R[:, s % 4, d, c, :], start=(s == 0 and d == 0), stop=(s == DS - 1 and d == 1))
                    last.then_inc(S["summed"], 1)

                def prep(i, u, use):
                    bank = PR[:, use % 2, :]
                    at(pe, read(use), BANK_USES[use % 2] * i + use // 2)
                    if use == 1:
                        at(pe, S["out_read"], i - 2)
                    if use == 0:
                        pe.wait_ge(S["xn_ready"], i + 1)
                        for k in range(G * TC):
                            last = nc.tensor.transpose(bank[:, k * P:(k + 1) * P], xn[:, k, :], core.ident[:])
                    elif use <= 4:
                        d, c = (use - 1) // C2, (use - 1) % C2
                        if use == 1:
                            pe.wait_ge(read(0), BANK_USES[0] * i + 1)
                        for k in range(DC):
                            off = k if d == 0 else 2 * (DC - 1) - k
                            last = mm(bank, Wt["taps"][:, d, c, k, :], xT[:, :, off:off + T], start=(k == 0), stop=(k == DC - 1))
                    elif use <= 6:
                        last = mm(bank, Wt["z"][:, use - 5, :], xT[:, :, DC - 1:DC - 1 + T], start=True, stop=True)
                    elif use <= 8:
                        d = use - 7
                        pe.wait_ge(S["silu_done"], i + 1)
                        for c in range(C2):
                            last = mm(bank[0:BC], Wt["bc"][:, d, c, :], xc[u][:, d, c, :], start=(c == 0), stop=(c == C2 - 1))
                    else:
                        d, c2 = (use - 9) // C2, (use - 9) % C2
                        for c in range(C2):
                            last = mm(bank, Wt["dt"][:, d, c, c2, :], xc[u][:, d, c, :], start=(c == 0), stop=(c == C2 - 1))
                    last.then_inc(S["prep_ps"], 1)

                USES_AT = {0: (0,), 1: (1,), 2: (2,), 3: (3,), 4: (4,), 5: (5, 6), 6: (7,), 7: (8, 9), 8: (10,), 9: (11,), 10: (12,)}

                def emit(i, u):
                    for s in range(DS):
                        if live(i, 1):
                            if s < DS - 1:
                                b_rows(i - 1, (u + 1) % 2, s + 1)
                            c_rows(i - 1, (u + 1) % 2, s)
                            if s > 0:
                                add_up(i - 1, s - 1)
                        if s == 0 and live(i, 2):
                            add_up(i - 2, DS - 1)
                        if live(i, 0):
                            for use in USES_AT.get(s, ()):
                                prep(i, u, use)
                        if s == 11 and live(i, 2):
                            j = i - 2
                            pe.wait_ge(S["gated"], j + 1)
                            if live(i, 0):
                                pe.wait_ge(read(11), BANK_USES[1] * (i + 1))
                            for k in range(G * TC):
                                for c in range(C2):
                                    last = mm(PR[:, 1, k * D:(k + 1) * D], yg[:, c, k * P:(k + 1) * P], Wt["out"][:, c, :], start=(c == 0), stop=(c == C2 - 1))
                            last.then_inc(S["out_ps"], 1)
                        if s == DS - 1 and live(i, 0):
                            b_rows(i, u, 0)
                rolled(pe, NP, 2, 3, emit, ring=2)

        s_back = core.sem("s_x_back")
        with nc.Block() as block:
            @block.sync
            def _(sp):
                sp.dma_start(core.X[:, 0:core.NT * D], xsave).then_inc(s_back, 16)
                sp.wait_ge(s_back, 16)


GRID = 8
KT = 4
KB = KT // TC
TURN = float(np.nextafter(np.float32(2 * np.pi), np.float32(0)))
MAGIC = 1.5 * 2.0 ** 23
NBASIS = 16
B_S1, B_C1, B_S2, B_D, B_DS1, B_DC1, B_DS2, B_E, B_ES1, B_EC1, B_ES2, B_ED, B_EDS1, B_EDC1, B_EDS2, B_EE = range(NBASIS)
COS, SIN = 0, 1
KAN_TERMS = {
    B_S1: (1.0, [(1, SIN, 1), (1, SIN, 3), (1, SIN, 5), (1, SIN, 7)]), B_DS1: (1.0, [(1, SIN, 3), (1, SIN, 5)]),
    B_ES1: (1.0, [(1, SIN, 5), (1, SIN, 7)]), B_EDS1: (1.0, [(1, SIN, 7)]),
    B_C1: (1.0, [(1, COS, 1), (-1, COS, 3), (1, COS, 5), (-1, COS, 7)]), B_DC1: (1.0, [(1, COS, 3), (-1, COS, 5)]),
    B_EC1: (1.0, [(1, COS, 5), (-1, COS, 7)]), B_EDC1: (1.0, [(1, COS, 7)]),
    B_S2: (2.0, [(1, SIN, 2), (1, SIN, 6)]), B_ES2: (2.0, [(1, SIN, 6)]), B_DS2: (2.0, [(1, SIN, 4)]), B_EDS2: (2.0, [(1, SIN, 8)]),
    B_D: (0.5, [(1, COS, 2), (-1, COS, 6)]), B_ED: (0.5, [(1, COS, 6)]), B_E: (0.5, [(1, COS, 4)]), B_EE: (0.5, [(1, COS, 8)]),
}


def kan_weights(core, WT, const):
    nc, aps = core.nc, core.aps
    tmp = ExitStack()
    with tmp:
        coef = core.sbuf("kw_coef", [P, 2, D * GRID], on=tmp)
        comb = core.sbuf("kw_combined", [P, NBASIS, D], on=tmp)
        minus2 = core.sbuf("kw_minus_two", [P, P], on=tmp)
        ps = core.psum("kw_ps", [P, NBASIS // 4 + 1, 512], on=tmp)
        s_in, s_comb, s_ps, s_wt, s_const = (core.sem(f"kw_{n}") for n in ("loaded", "combined", "ps", "kept", "const"))
        with nc.Block() as block:
            @block.sync
            def _(sp):
                sp.dma_start(coef[:], aps["L1_attn_kan_coef"].rearrange("p j i k -> j p (i k)")).then_inc(s_in, 16)

            @block.vector
            def _(dve):
                chain = Chain(core, dve, "kw_dve_chain")
                raw = lambda kind, k: coef[:, kind, :].rearrange("p (i k) -> p i k", k=GRID)[:, :, k - 1]
                nc.vector.memset(minus2[:], -2.0)
                dve.wait_ge(s_in, 16)
                depth = max(len(terms) for _, terms in KAN_TERMS.values())
                for n in range(depth):
                    for m, (factor, terms) in KAN_TERMS.items():
                        if n == 0:
                            last = nc.vector.tensor_scalar(comb[:, m, :], raw(*terms[0][1:]), factor, None, ALU.mult)
                        elif n < len(terms):
                            sign, kind, k = terms[n]
                            last = nc.vector.scalar_tensor_tensor(out=comb[:, m, :], in0=raw(kind, k), scalar=sign * factor, in1=comb[:, m, :],
                                                                  op0=ALU.mult, op1=ALU.add)
                    chain.step(last)
                nc.vector.tensor_copy(minus2[0:1, 0:1], minus2[0:1, 0:1]).then_inc(s_comb, 1)
                dve.wait_ge(s_ps, 1)
                nc.vector.tensor_copy(WT[:].rearrange("p m j -> p (m j)"), ps[:, 0:NBASIS // 4, :].rearrange("p m j -> p (m j)")).then_inc(s_wt, 1)
                dve.wait_ge(s_const, 1)
                chain.step(nc.vector.tensor_copy(const[:], ps[:, NBASIS // 4, 0:D]))

            @block.tensor
            def _(pe):
                pe.wait_ge(s_comb, 1)
                for m in range(NBASIS):
                    last = nc.tensor.transpose(ps[:, m // 4, (m % 4) * P:(m % 4 + 1) * P], comb[:, m, :], core.ident[:])
                last.then_inc(s_ps, 1)
                pe.wait_ge(s_wt, 1)
                nc.tensor.matmul(ps[:, NBASIS // 4, 0:D], minus2[:], WT[:, B_EE, :], start=True, stop=True).then_inc(s_const, 1)


def kan(core, Hr, OD):
    nc, NT, X, aps = core.nc, core.NT, core.X, core.aps
    NG, W4 = NT // KT, KT * P
    live = lambda i, lag: not isinstance(i, int) or 0 <= i - lag < NG
    on = ExitStack()
    with on:
        sb = lambda name, shape, dt=F32: core.sbuf("k_" + name, shape, dt, on=on)
        WT, const = sb("coef_T", [P, NBASIS, D]), sb("constant", [P, D])
        kan_weights(core, WT, const)
        ln = sb("ln_cols", [P, 2])
        quarter = sb("half_pi", [P, 1])
        od = [sb(f"od{n}", [P, KT, D]) for n in range(2)]
        xn = sb("xn", [P, KT, D])
        f, whole, t, at_ = sb("turns", [P, W4]), sb("whole", [P, W4]), sb("angle", [P, W4]), sb("abs_angle", [P, W4])
        q = sb("squares", [P, W4])
        basis = [sb(f"basis{n}", [P, NBASIS, W4]) for n in range(2)]
        gate = [sb(f"gate{n}", [P, KB, D]) for n in range(2)]
        hb, y1, y2 = (sb(n, [P, W4]) for n in ("h_const", "y_plus_h", "y_gated"))
        psT = core.psum("k_psT", [P, W4], on=on)
        psY = core.psum("k_psY", [P, 2, W4], on=on)
        S = {n: core.sem("k_" + n) for n in (
            "ln_loaded", "ln_ready", "od_loaded", "gate_loaded", "xn_ready", "xT_ps", "f_ready", "rounded", "reduced", "sin_done", "abs_done",
            "cos_done", "q_ready", "s2_done", "D_ready", "D_products", "D_square", "E_ready", "E_products", "E_square",
            "products", "hb_ready", "y1_ready", "gated", "x_updated", "passed")}
        with nc.Block() as block:
            @block.sync
            def _(sp):
                for n, name in enumerate(("g", "b")):
                    sp.dma_start(ln[:, n:n + 1], aps[f"L1_attn_ln_{name}"].rearrange("(p n) -> p n", n=1)).then_inc(S["ln_loaded"], 16)

                def emit(i, u):
                    if live(i, 0):
                        at_alone(sp, S["od_loaded"], 16 * i, S["passed"])
                        at(sp, S["xn_ready"], i - 1)
                        sp.dma_start(od[u][:], OD[ds(i * KT, KT)].rearrange("n p d -> p n d")).then_inc(S["od_loaded"], 16)
                        at(sp, S["gate_loaded"], 16 * i)
                        at(sp, S["gated"], i - 1)
                        sp.dma_start(gate[u][:], core.modrow[2, ds(i * KB, KB), :].partition_broadcast(P)).then_inc(S["gate_loaded"], 16)
                rolled(sp, NG, 1, 3, emit, ring=2)

            @block.vector
            def _(dve):
                tt, ts = nc.vector.tensor_tensor, nc.vector.tensor_scalar
                nc.vector.memset(quarter[:], float(np.pi / 2))
                dve.wait_ge(S["ln_loaded"], 32)
                ts(ln[:], ln[:], float(1 / (2 * np.pi)), None, ALU.mult).then_inc(S["ln_ready"], 1)

                def emit(i, u):
                    if live(i, 0):
                        bs = basis[u]
                        dve.wait_ge(S["od_loaded"], 16 * (i + 1))
                        at(dve, S["xT_ps"], i)
                        for k in range(KT):
                            c = i * KT + k
                            last = ts(xn[:, k, :], od[u][:, k, :], core.rstd[:, ds(c, 1)], core.nmr[:, ds(c, 1)], ALU.mult, ALU.add)
                        last.then_inc(S["xn_ready"], 1)
                        dve.wait_ge(S["f_ready"], i + 1)
                        ts(whole[:], f[:], MAGIC, MAGIC, ALU.add, ALU.subtract).then_inc(S["rounded"], 1)
                        dve.wait_ge(S["rounded"], i + 1)
                        tt(t[:], f[:], whole[:], ALU.subtract).then_inc(S["reduced"], 1)
                        dve.wait_ge(S["cos_done"], i + 1)
                        tt(bs[:, B_S2, :], bs[:, B_S1, :], bs[:, B_C1, :], ALU.mult).then_inc(S["s2_done"], 1)
                        dve.wait_ge(S["q_ready"], i + 1)
                        ts(bs[:, B_D, :], q[:], -2.0, 2.0, ALU.mult, ALU.add).then_inc(S["D_ready"], 1)
                        dve.wait_ge(S["s2_done"], i + 1)
                        dve.wait_ge(S["D_ready"], i + 1)
                        tt(bs[:, B_DS1:B_DS2 + 1, :], bs[:, B_S1:B_S2 + 1, :], bs[:, B_D, :].unsqueeze(1).broadcast_to([P, 3, W4]), ALU.mult)\
                            .then_inc(S["D_products"], 1)
                        dve.wait_ge(S["D_square"], i + 1)
                        ts(bs[:, B_E, :], q[:], -2.0, None, ALU.add).then_inc(S["E_ready"], 1)
                        dve.wait_ge(S["E_ready"], i + 1)
                        dve.wait_ge(S["D_products"], i + 1)
                        tt(bs[:, B_ES1:B_EDS2 + 1, :], bs[:, B_S1:B_DS2 + 1, :], bs[:, B_E, :].unsqueeze(1).broadcast_to([P, 7, W4]), ALU.mult)\
                            .then_inc(S["E_products"], 1)
                    if live(i, 1):
                        j = i - 1
                        dve.wait_ge(S["products"], j + 1)
                        dve.wait_ge(S["hb_ready"], j + 1)
                        at(dve, S["gated"], j)
                        tt(y1[:], psY[:, (u + 1) % 2, :], hb[:], ALU.add).then_inc(S["y1_ready"], 1)
                rolled(dve, NG, 1, 3, emit, ring=2)

            @block.scalar
            def _(act):
                func = nc.scalar.activation
                act.wait_ge(S["ln_ready"], 1)

                def emit(i, u):
                    if live(i, 0):
                        bs = basis[u]
                        act.wait_ge(S["xT_ps"], i + 1)
                        at(act, S["reduced"], i)
                        func(f[:], psT[:], ACT.Identity, scale=ln[:, 0:1], bias=ln[:, 1:2]).then_inc(S["f_ready"], 1)
                        act.wait_ge(S["reduced"], i + 1)
                        at(act, S["products"], i - 1)
                        func(bs[:, B_S1, :], t[:], ACT.Sin, scale=TURN).then_inc(S["sin_done"], 1)
                        at(act, S["cos_done"], i)
                        func(at_[:], t[:], ACT.Abs).then_inc(S["abs_done"], 1)
                        act.wait_ge(S["abs_done"], i + 1)
                        func(bs[:, B_C1, :], at_[:], ACT.Sin, scale=-TURN, bias=quarter[:, 0:1]).then_inc(S["cos_done"], 1)
                        act.wait_ge(S["sin_done"], i + 1)
                        at(act, S["E_ready"], i)
                        func(q[:], bs[:, B_S1, :], ACT.Square, scale=float(np.sqrt(2))).then_inc(S["q_ready"], 1)
                        act.wait_ge(S["D_ready"], i + 1)
                        func(q[:], bs[:, B_D, :], ACT.Square).then_inc(S["D_square"], 1)
                        act.wait_ge(S["E_ready"], i + 1)
                        func(bs[:, B_EE, :], bs[:, B_E, :], ACT.Square).then_inc(S["E_square"], 1)
                rolled(act, NG, 1, 3, emit, ring=2)

            @block.tensor
            def _(pe):
                def emit(i, u):
                    if live(i, 0):
                        pe.wait_ge(S["xn_ready"], i + 1)
                        at(pe, S["f_ready"], i)
                        for k in range(KT):
                            last = nc.tensor.transpose(psT[:, k * P:(k + 1) * P], xn[:, k, :], core.ident[:])
                        last.then_inc(S["xT_ps"], 1)
                    if live(i, 1):
                        j, n = i - 1, (u + 1) % 2
                        pe.wait_ge(S["E_products"], j + 1)
                        pe.wait_ge(S["E_square"], j + 1)
                        at(pe, S["y1_ready"], j - 1)
                        for k in range(KT):
                            for m in range(NBASIS):
                                last = nc.tensor.matmul(psY[:, n, k * D:(k + 1) * D], basis[n][:, m, k * P:(k + 1) * P], WT[:, m, :],
                                                        start=(m == 0), stop=(m == NBASIS - 1))
                        last.then_inc(S["products"], 1)
                rolled(pe, NG, 1, 3, emit, ring=2)

            @block.gpsimd
            def _(pool):
                tt = nc.gpsimd.tensor_tensor

                def emit(i, u):
                    if live(i, 1):
                        j, n = i - 1, (u + 1) % 2
                        at(pool, S["y1_ready"], j)
                        tt(hb[:].rearrange("p (n d) -> p n d", d=D), Hr[:, ds(j * W4, W4)].rearrange("p (n d) -> p n d", d=D),
                           const[:].unsqueeze(1).broadcast_to([P, KT, D]), ALU.add).then_inc(S["hb_ready"], 1)
                        pool.wait_ge(S["gate_loaded"], 16 * (j + 1))
                        pool.wait_ge(S["y1_ready"], j + 1)
                        at(pool, S["x_updated"], j)
                        tt(y2[:].rearrange("p (b n d) -> p b n d", b=KB, d=D), y1[:].rearrange("p (b n d) -> p b n d", b=KB, d=D),
                           gate[n][:].unsqueeze(2).broadcast_to([P, KB, TC, D]), ALU.mult).then_inc(S["gated"], 1)
                        pool.wait_ge(S["gated"], j + 1)
                        x = X[:, ds(j * W4, W4)]
                        tt(x, x, y2[:], ALU.add).then_inc(S["x_updated"], 1)
                rolled(pool, NG, 1, 3, emit, ring=2)


def layer1_attention(core):
    OD = core.nc.dram_tensor("mixer_out", [core.NT, P, D], F32, kind="Internal").ap()
    on = ExitStack()
    with on:
        Hr = core.sbuf("h_rows1", [P, core.NT * D], on=on)
        ln_stats(core, "lnC")
        modulated(core, 1, Hr, None, 8)
        ln_stats(core, "lnC1", Hr, 1e-12)
        mixer(core, Hr, OD)
        with core.nc.Block() as block:
            ln_finish(core, "lnC2", core.st, 1e-12, block)
        kan(core, Hr, OD)


def experts1(core, XS, YS):
    nc, aps = core.nc, core.aps
    on = ExitStack()
    with on:
        sb = lambda name, shape, dt=F32: core.sbuf("e1_" + name, shape, dt, on=on)
        w1, w2 = sb("w1", [P, E, F]), sb("w2", [P, E, FC, D])
        b1, b2 = sb("b1", [P, E, F]), sb("b2", [P, E, D])
        x = [sb(f"x{n}", [CAP, D]) for n in range(2)]
        xT = sb("xT", [P, CAP])
        h1, g = sb("h1", [CAP, F]), sb("gelu", [CAP, F])
        gT = sb("gelu_T", [P, FC, CAP])
        y = [sb(f"y{n}", [CAP, D]) for n in range(2)]
        psX, ps1, psY = (core.psum("e1_ps" + n, [P, 512], on=on) for n in "X1Y")
        psG = core.psum("e1_psG", [P, FC, P], on=on)
        S = start_counts(core, "e1", ["w_loaded", "x_loaded", "xT_ps", "xT_ready", "h1_ps", "h1_ready", "gelu_ready", "gT_ps", "gT_ready",
                                      "y_ps", "y_ready", "y_stored"])
        live = lambda i, lag: not isinstance(i, int) or 0 <= i - lag < E
        slots_of = lambda table, e: table[ds(e * CAP, CAP), :]
        of = lambda t, e: t[:, ds(e, 1)].rearrange("p n f -> p (n f)")

        with nc.Block() as block:
            @block.sync
            def _(sp):
                sp.dma_start(w1[:], aps["L1_ffn_w1"].rearrange("e d f -> d e f")).then_inc(S["w_loaded"], 16)
                sp.dma_start(b1[:], aps["L1_ffn_b1"].partition_broadcast(P)).then_inc(S["w_loaded"], 16)
                sp.dma_start(w2[:].rearrange("p e c d -> p (e c) d"), aps["L1_ffn_w2"].rearrange("e (c f) d -> f (e c) d", f=P)).then_inc(S["w_loaded"], 16)
                sp.dma_start(b2[:], aps["L1_ffn_b2"].partition_broadcast(P)).then_inc(S["w_loaded"], 16)

                def emit(i, u):
                    if live(i, 0):
                        upto(sp, S["x_loaded"], 16 * i)
                        upto(sp, S["xT_ps"], i - 1)
                        sp.dma_start(x[u][:], slots_of(XS, i)).then_inc(S["x_loaded"], 16)
                    if live(i, 1):
                        j = i - 1
                        upto(sp, S["y_ready"], j + 1)
                        upto(sp, S["y_stored"], 16 * j)
                        sp.dma_start(slots_of(YS, j), y[(u + 1) % 2][:]).then_inc(S["y_stored"], 16)
                rolled(sp, E, 1, 2, emit, ring=2)
                upto(sp, S["y_stored"], 16 * E)

            @block.tensor
            def _(pe):
                mm = nc.tensor.matmul
                upto(pe, S["w_loaded"], 64)

                def emit(i, u):
                    if live(i, 0):
                        upto(pe, S["x_loaded"], 16 * (i + 1))
                        upto(pe, S["xT_ready"], i)
                        nc.tensor.transpose(psX[:, 0:CAP], x[u][:], core.ident[0:CAP, 0:CAP]).then_inc(S["xT_ps"], 1)
                    if live(i, 1):
                        j = i - 1
                        upto(pe, S["gelu_ready"], j + 1)
                        upto(pe, S["gT_ready"], j)
                        for c in range(FC):
                            last = nc.tensor.transpose(psG[:, c, 0:CAP], g[:, c * P:(c + 1) * P], core.ident[0:CAP, 0:CAP])
                        last.then_inc(S["gT_ps"], 1)
                    if live(i, 0):
                        upto(pe, S["xT_ready"], i + 1)
                        upto(pe, S["h1_ready"], i)
                        mm(ps1[0:CAP, :], xT[:], of(w1, i), start=True, stop=True).then_inc(S["h1_ps"], 1)
                    if live(i, 1):
                        upto(pe, S["gT_ready"], j + 1)
                        upto(pe, S["y_ready"], j)
                        for c in range(FC):
                            last = mm(psY[0:CAP, 0:D], gT[:, c, :], w2[:, ds(j, 1), c, :].rearrange("p n d -> p (n d)"), start=(c == 0), stop=(c == FC - 1))
                        last.then_inc(S["y_ps"], 1)
                rolled(pe, E, 1, 2, emit, ring=2)

            @block.scalar
            def _(act):
                def emit(i, u):
                    if live(i, 1):
                        j = i - 1
                        upto(act, S["gT_ps"], j + 1)
                        upto(act, S["y_ps"], j)
                        nc.scalar.activation(gT[:], psG[:, :, 0:CAP], ACT.Copy).then_inc(S["gT_ready"], 1)
                    if live(i, 0):
                        upto(act, S["h1_ready"], i + 1)
                        upto(act, S["gT_ps"], i)
                        nc.scalar.activation(g[:], h1[:], ACT.Gelu_apprx_tanh).then_inc(S["gelu_ready"], 1)
                rolled(act, E, 1, 2, emit, ring=2)

            @block.vector
            def _(dve):
                upto(dve, S["w_loaded"], 64)

                def emit(i, u):
                    if live(i, 0):
                        upto(dve, S["xT_ps"], i + 1)
                        upto(dve, S["h1_ps"], i)
                        nc.vector.tensor_copy(xT[:], psX[:, 0:CAP]).then_inc(S["xT_ready"], 1)
                        upto(dve, S["h1_ps"], i + 1)
                        upto(dve, S["gelu_ready"], i)
                        nc.vector.tensor_tensor(h1[:], ps1[0:CAP, :], of(b1, i)[0:CAP], ALU.add).then_inc(S["h1_ready"], 1)
                    if live(i, 1):
                        j = i - 1
                        upto(dve, S["y_ps"], j + 1)
                        upto(dve, S["y_stored"], 16 * (j - 1))
                        nc.vector.tensor_tensor(y[(u + 1) % 2][:], psY[0:CAP, 0:D], of(b2, j)[0:CAP], ALU.add).then_inc(S["y_ready"], 1)
                rolled(dve, E, 1, 2, emit, ring=2)


def ffn1(core):
    nc, NT = core.nc, core.NT
    rows = E * CAP
    XS = nc.dram_tensor("slot_inputs1", [rows, D], F32, kind="Internal").ap()
    YS = nc.dram_tensor("slot_outputs1", [(rows // P + 1) * P, D], F32, kind="Internal").ap()
    on = ExitStack()
    with on:
        slots, weights = [core.sbuf("slots1", [P, NT], U32, on=on)], [core.sbuf("weights1", [P, NT], on=on)]
        scratch = ExitStack()
        with scratch:
            Hr = core.sbuf("h_rows2", [P, NT * D], on=scratch)
            L = core.sbuf("logits1", [P, NT * E], on=scratch)
            fill_zero(core, "xs1", XS, rows // P)
            fill_zero(core, "ys1", YS, rows // P + 1)
            ln_stats(core, "lnD")
            modulated(core, 1, Hr, L, 6)
            moe_route(core, 1, L, slots, weights)
            scatter_rows(core, "sc1", Hr, slots, XS, rows)
        experts1(core, XS, YS[0:rows, :])
        gather_and_add(core, "ga1", 1, slots, weights, YS)


def store_x(core):
    with core.nc.Block() as block:
        s_stored = core.sem("out_stored")

        @block.sync
        def _(sp):
            sp.dma_start(core.aps["out_tiles"].rearrange("n p d -> p n d"), core.X[:, 0:core.NT * D].rearrange("p (n d) -> p n d", d=D))\
                .then_inc(s_stored, 16)
            sp.wait_ge(s_stored, 16)


def adaln_two_layers(nc, aps, B):
    core = Core(nc, aps, B)
    with core.stack:
        load_and_modulate(core)
        ln_stats(core, "lnA")
        attention(core)
        ln_stats(core, "lnB")
        ffn0(core)
        core.next_stage()
        layer1_attention(core)
        core.next_stage()
        ffn1(core)
        store_x(core)


def shape_constants():
    out = {"ident": np.eye(P, dtype=np.float32)}
    inv_freq = (1.0 / (np.float32(10000.0) ** (np.arange(0, DH, 2, dtype=np.float32) / np.float32(DH)))).astype(np.float32)
    freqs = np.arange(T, dtype=np.float32)[:, None] * inv_freq[None, :]
    emb = np.concatenate([freqs, freqs], -1)
    out["rope_cos"] = np.tile(np.cos(emb).astype(np.float32).T, (H, 1))
    out["rope_sin"] = np.tile(np.sin(emb).astype(np.float32).T, (H, 1))
    rot = np.zeros((D, D), np.float32)
    for m in range(D):
        half = DH // 2
        rot[m + half if m % DH < half else m - half, m] = -1 if m % DH < half else 1
    out["rope_rot"] = rot
    out["selector"] = np.tile(np.eye(BC, dtype=np.float32), (PARTS, 1))
    out["rev_rank"] = np.tile(np.arange(E, 0, -1, dtype=np.float32), (P, 1))
    out["tri"] = np.triu(np.ones((P, P), np.float32))
    return out


def kernel(**inputs):
    import concourse.bacc as bacc
    from concourse.bass_utils import run_bass_kernel_spmd

    arrays = {name: np.ascontiguousarray(a) for name, a in inputs.items()}
    x = arrays.pop("L0_attn_x")
    B = x.shape[0]
    arrays["x_tiles"] = x.reshape(B * TC, P, D)
    arrays.update({name: np.ascontiguousarray(a) for name, a in shape_constants().items()})
    nc = bacc.Bacc("TRN2", target_bir_lowering=False, num_devices=1)
    aps = {name: nc.dram_tensor(name, a.shape, mybir.dt.from_np(a.dtype), kind="ExternalInput").ap() for name, a in arrays.items()}
    aps["out_tiles"] = nc.dram_tensor("out_tiles", [B * TC, P, D], F32, kind="ExternalOutput").ap()
    adaln_two_layers(nc, aps, B)
    r = run_bass_kernel_spmd(nc, [arrays], core_ids=[0])
    return np.asarray(r.results[0]["out_tiles"]).reshape(x.shape)
```

```python
import numpy as np

import concourse.bass as bass
from concourse import mybir
from contextlib import ExitStack

P = 128
F32 = mybir.dt.float32
BF16 = mybir.dt.bfloat16
U32 = mybir.dt.uint32
I32 = mybir.dt.int32
ALU = mybir.AluOpType
ACT = mybir.ActivationFunctionType
AX = mybir.AxisListType
ds = bass.ds

T, D = 256, 128
TC = T // P
SHIFT_A, SCALE_A, GATE_A, SHIFT_B, SCALE_B, GATE_B = range(6)
LN_EPS = 1e-5


def at(eng, sem, count):
    if isinstance(count, int) and count <= 0:
        return
    eng.wait_ge(sem, count)


def at_alone(eng, sem, count, passed):
    at(eng, sem, count)
    if not isinstance(count, int):
        eng.sem_inc(passed, 1)


class Core:

    def __init__(self, nc, aps, B):
        self.nc, self.aps, self.B = nc, aps, B
        self.NT = B * TC
        self.stack = ExitStack()
        self.sems = []
        self.X = self.sbuf("resid_x", [P, max(self.NT * D, 8192)])
        self.mod = self.sbuf("mod_cols", [P, 2 * 6 * B])
        self.ident = self.sbuf("identity", [P, P])
        self.rstd = self.sbuf("rstd", [P, self.NT])
        self.nmr = self.sbuf("neg_mean_rstd", [P, self.NT])
        self.st = self.sbuf("bn_stats", [P, self.NT, 6])
        self.ln_tmp = [self.sbuf(f"ln_{n}", [P, self.NT]) for n in ("mean", "dmean", "var", "std")]
        self.modrow = nc.dram_tensor("mod_rows", [10, B, D], F32, kind="Internal").ap()

    def sbuf(self, name, shape, dt=F32, on=None):
        return (on or self.stack).enter_context(self.nc.sbuf_tensor(name, shape, dt))

    def psum(self, name, shape, dt=F32, on=None):
        return (on or self.stack).enter_context(self.nc.psum_tensor(name, shape, dt))

    def sem(self, name):
        self.sems.append(self.nc.alloc_semaphore(name=name))
        return self.sems[-1]

    def next_stage(self):
        self.nc.all_engine_barrier()
        self.nc.clear_and_free_semaphores(self.sems)
        self.nc.all_engine_barrier()
        self.sems = []

    def modcol(self, layer, kind, b):
        o = (layer * 6 + kind) * self.B
        return self.mod[:, ds(b + o, 1)]


class Chain:

    def __init__(self, core, eng, name, base=0):
        self.eng, self.sem, self.n = eng, core.sem(name), 0

    def step(self, ins):
        ins.then_inc(self.sem, 1)
        self.n += 1
        self.eng.wait_ge(self.sem, self.n)


def load_and_modulate(core):
    nc, B, aps = core.nc, core.B, core.aps
    on = ExitStack()
    with on:
        c = core.sbuf("c_rows", [2 * B, D], on=on)
        cs = core.sbuf("c_silu", [2 * B, D], on=on)
        cT = core.sbuf("c_silu_T", [P, 2 * B], on=on)
        w = core.sbuf("wmod", [P, 2, 6 * D], on=on)
        rows = core.sbuf("mod_rows_sb", [B, 10, D], on=on)
        sgn = core.sbuf("gate_sign", [P, 4 * D], on=on)
        psT = core.psum("m_psT", [P, 512], on=on)
        psC = core.psum("m_psC", [P, 512], on=on)
        psR = core.psum("m_psR", [P, 3, 512], on=on)
        s_x, s_in, s_silu = core.sem("x_loaded"), core.sem("mod_in_loaded"), core.sem("c_silu_ready")
        s_T, s_cT, s_mm, s_rows, s_out = core.sem("cT_ps"), core.sem("cT_ready"), core.sem("mod_ps"), core.sem("modrows_ready"), core.sem("modrows_stored")
        with nc.Block() as block:
            @block.sync
            def _(sp):
                for l, (cn, wn) in enumerate((("L0_c", "L0_wmod"), ("L1_c", "L1_wmod"))):
                    sp.dma_start(c[l * B:(l + 1) * B, :], aps[cn][0:B]).then_inc(s_in, 16)
                    sp.dma_start(w[:, l, :], aps[wn]).then_inc(s_in, 16)
                sp.dma_start(core.ident[:], aps["ident"]).then_inc(s_in, 16)
                half = core.NT // 2
                for k in range(2):
                    sp.dma_start(core.X[:, k * half * D:(k + 1) * half * D].rearrange("p (n d) -> p n d", d=D),
                                 aps["x_tiles"][k * half:(k + 1) * half].rearrange("n p d -> p n d")).then_inc(s_x, 16)
                sp.wait_ge(s_rows, 1)
                sp.dma_start(core.modrow.rearrange("k b d -> b k d"), rows[:]).then_inc(s_out, 16)
                sp.wait_ge(s_out, 16)
                sp.wait_ge(s_x, 32)

            @block.scalar
            def _(act):
                act.wait_ge(s_in, 80)
                nc.scalar.activation(cs[:], c[:], ACT.Silu).then_inc(s_silu, 1)

            @block.tensor
            def _(pe):
                pe.wait_ge(s_silu, 1)
                nc.tensor.transpose(psT[:, 0:2 * B], cs[:], core.ident[0:2 * B, 0:2 * B]).then_inc(s_T, 1)
                pe.wait_ge(s_cT, 1)
                for l in range(2):
                    for k in range(6):
                        o = (l * 6 + k) * B
                        nc.tensor.matmul(psC[:, o:o + B], w[:, l, k * D:(k + 1) * D], cT[:, l * B:(l + 1) * B],
                                         start=True, stop=True)
                for n, (l, k) in enumerate(((0, GATE_A), (0, GATE_B), (1, GATE_A), (1, GATE_B), (0, SHIFT_B), (0, SCALE_B), (1, SHIFT_B), (1, SCALE_B),
                                             (1, SHIFT_A), (1, SCALE_A))):
                    last = nc.tensor.matmul(psR[0:B, n // 4, (n % 4) * D:(n % 4 + 1) * D], cT[:, l * B:(l + 1) * B],
                                            w[:, l, k * D:(k + 1) * D], start=True, stop=True)
                last.then_inc(s_mm, 1)

            @block.vector
            def _(dve):
                chain = Chain(core, dve, "mod_dve_chain")
                dve.wait_ge(s_T, 1)
                nc.vector.tensor_copy(cT[:], psT[:, 0:2 * B]).then_inc(s_cT, 1)
                dve.wait_ge(s_mm, 1)
                chain.step(nc.vector.tensor_copy(core.mod[:], psC[:, 0:12 * B]))
                for l in range(2):
                    for k in (SCALE_A, SCALE_B):
                        o = (l * 6 + k) * B
                        nc.vector.tensor_scalar(core.mod[:, o:o + B], core.mod[:, o:o + B], 1.0, None, ALU.add)
                chain.step(nc.vector.tensor_scalar(sgn[0:B, :], psR[0:B, 0, :], 0.0, None, ALU.is_ge))
                chain.step(nc.vector.tensor_scalar(sgn[0:B, :], sgn[0:B, :], 2.0, -1.0, ALU.mult, ALU.add))
                for k in range(3):
                    pair = psR[0:B, 1 + k // 2, (k % 2) * 2 * D:(k % 2 + 1) * 2 * D]
                    nc.vector.tensor_copy(rows[:, 4 + 2 * k, :], pair[:, 0:D])
                    nc.vector.tensor_scalar(rows[:, 5 + 2 * k, :], pair[:, D:2 * D], 1.0, None, ALU.add)
                gates = rows[:, 0:4, :].rearrange("b k d -> b (k d)")
                chain.step(nc.vector.tensor_copy(gates, psR[0:B, 0, :]))
                chain.step(nc.vector.scalar_tensor_tensor(out=gates, in0=gates, scalar=-1.0, in1=gates,
                                                          op0=ALU.mult, op1=ALU.max))
                chain.step(nc.vector.tensor_scalar(gates, gates, 0.25, None, ALU.max))
                nc.vector.tensor_tensor(gates, gates, sgn[0:B, :], ALU.mult).then_inc(s_rows, 1)


def ln_finish(core, tag, st, eps, block):
    nc, NT = core.nc, core.NT
    on = core.stack
    m, dm, v, sd = core.ln_tmp
    s_v, s_sd = core.sem(f"{tag}_var_ready"), core.sem(f"{tag}_std_ready")

    @block.vector
    def _(dve):
        chain = Chain(core, dve, f"{tag}_dve_chain")
        chain.step(nc.vector.tensor_tensor(m[:], st[:, :, 1], st[:, :, 4], ALU.add))
        nc.vector.tensor_tensor(dm[:], st[:, :, 1], st[:, :, 4], ALU.subtract)
        chain.step(nc.vector.tensor_tensor(v[:], st[:, :, 2], st[:, :, 5], ALU.add))
        chain.step(nc.vector.tensor_tensor(dm[:], dm[:], dm[:], ALU.mult))
        chain.step(nc.vector.tensor_scalar(dm[:], dm[:], 0.25, eps, ALU.mult, ALU.add))
        nc.vector.scalar_tensor_tensor(out=v[:], in0=v[:], scalar=1.0 / D, in1=dm[:],
                                       op0=ALU.mult, op1=ALU.add).then_inc(s_v, 1)
        dve.wait_ge(s_sd, 1)
        chain.step(nc.vector.reciprocal(core.rstd[:], sd[:]))
        chain.step(nc.vector.scalar_tensor_tensor(out=core.nmr[:], in0=m[:], scalar=-0.5, in1=core.rstd[:],
                                                  op0=ALU.mult, op1=ALU.mult))

    @block.scalar
    def _(act):
        act.wait_ge(s_v, 1)
        nc.scalar.activation(sd[:], v[:], ACT.Sqrt).then_inc(s_sd, 1)


def ln_stats(core, tag, src=None, eps=LN_EPS):
    nc, NT = core.nc, core.NT
    src = core.X if src is None else src
    s_st = core.sem(f"{tag}_bn_ready")
    with nc.Block() as block:
        @block.vector
        def _(dve):
            for t in range(NT):
                last = nc.vector.bn_stats(core.st[:, t, :], src[:, t * D:(t + 1) * D])
            last.then_inc(s_st, 1)
            dve.wait_ge(s_st, 1)
    with nc.Block() as block:
        ln_finish(core, tag, core.st, eps, block)
H, DH = 16, 8
HQ = 4
PARTS = 3
KROWS = PARTS * PARTS * DH
RING = 4
PAIRS = H // 2
MAXHEADS = (3, 3, 3, 3, 3, 1, 0, 0)
MAXFROM = [sum(MAXHEADS[:p]) for p in range(PAIRS)]


def pair_heads(p):
    r, q = p // 2, 2 * (p % 2)
    return [HQ * q + r, HQ * (q + 1) + r]


def rolled(eng, n, lag, first, emit, ring=RING):
    turns = max(0, (n - first) // ring)
    for i in range(first):
        emit(i, i % ring)
    if turns:
        with eng.Fori(0, turns) as turn:
            for u in range(ring):
                emit(turn * ring + (first + u), (first + u) % ring)
    for i in range(first + turns * ring, n + lag):
        emit(i, i % ring)


def attention(core):
    nc, B, X, aps = core.nc, core.B, core.X, core.aps
    SCALE = float(DH) ** -0.5
    live = lambda i, lag: not isinstance(i, int) or 0 <= i - lag < B
    MAX, SCORES, LAG = 2, 3, 4
    on = ExitStack()
    with on:
        sb = lambda name, shape, dt=F32: core.sbuf("a_" + name, shape, dt, on=on)
        w_dk, w_dv, w_uk, w_uv, w_o, rot = (sb(n, [P, D]) for n in ("w_dk", "w_dv", "w_uk", "w_uv", "w_o", "rot"))
        bias = sb("bias_cols", [P, 4])
        bo = sb("bias_out", [P, TC * D])
        bo_row = sb("bias_out_row", [1, D])
        bo_in = sb("b_o_row", [1, D])
        ones1 = sb("ones_row", [1, P])
        cos, sin = sb("cos", [P, 2 * T]), sb("sin", [P, 2 * T])
        xn = sb("xn", [P, TC, D])
        qk = sb("qk", [P, 2, T])
        ckv = sb("ckv", [P, 2, T])
        qcos, qsin = sb("qk_cos", [P, 2 * T]), sb("qk_sin", [P, 2 * T])
        roped, left = sb("roped", [P, 2 * T]), sb("left", [P, 2 * T])
        parts = sb("parts", [P, PARTS, 2, T], BF16)
        Q9 = [sb(f"Q9_{n}", [KROWS + 2, H, T], BF16) for n in range(RING)]
        K9 = [sb(f"K9_{n}", [KROWS + 2, H, T], BF16) for n in range(RING)]
        V = [sb(f"V_{n}", [P, TC, HQ, HQ, 32]) for n in range(RING)]
        ones = sb("ones_pad", [P, HQ, 32])
        mx = sb("row_max", [P, H, TC])
        mhi, mlo = sb("max_hi", [2 * H, P], BF16), sb("max_lo", [2 * H, P], BF16)
        PT = sb("probs", [P, 4, 2, TC, T])
        rden, oT = sb("rden", [P, T]), sb("oT", [P, T])
        ga = sb("gate_rows", [P, D])
        minus = sb("minus_one", [2, H * T], BF16)
        y1, y2 = sb("y1", [P, TC * D]), sb("y2", [P, TC * D])
        ST = core.psum("a_scores", [P, 2, 2, TC, T], on=on)
        MX = core.psum("a_maxscores", [P, 2, TC, T], on=on)
        O = core.psum("a_out", [P, 2, T], on=on)
        PP = core.psum("a_proj", [P, 512], on=on)
        split = [nc.dram_tensor(f"split_qk_{n}", [P, PARTS, 2, T], BF16, kind="Internal").ap() for n in range(RING)]

        S = {n: core.sem("a_" + n) for n in (
            "w_loaded", "const_ready", "mrow_const", "bo_ps", "bo_row", "bo_ready", "gate_loaded", "xn_ready", "hT_ps", "hT_ready", "ckv_ps",
            "ckv_ready", "kv_ps", "k_ready", "v_ready", "rot_ps", "cos_done", "sin_done", "roped_ready", "part0",
            "left1", "part1", "part2", "stored", "loaded", "batch_loaded", "max_ps", "max_done", "maxT_ps", "max_hi", "max_lo",
            "max_rows", "scores_ps", "exp_done", "av_done", "rden_ready", "oT_ready", "y_ps", "y_biased",
            "y_gated", "x_updated", "passed")}

        with nc.Block() as block:
            @block.sync
            def _(sp):
                for t, n in ((w_dk, "L0_attn_w_dk"), (w_dv, "L0_attn_w_dv"), (w_uk, "L0_attn_w_uk"), (w_uv, "L0_attn_w_uv"),
                             (w_o, "L0_attn_w_o"), (rot, "rope_rot")):
                    sp.dma_start(t[:], aps[n]).then_inc(S["w_loaded"], 16)
                for k, n in enumerate(("L0_attn_b_dk", "L0_attn_b_dv", "L0_attn_b_uk", "L0_attn_b_uv")):
                    sp.dma_start(bias[:, k:k + 1], aps[n].rearrange("(p n) -> p n", n=1)).then_inc(S["w_loaded"], 16)
                sp.dma_start(bo_in[:], aps["L0_attn_b_o"].rearrange("(n d) -> n d", n=1)).then_inc(S["w_loaded"], 16)
                for t, n in ((cos, "rope_cos"), (sin, "rope_sin")):
                    for k in range(2):
                        sp.dma_start(t[:, k * T:(k + 1) * T], aps[n]).then_inc(S["w_loaded"], 16)
                sp.wait_ge(S["const_ready"], 1)
                for n in range(RING):
                    sp.dma_start(K9[n][KROWS:KROWS + 2, :, :], minus[:].rearrange("p (h t) -> p h t", t=T)).then_inc(S["mrow_const"], 16)

                def emit(i, u):
                    if live(i, 1):
                        sp.wait_ge(S["loaded"], 16 * 2 * PARTS * PARTS * i)
                        sp.sem_inc(S["batch_loaded"], 1)
                    if live(i, LAG):
                        at(sp, S["y_gated"], i - LAG)
                        sp.dma_start(ga[:], core.modrow[0, ds(i - LAG, 1), :].rearrange("n d -> (n d)").partition_broadcast(P)).then_inc(S["gate_loaded"], 16)
                    if live(i, MAX):
                        n = (u - MAX) % RING
                        at_alone(sp, S["max_lo"], i - MAX + 1, S["passed"])
                        at(sp, S["scores_ps"], PAIRS * (i - MAX - RING + 1))
                        for k, m in enumerate((mhi, mlo)):
                            sp.dma_start(Q9[n][KROWS + k:KROWS + k + 1, :, :], m[:]).then_inc(S["max_rows"], 16)
                    if live(i, 0):
                        sp.wait_ge(S["part2"], i + 1)
                        sp.dma_start(split[u], parts[:]).then_inc(S["stored"], 16)
                        at_alone(sp, S["stored"], 16 * (i + 1), S["passed"])
                        at(sp, S["scores_ps"], PAIRS * (i - RING + 1))
                        view = split[u].rearrange("(h e) a w t -> a w e h t", e=DH)
                        for a in range(PARTS):
                            for b in range(PARTS):
                                row = (a * PARTS + b) * DH
                                sp.dma_start(Q9[u][row:row + DH, :, :], view[a, 0]).then_inc(S["loaded"], 16)
                                sp.dma_start(K9[u][row:row + DH, :, :], view[b, 1]).then_inc(S["loaded"], 16)
                rolled(sp, B, LAG, 6, emit)

            @block.gpsimd
            def _(pool):
                nc.gpsimd.memset(ones[:], 0.0)
                for n in range(RING):
                    last = nc.gpsimd.memset(V[n][:], 0.0)
                last.then_inc(S["bo_row"], 1)
                pool.wait_ge(S["bo_row"], 1)
                for r in range(HQ):
                    nc.gpsimd.memset(ones[:, r, r * DH:(r + 1) * DH], 1.0)
                nc.gpsimd.memset(minus[:], -1.0)
                nc.gpsimd.memset(ones1[:], 1.0).then_inc(S["const_ready"], 1)
                pool.wait_ge(S["w_loaded"], 15 * 16)
                pool.wait_ge(S["bo_ready"], 1)

                def emit(i, u):
                    if live(i, 0):
                        pool.wait_ge(S["k_ready"], i + 1)
                        at(pool, S["roped_ready"], i)
                        nc.gpsimd.tensor_tensor(qcos[:], qk[:].rearrange("p a t -> p (a t)"), cos[:], ALU.mult).then_inc(S["cos_done"], 1)
                    if live(i, LAG):
                        b = i - LAG
                        pool.wait_ge(S["y_biased"], b + 1)
                        pool.wait_ge(S["gate_loaded"], 16 * (b + 1))
                        at(pool, S["x_updated"], b)
                        g = ga[:].unsqueeze(1).broadcast_to([P, TC, D])
                        nc.gpsimd.tensor_tensor(y2[:].rearrange("p (n d) -> p n d", d=D), y1[:].rearrange("p (n d) -> p n d", d=D), g,
                                                ALU.mult).then_inc(S["y_gated"], 1)
                        pool.wait_ge(S["y_gated"], b + 1)
                        x = X[:, ds(b * (TC * D), TC * D)]
                        nc.gpsimd.tensor_tensor(x, x, y2[:], ALU.add).then_inc(S["x_updated"], 1)
                rolled(pool, B, LAG, 6, emit)

            @block.scalar
            def _(act):
                act.wait_ge(S["w_loaded"], 15 * 16)

                def emit(i, u):
                    for p in range(PAIRS):
                        if live(i, SCORES):
                            act.wait_ge(S["scores_ps"], PAIRS * (i - SCORES) + p + 1)
                            at(act, S["av_done"], 4 * (i - SCORES) + p // 2 - 1)
                            nc.scalar.activation(PT[:, p % 4].rearrange("p a b t -> p (a b t)"), ST[:, p % 2].rearrange("p a b t -> p (a b t)"),
                                                 ACT.Exp, scale=SCALE).then_inc(S["exp_done"], 1)
                        if p == 1 and live(i, 0):
                            act.wait_ge(S["hT_ps"], i + 1)
                            at(act, S["rot_ps"], i)
                            at(act, S["cos_done"], i)
                            nc.scalar.activation(qk[:, 0, :], PP[:, 0:T], ACT.Identity, scale=core.modcol(0, SCALE_A, i),
                                                 bias=core.modcol(0, SHIFT_A, i)).then_inc(S["hT_ready"], 1)
                        if p == 2 and live(i, 0):
                            act.wait_ge(S["ckv_ps"], i + 1)
                            at(act, S["kv_ps"], i)
                            for k in range(2):
                                last = nc.scalar.activation(ckv[:, k, :], PP[:, k * T:(k + 1) * T], ACT.Identity, bias=bias[:, k:k + 1])
                            last.then_inc(S["ckv_ready"], 1)
                        if p == 3 and live(i, 0):
                            act.wait_ge(S["v_ready"], i + 1)
                            nc.scalar.activation(qk[:, 1, :], PP[:, 0:T], ACT.Identity, bias=bias[:, 2:3]).then_inc(S["k_ready"], 1)
                        if p == 6 and live(i, 0):
                            act.wait_ge(S["roped_ready"], i + 1)
                            at(act, S["stored"], 16 * i)
                            nc.scalar.activation(parts[:, 0].rearrange("p a t -> p (a t)"), roped[:], ACT.Copy).then_inc(S["part0"], 1)
                            act.wait_ge(S["left1"], i + 1)
                            nc.scalar.activation(parts[:, 1].rearrange("p a t -> p (a t)"), left[:], ACT.Copy).then_inc(S["part1"], 1)
                rolled(act, B, LAG, 6, emit)

            @block.vector
            def _(dve):
                dve.wait_ge(S["bo_ps"], 1)
                nc.vector.tensor_tensor(bo_row[:], PP[0:1, 0:D], bo_in[:], ALU.add).then_inc(S["bo_ready"], 1)
                dve.wait_ge(S["bo_ps"], 2)
                for k in range(TC):
                    last = nc.vector.tensor_copy(bo[:, k * D:(k + 1) * D], PP[:, D:2 * D])
                last.then_inc(S["bo_ready"], 1)
                dve.wait_ge(S["bo_ready"], 2)

                def emit(i, u):
                    for p in range(PAIRS):
                        if p == 0 and live(i, 0):
                            at(dve, S["hT_ps"], i)
                            for k in range(TC):
                                c = 2 * i + k
                                last = nc.vector.tensor_scalar(xn[:, k, :], X[:, ds(i * (TC * D) + k * D, D)], core.rstd[:, ds(c, 1)],
                                                               core.nmr[:, ds(c, 1)], ALU.mult, ALU.add)
                            last.then_inc(S["xn_ready"], 1)
                        if p == 2 and live(i, LAG):
                            b = i - LAG
                            dve.wait_ge(S["av_done"], 4 * (b + 1))
                            nc.vector.reciprocal(rden[:], O[:, 1, :]).then_inc(S["rden_ready"], 1)
                            dve.wait_ge(S["rden_ready"], b + 1)
                            at(dve, S["y_ps"], b)
                            nc.vector.tensor_tensor(oT[:], O[:, 0, :], rden[:], ALU.mult).then_inc(S["oT_ready"], 1)
                        if live(i, MAX):
                            b = i - MAX
                            for h in range(MAXFROM[p], MAXFROM[p] + MAXHEADS[p]):
                                dve.wait_ge(S["max_ps"], H * b + h + 1)
                                if h == 0:
                                    at(dve, S["maxT_ps"], b)
                                nc.vector.tensor_reduce(mx[:, h, :], MX[:, h % 2], AX.X, ALU.max).then_inc(S["max_done"], 1)
                        if p == 3 and live(i, 0):
                            dve.wait_ge(S["kv_ps"], i + 1)
                            at(dve, S["av_done"], 4 * (i - RING + 1))
                            for k in range(TC):
                                v = V[u][:, k]
                                heads = bass.AP(tensor=v.tensor, offset=v.offset, ap=[list(v.ap[0]), [HQ * 32, HQ], [32 + DH, HQ], [1, DH]])
                                last = nc.vector.tensor_copy(heads, PP[:, T + k * D:T + (k + 1) * D].rearrange("p (q r e) -> p q r e", q=HQ, r=HQ))
                            last.then_inc(S["v_ready"], 1)
                        if p == 5 and live(i, 0):
                            dve.wait_ge(S["rot_ps"], i + 1)
                            nc.vector.tensor_tensor(qsin[:], PP[:], sin[:], ALU.mult).then_inc(S["sin_done"], 1)
                            dve.wait_ge(S["sin_done"], i + 1)
                            dve.wait_ge(S["cos_done"], i + 1)
                            nc.vector.tensor_tensor(roped[:], qcos[:], qsin[:], ALU.add).then_inc(S["roped_ready"], 1)
                        if p == 7 and live(i, LAG):
                            b = i - LAG
                            dve.wait_ge(S["y_ps"], b + 1)
                            at(dve, S["y_gated"], b)
                            nc.vector.tensor_tensor(y1[:], PP[:, 0:TC * D], bo[:], ALU.add).then_inc(S["y_biased"], 1)
                        if p == 6 and live(i, 0):
                            dve.wait_ge(S["part0"], i + 1)
                            nc.vector.tensor_tensor(left[:], roped[:], parts[:, 0].rearrange("p a t -> p (a t)"), ALU.subtract).then_inc(S["left1"], 1)
                        if p == 6 and live(i, MAX):
                            b = i - MAX
                            dve.wait_ge(S["maxT_ps"], b + 1)
                            at(dve, S["max_rows"], 32 * b)
                            nc.vector.tensor_copy(mhi[:], PP[0:2 * H, 0:P]).then_inc(S["max_hi"], 1)
                            dve.wait_ge(S["max_hi"], b + 1)
                            nc.vector.tensor_tensor(mlo[:], PP[0:2 * H, 0:P], mhi[:], ALU.subtract).then_inc(S["max_lo"], 1)
                        if p == 7 and live(i, 0):
                            dve.wait_ge(S["part1"], i + 1)
                            nc.vector.tensor_tensor(parts[:, 2].rearrange("p a t -> p (a t)"), left[:], parts[:, 1].rearrange("p a t -> p (a t)"),
                                                    ALU.subtract).then_inc(S["part2"], 1)
                rolled(dve, B, LAG, 6, emit)

            @block.tensor
            def _(pe):
                mm = nc.tensor.matmul
                pe.wait_ge(S["w_loaded"], 15 * 16)
                pe.wait_ge(S["const_ready"], 1)
                pe.wait_ge(S["mrow_const"], 16 * RING)
                mm(PP[0:1, 0:D], bias[:, 3:4], w_o[:], start=True, stop=True).then_inc(S["bo_ps"], 1)
                pe.wait_ge(S["bo_ready"], 1)
                mm(PP[:, D:2 * D], ones1[:], bo_row[:], start=True, stop=True).then_inc(S["bo_ps"], 1)
                pe.wait_ge(S["bo_ready"], 2)

                def values(b, u, g):
                    pe.wait_ge(S["exp_done"], PAIRS * b + 2 * g + 2)
                    if g == 0:
                        at(pe, S["oT_ready"], b)
                    for k in range(TC):
                        for kind in range(2):
                            for q in range(HQ):
                                w = V[u][:, k, q, g, :] if kind == 0 else ones[:, g, :]
                                pr = PT[:, (2 * g + q // 2) % 4, q % 2, k, :]
                                last = mm(O[32 * q:32 * q + 32, kind, :], w, pr, start=(g == 0 and k == 0 and kind == 0),
                                          stop=(g == 3 and k == TC - 1 and kind == 1), skip_group_check=True)
                    last.then_inc(S["av_done"], 1)

                def emit(i, u):
                    for p in range(PAIRS):
                        if live(i, SCORES):
                            b, n = i - SCORES, (u - SCORES) % RING
                            if p == 0:
                                pe.wait_ge(S["max_rows"], 32 * (b + 1))
                            at(pe, S["exp_done"], PAIRS * b + p - 1)
                            for j, h in enumerate(pair_heads(p)):
                                for k in range(TC):
                                    last = mm(ST[:, p % 2, j, k, :], K9[n][:, h, k * P:(k + 1) * P], Q9[n][:, h, :], start=True, stop=True)
                            last.then_inc(S["scores_ps"], 1)
                        if p == 1 and live(i, LAG):
                            values(i - LAG, u, 3)
                        if p % 2 == 1 and p >= 3 and live(i, SCORES):
                            if p == 3:
                                pe.wait_ge(S["v_ready"], i - SCORES + 1)
                            values(i - SCORES, (u - SCORES) % RING, p // 2 - 1)
                        if p == 1 and live(i, 0):
                            pe.wait_ge(S["xn_ready"], i + 1)
                            at(pe, S["max_lo"], i - MAX)
                            at(pe, S["y_biased"], i - LAG)
                            for k in range(TC):
                                last = nc.tensor.transpose(PP[:, k * P:(k + 1) * P], xn[:, k, :], core.ident[:])
                            last.then_inc(S["hT_ps"], 1)
                        if p == 2 and live(i, 0):
                            pe.wait_ge(S["hT_ready"], i + 1)
                            mm(PP[:, 0:T], w_dk[:], qk[:, 0, :], start=True, stop=True)
                            mm(PP[:, T:2 * T], w_dv[:], qk[:, 0, :], start=True, stop=True).then_inc(S["ckv_ps"], 1)
                        if live(i, MAX):
                            b, n = i - MAX, (u - MAX) % RING
                            for h in range(MAXFROM[p], MAXFROM[p] + MAXHEADS[p]):
                                if h == 0:
                                    pe.wait_ge(S["batch_loaded"], b + 1)
                                at(pe, S["max_done"], H * b + h - 1)
                                for k in range(TC):
                                    last = mm(MX[:, h % 2, k, :], Q9[n][0:KROWS, h, k * P:(k + 1) * P], K9[n][0:KROWS, h, :], start=True, stop=True)
                                last.then_inc(S["max_ps"], 1)
                        if p == 3 and live(i, 0):
                            pe.wait_ge(S["ckv_ready"], i + 1)
                            mm(PP[:, 0:T], w_uk[:], ckv[:, 0, :], start=True, stop=True)
                            for k in range(TC):
                                last = mm(PP[:, T + k * D:T + (k + 1) * D], ckv[:, 1, k * P:(k + 1) * P], w_uv[:], start=True, stop=True)
                            last.then_inc(S["kv_ps"], 1)
                        if p == 4 and live(i, 0):
                            pe.wait_ge(S["k_ready"], i + 1)
                            pe.wait_ge(S["v_ready"], i + 1)
                            mm(PP[:], rot[:], qk[:].rearrange("p a t -> p (a t)"), start=True, stop=True).then_inc(S["rot_ps"], 1)
                        if p == 6 and live(i, MAX):
                            b = i - MAX
                            pe.wait_ge(S["max_done"], H * (b + 1))
                            if live(i, 0):
                                pe.wait_ge(S["sin_done"], i + 1)
                            else:
                                at(pe, S["y_biased"], i - LAG)
                            nc.tensor.transpose(PP[0:2 * H, 0:P], mx[:].rearrange("p h k -> p (h k)"), core.ident[:]).then_inc(S["maxT_ps"], 1)
                        if p == 7 and live(i, LAG):
                            b = i - LAG
                            if live(i, MAX):
                                pe.wait_ge(S["max_lo"], i - MAX + 1)
                            else:
                                pe.wait_ge(S["y_biased"], b)
                            pe.wait_ge(S["oT_ready"], b + 1)
                            for k in range(TC):
                                last = mm(PP[:, k * D:(k + 1) * D], oT[:, k * P:(k + 1) * P], w_o[:], start=True, stop=True)
                            last.then_inc(S["y_ps"], 1)
                rolled(pe, B, LAG, 6, emit)
E, F = 8, 512
FC = F // P
STAGES = 4
CAP = 80


def start_counts(core, tag, names):
    S = {n: core.sem(f"{tag}_{n}") for n in names}
    with core.nc.Block() as block:
        @block.sync
        def _(sp):
            for n in names:
                sp.sem_inc(S[n], 1)
    return S


def upto(eng, sem, count):
    if isinstance(count, int) and count < 0:
        return
    eng.wait_ge(sem, count + 1)


def fill_zero(core, tag, table, tiles):
    nc = core.nc
    on = ExitStack()
    with on:
        zero = core.sbuf(f"{tag}_zero", [P, tiles, D // 8], on=on)
        s_zero, s_out = core.sem(f"{tag}_zero_ready"), core.sem(f"{tag}_zeroed")
        with nc.Block() as block:
            @block.vector
            def _(dve):
                nc.vector.memset(zero[:], 0.0).then_inc(s_zero, 1)

            @block.sync
            def _(sp):
                sp.wait_ge(s_zero, 1)
                w = tiles * D // 8
                flat = table.rearrange("r d -> (r d)").rearrange("(k p w) -> k p w", k=8, p=P)
                for k in range(8):
                    sp.dma_start(flat[k], zero[:].rearrange("p n d -> p (n d)")).then_inc(s_out, 16)
                sp.wait_ge(s_out, 128)


def modulated(core, layer, Hr, L, row):
    nc, B, X, aps, tag = core.nc, core.B, core.X, core.aps, f"r{row}"
    on = ExitStack()
    with on:
        sb = lambda name, shape, dt=F32: core.sbuf(f"{tag}_{name}", shape, dt, on=on)
        gw = sb("gate_w", [P, E])
        mod = [sb(f"mod_rows{n}", [P, 2, D]) for n in range(2)]
        xn = [sb(f"xn{n}", [P, TC, D]) for n in range(2)]
        scaled = [sb(f"scaled{n}", [P, TC, D]) for n in range(2)]
        if L is not None:
            h = [sb(f"h{n}", [P, TC, D]) for n in range(2)]
            hT = [sb(f"hT{n}", [P, TC, P]) for n in range(2)]
            psT = core.psum(f"{tag}_psT", [P, 2, 512], on=on)
            psL = core.psum(f"{tag}_psL", [P, 2, 512], on=on)
        S = start_counts(core, tag, ("w_loaded", "mod_loaded0", "mod_loaded1", "xn_ready", "scaled", "h_ready", "h_kept", "hT_ps", "hT_ready",
                                     "logits_ps", "logits_kept"))

        def loop(eng, emit):
            for u in range(2):
                emit(u, u, 0)
            with eng.Fori(0, B // 2 - 1) as t:
                for u in range(2):
                    emit(t * 2 + (2 + u), u, t + 1)

        with nc.Block() as block:
            @block.sync
            def _(sp):
                if L is not None:
                    sp.dma_start(gw[:], aps[f"L{layer}_ffn_gate_w"]).then_inc(S["w_loaded"], 16)

                def emit(b, u, turn):
                    upto(sp, S["h_ready"], b - 1)
                    sp.dma_start(mod[u][:], core.modrow[row:row + 2, ds(b, 1), :].rearrange("k n d -> (k n) d").partition_broadcast(P))\
                        .then_inc(S[f"mod_loaded{u}"], 16)
                loop(sp, emit)

            @block.vector
            def _(dve):
                def keep_logits(b, u):
                    upto(dve, S["logits_ps"], b + 1)
                    nc.vector.tensor_copy(L[:, ds(b * (TC * E), TC * E)], psL[:, u, 0:TC * E]).then_inc(S["logits_kept"], 1)

                def emit(b, u, turn):
                    for k in range(TC):
                        c = b * TC + k
                        last = nc.vector.tensor_scalar(xn[u][:, k, :], X[:, ds(b * (TC * D) + k * D, D)], core.rstd[:, ds(c, 1)],
                                                       core.nmr[:, ds(c, 1)], ALU.mult, ALU.add)
                    last.then_inc(S["xn_ready"], 1)
                    upto(dve, S[f"mod_loaded{u}"], 16 * (turn + 1))
                    upto(dve, S["h_ready"], b - 1)
                    upto(dve, S["xn_ready"], b + 1)
                    nc.vector.tensor_tensor(scaled[u][:], xn[u][:], mod[u][:, 1, :].unsqueeze(1).broadcast_to([P, TC, D]), ALU.mult).then_inc(S["scaled"], 1)
                    if L is not None and not (isinstance(b, int) and b == 0):
                        keep_logits(b - 1, 1 - u)
                loop(dve, emit)
                if L is not None:
                    keep_logits(B - 1, 1)

            @block.gpsimd
            def _(pool):
                def emit(b, u, turn):
                    if L is None:
                        out = Hr[:, ds(b * (TC * D), TC * D)].rearrange("p (k d) -> p k d", d=D)
                    else:
                        out = h[u][:]
                        upto(pool, S["h_kept"], b - 1)
                        upto(pool, S["hT_ps"], b - 1)
                    upto(pool, S["scaled"], b + 1)
                    nc.gpsimd.tensor_tensor(out, scaled[u][:], mod[u][:, 0, :].unsqueeze(1).broadcast_to([P, TC, D]), ALU.add).then_inc(S["h_ready"], 1)
                loop(pool, emit)

            if L is not None:
                @block.tensor
                def _(pe):
                    upto(pe, S["w_loaded"], 16)

                    def logits(b, u):
                        upto(pe, S["hT_ready"], b + 1)
                        upto(pe, S["logits_kept"], b - 1)
                        for k in range(TC):
                            last = nc.tensor.matmul(psL[:, u, k * E:(k + 1) * E], hT[u][:, k, :], gw[:], start=True, stop=True)
                        last.then_inc(S["logits_ps"], 1)

                    def emit(b, u, turn):
                        upto(pe, S["h_ready"], b + 1)
                        upto(pe, S["hT_ready"], b - 1)
                        for k in range(TC):
                            last = nc.tensor.transpose(psT[:, u, k * P:(k + 1) * P], h[u][:, k, :], core.ident[:])
                        last.then_inc(S["hT_ps"], 1)
                        if not (isinstance(b, int) and b == 0):
                            logits(b - 1, 1 - u)
                    loop(pe, emit)
                    logits(B - 1, 1)

                @block.scalar
                def _(act):
                    def emit(b, u, turn):
                        upto(act, S["h_ready"], b + 1)
                        nc.scalar.activation(Hr[:, ds(b * (TC * D), TC * D)], h[u][:].rearrange("p k d -> p (k d)"), ACT.Copy).then_inc(S["h_kept"], 1)
                        upto(act, S["hT_ps"], b + 1)
                        upto(act, S["logits_ps"], b - 1)
                        nc.scalar.activation(hT[u][:].rearrange("p k t -> p (k t)"), psT[:, u, 0:TC * P], ACT.Copy).then_inc(S["hT_ready"], 1)
                    loop(act, emit)


def moe_route(core, layer, L, slots, weights, expert_of_tile=None, tiles=0):
    nc, NT, aps, tag = core.nc, core.NT, core.aps, f"q{layer}"
    K = 2 if layer == 0 else 1
    on = ExitStack()
    with on:
        sb = lambda name, shape, dt=F32: core.sbuf(f"{tag}_{name}", shape, dt, on=on)
        big = lambda name: sb(name, [P, NT, E])
        rev, tri, allone = sb("rev", [P, E]), sb("tri", [P, P]), sb("allone", [P, P])
        gb = sb("gate_b", [P, E])
        m = [big(f"choice{k}") for k in range(K)]
        L2, eq, cand, lim, dist, ex = big("masked_logits"), big("is_max"), big("candidates"), big("limit"), big("distance"), big("expd")
        both, before, within, place = big("chosen"), big("tiles_before"), big("within"), big("place")
        v, r = [sb(f"top{k}", [P, NT]) for k in range(K)], sb("rank", [P, NT])
        total = sb("sum", [P, NT])
        zero = sb("zeros", [P, NT])
        cnt, cnt_i = sb("counts", [P, E]), sb("counts_int", [P, E], I32)
        ends, base = sb("tile_ends", [P, E]), sb("base", [P, E])
        slot_f = sb("slot_f", [P, NT])
        ps = core.psum(f"{tag}_ps", [P, 2, 512], on=on)
        s_in, s_exp, s_exped = core.sem(f"{tag}_loaded"), core.sem(f"{tag}_exp_in"), core.sem(f"{tag}_exp_out")
        s_m, s_cum = core.sem(f"{tag}_chosen"), core.sem(f"{tag}_cum_ps")
        per_token = lambda t: t[:].unsqueeze(2).broadcast_to([P, NT, E])
        per_expert = lambda t: t[:].unsqueeze(1).broadcast_to([P, NT, E])
        flat = lambda t: t[:].rearrange("p n e -> p (n e)")
        with nc.Block() as block:
            @block.sync
            def _(sp):
                sp.dma_start(rev[:], aps["rev_rank"]).then_inc(s_in, 16)
                sp.dma_start(tri[:], aps["tri"]).then_inc(s_in, 16)
                if layer:
                    sp.dma_start(gb[:], aps["L1_ffn_gate_b"].partition_broadcast(P)).then_inc(s_in, 16)

            @block.scalar
            def _(act):
                for k in range(K):
                    act.wait_ge(s_exp, k + 1)
                    nc.scalar.activation(flat(ex), flat(dist), ACT.Exp).then_inc(s_exped, 1)

            @block.tensor
            def _(pe):
                pe.wait_ge(s_m, 1)
                nc.tensor.matmul(ps[:, 0, 0:NT * E], tri[:], flat(both), start=True, stop=True)
                nc.tensor.matmul(ps[:, 1, 0:NT * E], allone[:], flat(both), start=True, stop=True).then_inc(s_cum, 1)

            @block.vector
            def _(dve):
                chain = Chain(core, dve, f"{tag}_dve_chain")
                step = chain.step
                tt, ts, stt, red = nc.vector.tensor_tensor, nc.vector.tensor_scalar, nc.vector.scalar_tensor_tensor, nc.vector.tensor_reduce
                L3 = L[:].rearrange("p (n e) -> p n e", e=E)
                dve.wait_ge(s_in, 32 + 16 * layer)
                nc.vector.memset(allone[:], 1.0)
                step(nc.vector.memset(zero[:], 0.0))
                if layer:
                    step(tt(L3, L3, per_expert(gb), ALU.add))

                def first_max(src, k):
                    step(red(v[k][:], src, AX.X, ALU.max))
                    step(tt(eq[:], src, per_token(v[k]), ALU.is_equal))
                    step(tt(cand[:], eq[:], per_expert(rev), ALU.mult))
                    step(red(r[:], cand[:], AX.X, ALU.max))
                    step(tt(m[k][:], cand[:], per_token(r), ALU.is_equal))

                first_max(L3, 0)
                if K == 2:
                    step(ts(flat(L2), flat(m[0]), -2e38, 1e38, ALU.mult, ALU.add))
                    step(tt(L2[:], L2[:], L3, ALU.min))
                    first_max(L2[:], 1)
                for k in range(K):
                    src = L3 if k == 0 else L2[:]
                    step(tt(dist[:], src, per_token(v[k]), ALU.subtract))
                    dist_ready = nc.vector.tensor_copy(total[:], zero[:])
                    dist_ready.then_inc(s_exp, 1)
                    dve.wait_ge(s_exp, k + 1)
                    if layer == 0:
                        step(stt(out=lim[:], in0=L3, scalar=-1.0, in1=L3, op0=ALU.mult, op1=ALU.max))
                        step(tt(lim[:], lim[:], per_token(v[k]), ALU.max))
                        step(stt(out=flat(lim), in0=flat(lim), scalar=0.02, in1=flat(dist), op0=ALU.mult, op1=ALU.add))
                        step(ts(flat(lim), flat(lim), 0.0, None, ALU.is_ge))
                        dve.wait_ge(s_exped, k + 1)
                        step(tt(flat(ex), flat(ex), flat(lim), ALU.mult))
                    else:
                        dve.wait_ge(s_exped, k + 1)
                    step(red(total[:], ex[:], AX.X, ALU.add))
                    step(nc.vector.reciprocal(weights[k][:], total[:]))
                if K == 2:
                    tt(both[:], m[0][:], m[1][:], ALU.add).then_inc(s_m, 1)
                else:
                    nc.vector.tensor_copy(flat(both), flat(m[0])).then_inc(s_m, 1)
                dve.wait_ge(s_cum, 1)
                tot = ps[:, 1, 0:NT * E].rearrange("p (n e) -> p n e", e=E)
                step(nc.vector.tensor_copy(within[:], tot))
                for e in range(E):
                    last = nc.vector.tensor_tensor_scan(before[:, :, e], within[:, :, e], zero[:], 0.0, ALU.add, ALU.add)
                step(last)
                step(nc.vector.tensor_copy(cnt[:], before[:, NT - 1, :]))
                step(tt(before[:], before[:], within[:], ALU.subtract))
                step(tt(place[:], before[:], ps[:, 0, 0:NT * E].rearrange("p (n e) -> p n e", e=E), ALU.add))
                if layer == 0:
                    step(ts(cnt_i[:], cnt[:], float(P - 1), None, ALU.add))
                    step(ts(cnt_i[:], cnt_i[:], 7, None, ALU.arith_shift_right))
                    step(nc.vector.tensor_copy(cnt[:], cnt_i[:]))
                    step(nc.vector.tensor_tensor_scan(ends[:], cnt[:], zero[:, 0:E], 0.0, ALU.add, ALU.add))
                    step(tt(base[:], ends[:], cnt[:], ALU.subtract))
                    step(ts(base[:], base[:], float(P), -1.0, ALU.mult, ALU.add))
                    step(tt(place[:], place[:], per_expert(base), ALU.add))
                    for k in range(K):
                        step(tt(cand[:], m[k][:], place[:], ALU.mult))
                        step(red(slot_f[:], cand[:], AX.X, ALU.add))
                        step(nc.vector.tensor_copy(slots[k][:], slot_f[:]))
                    tile_no = sb("tile_no", [1, tiles])
                    acc = sb("tile_expert", [1, tiles])
                    step(nc.vector.memset(acc[:], 1.0))
                    step(nc.vector.tensor_tensor_scan(tile_no[:], acc[:], acc[:], -1.0, ALU.mult, ALU.add))
                    step(nc.vector.memset(acc[:], 0.0))
                    for e in range(E - 1):
                        step(stt(out=acc[:], in0=tile_no[:], scalar=ends[0:1, e:e + 1], in1=acc[:], op0=ALU.is_ge, op1=ALU.add))
                    step(nc.vector.tensor_copy(expert_of_tile[:], acc[:]))
                else:
                    step(tt(cand[:], m[0][:], place[:], ALU.mult))
                    step(red(r[:], cand[:], AX.X, ALU.add))
                    step(ts(base[:], rev[:], -float(CAP), float(E * CAP - 1), ALU.mult, ALU.add))
                    step(tt(place[:], place[:], per_expert(base), ALU.add))
                    step(tt(cand[:], m[0][:], place[:], ALU.mult))
                    step(red(slot_f[:], cand[:], AX.X, ALU.add))
                    step(ts(r[:], r[:], float(CAP), None, ALU.is_le))
                    nc.vector.tensor_tensor(weights[0][:], weights[0][:], r[:], ALU.mult)
                    step(ts(slot_f[:], slot_f[:], -float(E * CAP), None, ALU.add))
                    step(tt(slot_f[:], slot_f[:], r[:], ALU.mult))
                    step(ts(slot_f[:], slot_f[:], float(E * CAP), None, ALU.add))
                    step(nc.vector.tensor_copy(slots[0][:], slot_f[:]))


def scatter_rows(core, tag, Hr, slots, table, rows):
    nc, NT, K = core.nc, core.NT, len(slots)
    on = ExitStack()
    with on:
        row = [core.sbuf(f"{tag}_row{n}", [P, D], on=on) for n in range(STAGES)]
        idx = [[core.sbuf(f"{tag}_idx{n}_{k}", [P, 1], U32, on=on) for k in range(K)] for n in range(STAGES)]
        S = start_counts(core, tag, ["row_staged", "slot_staged", "passed"])
        scattered = [core.sem(f"{tag}_scattered{u}") for u in range(STAGES)]

        def loop(eng, emit):
            for u in range(STAGES):
                emit(u, u, 0)
            with eng.Fori(0, NT // STAGES - 1) as t:
                for u in range(STAGES):
                    emit((t + 1) * STAGES + u, u, t + 1)

        with nc.Block() as block:
            @block.scalar
            def _(act):
                def emit(t, u, turn):
                    at(act, scattered[u], turn * (16 * K))
                    nc.scalar.activation(row[u][:], Hr[:, ds(t * D, D)], ACT.Copy).then_inc(S["row_staged"], 1)
                loop(act, emit)

            @block.vector
            def _(dve):
                def emit(t, u, turn):
                    at(dve, scattered[u], turn * (16 * K))
                    for k in range(K):
                        last = nc.vector.tensor_copy(idx[u][k][:], slots[k][:, ds(t, 1)])
                    last.then_inc(S["slot_staged"], 1)
                loop(dve, emit)

            @block.gpsimd
            def _(pool):
                def emit(t, u, turn):
                    upto(pool, S["row_staged"], t + 1)
                    at_alone(pool, S["slot_staged"], t + 2, S["passed"])
                    for k in range(K):
                        nc.gpsimd.indirect_dma_start(out=table, out_offset=bass.IndirectOffsetOnAxis(ap=idx[u][k][:, 0:1], axis=0),
                                                     in_=row[u][:], in_offset=None, bounds_check=rows - 1, oob_is_err=False)\
                            .then_inc(scattered[u], 16)
                loop(pool, emit)
                for u in range(STAGES):
                    pool.wait_ge(scattered[u], 16 * K * (NT // STAGES))


def experts0(core, XS, YS, expert_of_tile, tiles):
    nc, aps = core.nc, core.aps
    U = 3
    assert tiles % U == 0
    on = ExitStack()
    with on:
        sb = lambda name, shape, dt=F32: core.sbuf("e0_" + name, shape, dt, on=on)
        w1, w3, w2 = sb("w1", [P, E, F]), sb("w3", [P, E, F]), sb("w2", [P, E, FC, D])
        x = [sb(f"x{n}", [P, D]) for n in range(U)]
        xT = [sb(f"xT{n}", [P, P]) for n in range(U)]
        act_h = [sb(f"silu{n}", [P, F]) for n in range(U)]
        g = [sb(f"g{n}", [P, FC, P]) for n in range(U)]
        gT = [sb(f"gT{n}", [P, FC, P]) for n in range(U)]
        y = [sb(f"y{n}", [P, D]) for n in range(U)]
        psX, ps1, ps3, psY = (core.psum("e0_ps" + n, [P, 512], on=on) for n in "X13Y")
        psG = core.psum("e0_psG", [P, FC, P], on=on)
        S = start_counts(core, "e0", ["w_loaded", "xT_ps", "xT_ready", "h1_ps", "h3_ps", "silu_ready", "g_ready", "gT_ps", "gT_ready",
                                      "y_ps", "y_ready"] + [f"{n}{u}" for n in ("x_loaded", "y_stored") for u in range(U)])
        turns = tiles // U
        LAG = 4

        def loop(eng, emit):
            peeled = 2 * U
            for i in range(peeled):
                emit(i, i % U, i // U)
            with eng.Fori(0, turns - 2) as t:
                for u in range(U):
                    emit(t * U + (peeled + u), u, t + 2)
            for i in range(tiles, tiles + LAG):
                emit(i, i % U, i // U)

        live = lambda i, lag: not isinstance(i, int) or 0 <= i - lag < tiles
        buf = lambda u, lag: (u - lag) % U
        times = lambda u, turn, lag: turn + (u - lag) // U

        with nc.Block() as block:
            @block.sync
            def _(sp):
                for t, n in ((w1, "L0_ffn_w1"), (w3, "L0_ffn_w3")):
                    sp.dma_start(t[:], aps[n].rearrange("e d f -> d e f")).then_inc(S["w_loaded"], 16)
                sp.dma_start(w2[:].rearrange("p e c d -> p (e c) d"), aps["L0_ffn_w2"].rearrange("e (c f) d -> f (e c) d", f=P)).then_inc(S["w_loaded"], 16)

                def emit(i, u, turn):
                    if live(i, 0):
                        upto(sp, S["xT_ps"], i - U + 1)
                        sp.dma_start(x[u][:], XS[ds(i * P, P), :]).then_inc(S[f"x_loaded{u}"], 16)
                    if live(i, 4):
                        j, n = i - 4, buf(u, 4)
                        upto(sp, S["y_ready"], j + 1)
                        sp.dma_start(YS[ds(j * P, P), :], y[n][:]).then_inc(S[f"y_stored{n}"], 16)
                loop(sp, emit)
                for u in range(U):
                    upto(sp, S[f"y_stored{u}"], 16 * turns)

            @block.tensor
            def _(pe):
                mm = nc.tensor.matmul
                upto(pe, S["w_loaded"], 48)
                expert = lambda j: pe.value_load(expert_of_tile[0:1, ds(j, 1)], min_val=0, max_val=E - 1)

                def emit(i, u, turn):
                    if live(i, 1):
                        j, n = i - 1, buf(u, 1)
                        e = expert(j)
                        upto(pe, S["xT_ready"], j + 1)
                        upto(pe, S["silu_ready"], j)
                        mm(ps1[:], xT[n][:], w1[:, ds(e, 1), :].rearrange("p n f -> p (n f)"), start=True, stop=True).then_inc(S["h1_ps"], 1)
                        upto(pe, S["g_ready"], j)
                        mm(ps3[:], xT[n][:], w3[:, ds(e, 1), :].rearrange("p n f -> p (n f)"), start=True, stop=True).then_inc(S["h3_ps"], 1)
                    if live(i, 3):
                        j, n = i - 3, buf(u, 3)
                        e = expert(j)
                        upto(pe, S["gT_ready"], j + 1)
                        upto(pe, S["y_ready"], j)
                        for c in range(FC):
                            last = mm(psY[:, 0:D], gT[n][:, c, :], w2[:, ds(e, 1), c, :].rearrange("p n d -> p (n d)"), start=(c == 0), stop=(c == FC - 1))
                        last.then_inc(S["y_ps"], 1)
                    if live(i, 0):
                        upto(pe, S[f"x_loaded{u}"], 16 * (turn + 1))
                        upto(pe, S["xT_ready"], i)
                        nc.tensor.transpose(psX[:, 0:P], x[u][:], core.ident[:]).then_inc(S["xT_ps"], 1)
                    if live(i, 2):
                        j, n = i - 2, buf(u, 2)
                        upto(pe, S["g_ready"], j + 1)
                        upto(pe, S["gT_ready"], j)
                        for c in range(FC):
                            last = nc.tensor.transpose(psG[:, c, :], g[n][:, c, :], core.ident[:])
                        last.then_inc(S["gT_ps"], 1)
                loop(pe, emit)

            @block.scalar
            def _(act):
                def emit(i, u, turn):
                    if live(i, 1):
                        j, n = i - 1, buf(u, 1)
                        upto(act, S["h1_ps"], j + 1)
                        upto(act, S["g_ready"], j - U + 1)
                        nc.scalar.activation(act_h[n][:], ps1[:], ACT.Silu).then_inc(S["silu_ready"], 1)
                    if live(i, 2):
                        j, n = i - 2, buf(u, 2)
                        upto(act, S["gT_ps"], j + 1)
                        upto(act, S["y_ps"], j - U + 1)
                        nc.scalar.activation(gT[n][:].rearrange("p c t -> p (c t)"), psG[:].rearrange("p c t -> p (c t)"), ACT.Copy).then_inc(S["gT_ready"], 1)
                loop(act, emit)

            @block.vector
            def _(dve):
                def emit(i, u, turn):
                    if live(i, 1):
                        j, n = i - 1, buf(u, 1)
                        upto(dve, S["silu_ready"], j + 1)
                        upto(dve, S["h3_ps"], j + 1)
                        upto(dve, S["gT_ps"], j - U + 1)
                        nc.vector.tensor_tensor(g[n][:].rearrange("p c t -> p (c t)"), act_h[n][:], ps3[:], ALU.mult).then_inc(S["g_ready"], 1)
                    if live(i, 3):
                        j, n = i - 3, buf(u, 3)
                        upto(dve, S["y_ps"], j + 1)
                        upto(dve, S[f"y_stored{n}"], times(u, turn, 3) * 16)
                        nc.vector.tensor_copy(y[n][:], psY[:, 0:D]).then_inc(S["y_ready"], 1)
                    if live(i, 0):
                        upto(dve, S["xT_ps"], i + 1)
                        upto(dve, S["h3_ps"], i - U + 1)
                        nc.vector.tensor_copy(xT[u][:], psX[:, 0:P]).then_inc(S["xT_ready"], 1)
                loop(dve, emit)


def gather_and_add(core, tag, layer, slots, weights, table):
    nc, NT, B, X, K = core.nc, core.NT, core.B, core.X, len(slots)
    GB = STAGES // TC
    on = ExitStack()
    with on:
        yg = [[core.sbuf(f"{tag}_y{n}_{k}", [P, D], on=on) for k in range(K)] for n in range(STAGES)]
        idx = [[core.sbuf(f"{tag}_idx{n}_{k}", [P, 1], U32, on=on) for k in range(K)] for n in range(STAGES)]
        acc = [core.sbuf(f"{tag}_acc{n}", [P, D], on=on) for n in range(STAGES)]
        gate = [core.sbuf(f"{tag}_gate{n}", [P, D], on=on) for n in range(GB)]
        S = start_counts(core, tag, ["slot_staged", "weighted", "summed", "gated", "x_updated", "passed"] + [f"gate_loaded{u}" for u in range(GB)])
        gathered = [core.sem(f"{tag}_gathered{u}") for u in range(STAGES)]
        turns = NT // STAGES

        with nc.Block() as block:
            @block.sync
            def _(sp):
                with sp.Fori(0, turns) as turn:
                    for n in range(GB):
                        upto(sp, S["gated"], turn * STAGES)
                        sp.dma_start(gate[n][:], core.modrow[1 + 2 * layer, ds(turn * GB + n, 1), :].rearrange("n d -> (n d)").partition_broadcast(P))\
                            .then_inc(S[f"gate_loaded{n}"], 16)

            @block.gpsimd
            def _(pool):
                with pool.Fori(0, turns) as turn:
                    for u in range(STAGES):
                        at_alone(pool, S["slot_staged"], turn * STAGES + (u + 1) + 1, S["passed"])
                        for k in range(K):
                            nc.gpsimd.indirect_dma_start(out=yg[u][k][:], out_offset=None, in_=table,
                                                         in_offset=bass.IndirectOffsetOnAxis(ap=idx[u][k][:, 0:1], axis=0))\
                                .then_inc(gathered[u], 16)

            @block.vector
            def _(dve):
                ahead = STAGES - 1

                def stage(t, u):
                    for k in range(K):
                        last = nc.vector.tensor_copy(idx[u][k][:], slots[k][:, ds(t, 1)])
                    last.then_inc(S["slot_staged"], 1)

                for t in range(ahead):
                    stage(t, t)

                def emit(t, u, turn):
                    if not isinstance(t, int) or t + ahead < NT:
                        stage(t + ahead, (u + ahead) % STAGES)
                    dve.wait_ge(gathered[u], (turn + 1) * (16 * K))
                    nc.vector.tensor_scalar(acc[u][:], yg[u][0][:], weights[0][:, ds(t, 1)], None, ALU.mult).then_inc(S["weighted"], 1)
                    upto(dve, S["weighted"], t + 1)
                    if K == 2:
                        nc.vector.scalar_tensor_tensor(out=acc[u][:], in0=yg[u][1][:], scalar=weights[1][:, ds(t, 1)], in1=acc[u][:],
                                                       op0=ALU.mult, op1=ALU.add).then_inc(S["summed"], 1)
                        upto(dve, S["summed"], t + 1)
                    upto(dve, S[f"gate_loaded{u // TC}"], (turn + 1) * 16)
                    nc.vector.tensor_tensor(acc[u][:], acc[u][:], gate[u // TC][:], ALU.mult).then_inc(S["gated"], 1)
                    upto(dve, S["gated"], t + 1)
                    x = X[:, ds(t * D, D)]
                    nc.vector.tensor_tensor(x, x, acc[u][:], ALU.add).then_inc(S["x_updated"], 1)

                with dve.Fori(0, turns - 1) as turn:
                    for u in range(STAGES):
                        emit(turn * STAGES + u, u, turn)
                for u in range(STAGES):
                    emit((turns - 1) * STAGES + u, u, turns - 1)
                upto(dve, S["x_updated"], NT)


def ffn0(core):
    nc, NT = core.nc, core.NT
    tiles = 2 * NT + E - 1
    tiles += -tiles % 3
    XS = nc.dram_tensor("slot_inputs", [tiles * P, D], F32, kind="Internal").ap()
    YS = nc.dram_tensor("slot_outputs", [tiles * P, D], F32, kind="Internal").ap()
    on = ExitStack()
    with on:
        slots = [core.sbuf(f"slots0_{k}", [P, NT], U32, on=on) for k in range(2)]
        weights = [core.sbuf(f"weights0_{k}", [P, NT], on=on) for k in range(2)]
        expert_of_tile = core.sbuf("expert_of_tile", [1, tiles], I32, on=on)
        scratch = ExitStack()
        with scratch:
            Hr = core.sbuf("h_rows0", [P, NT * D], on=scratch)
            L = core.sbuf("logits0", [P, NT * E], on=scratch)
            fill_zero(core, "xs0", XS, tiles)
            modulated(core, 0, Hr, L, 4)
            moe_route(core, 0, L, slots, weights, expert_of_tile, tiles)
            scatter_rows(core, "sc0", Hr, slots, XS, tiles * P)
        experts0(core, XS, YS, expert_of_tile, tiles)
        gather_and_add(core, "ga0", 0, slots, weights, YS)
DI, DS, DC, DTR = 256, 16, 4, 8
C2 = DI // P
DIRS = 2
G = 2
W = G * T
BC = 2 * DS
PREP = [("x",), ("conv", 0, 0), ("conv", 0, 1), ("conv", 1, 0), ("dt", 0, 0), ("conv", 1, 1), ("dt", 0, 1), ("bc", 0),
        ("dt", 1, 0), ("dt", 1, 1), ("bc", 1), ("z", 0), ("z", 1)]
USES = len(PREP)
BANK_USES = ((USES + 1) // 2, USES // 2)
USE = {what: n for n, what in enumerate(PREP)}
PREP_AT = {0: [("x", 0, 1)], 1: [("conv", 0, 0, 0, 3)], 2: [("conv", 0, 0, 3, 4), ("conv", 0, 1, 0, 2)],
           3: [("conv", 0, 1, 2, 4), ("conv", 1, 0, 0, 1)], 4: [("conv", 1, 0, 1, 4)], 5: [("dt", 0, 0, 0, 2)],
           6: [("conv", 1, 1, 0, 3)], 7: [("conv", 1, 1, 3, 4), ("dt", 0, 1, 0, 2)], 8: [("bc", 0, 0, 2)], 9: [("dt", 1, 0, 0, 2)],
           10: [("dt", 1, 1, 0, 2)], 11: [("bc", 1, 0, 2)], 12: [("z", 0, 0, 1)], 13: [("z", 1, 0, 1)]}


def mixer_weights(core, Wt, on):
    nc, aps = core.nc, core.aps
    tmp = ExitStack()
    with tmp:
        sb = lambda name, shape, dt=F32: core.sbuf("w_" + name, shape, dt, on=tmp)
        win = sb("in_proj", [P, 4, D])
        taps = sb("conv_w", [P, DIRS, C2, DC])
        scaled = sb("in_taps", [P, DIRS, C2, DC, D])
        wout = sb("out_proj", [P, DI])
        xp = sb("x_proj", [BC + DTR, DIRS, DI])
        xdt = sb("x_proj_dt", [DTR, DIRS, DI])
        dtT = sb("dt_w_T", [DTR, DIRS, DI])
        sel = sb("selector", [PARTS * BC, BC])
        alog = sb("A_log", [P, DIRS, C2, DS])
        ps = core.psum("w_ps", [P, 4, 512], on=tmp)
        S = {n: core.sem("w_" + n) for n in ("loaded", "scaled", "ps", "kept", "exp_done", "done")}
        names = "fb"
        jobs = []
        for d in range(DIRS):
            for c in range(C2):
                for k in range(DC):
                    jobs.append((Wt["taps"][:, d, c, k, :], scaled[:, d, c, k, :], None))
        for c in range(C2):
            jobs.append((Wt["z"][:, c, :], win[:, C2 + c, :], None))
            jobs.append((Wt["out"][:, c, :], wout[:, c * P:(c + 1) * P], None))
        for d in range(DIRS):
            for c in range(C2):
                jobs.append((Wt["bc"][:, d, c, :], xp[0:BC, d, c * P:(c + 1) * P], None))
                for c2 in range(C2):
                    jobs.append((Wt["dt"][:, d, c, c2, :], xdt[:, d, c * P:(c + 1) * P], dtT[:, d, c2 * P:(c2 + 1) * P]))
        with nc.Block() as block:
            @block.sync
            def _(sp):
                n = 0

                def load(dst, src, **how):
                    sp.dma_start(dst, src, **how).then_inc(S["loaded"], 16)
                load(win[:], aps["L1_attn_in_proj_w"].rearrange("(c p) e -> p c e", p=P))
                load(wout[:], aps["L1_attn_out_proj_w"])
                load(sel[:], aps["selector"])
                for d, f in enumerate(names):
                    load(taps[:, d], aps[f"L1_attn_conv_w_{f}"].rearrange("(c p) k -> p c k", p=P))
                    x = aps[f"L1_attn_x_proj_w_{f}"]
                    load(xp[0:BC, d], x[DTR:DTR + BC])
                    load(xdt[:, d], x[0:DTR])
                    load(dtT[:, d], aps[f"L1_attn_dt_w_{f}"].rearrange("d r -> r d"), allow_slow_non_contiguous=True)
                    load(alog[:, d], aps[f"L1_attn_A_log_{f}"].rearrange("(c p) s -> p c s", p=P))
                    for name, key in (("conv_b", "conv_b"), ("dt_b", "dt_b"), ("D", "D")):
                        load(Wt[key][:, d], aps[f"L1_attn_{name}_{f}"].rearrange("(c p n) -> p c n", p=P, n=1), allow_slow_non_contiguous=True)
                load(Wt["ln1"][:, 0:1], aps["L1_attn_ln1_g"].rearrange("(p n) -> p n", n=1))
                load(Wt["ln1"][:, 1:2], aps["L1_attn_ln1_b"].rearrange("(p n) -> p n", n=1))

            loads = 16 * (3 + DIRS * 8 + 2)

            @block.scalar
            def _(act):
                act.wait_ge(S["loaded"], loads)
                nc.scalar.activation(Wt["A"][:].rearrange("p d c s -> p (d c s)"), alog[:].rearrange("p d c s -> p (d c s)"), ACT.Exp).then_inc(S["exp_done"], 1)

            @block.vector
            def _(dve):
                dve.wait_ge(S["loaded"], loads)
                for d in range(DIRS):
                    for c in range(C2):
                        for k in range(DC):
                            last = nc.vector.tensor_scalar(scaled[:, d, c, k, :], win[:, c, :], taps[:, d, c, k:k + 1], None, ALU.mult)
                last.then_inc(S["scaled"], 1)
                nc.vector.tensor_copy(Wt["sel"][:], sel[:].unsqueeze(2).broadcast_to([PARTS * BC, BC, P]))
                nc.vector.memset(Wt["one"][:], 1.0)
                dve.wait_ge(S["exp_done"], 1)
                a = Wt["A"][:].rearrange("p d c s -> p (d c s)")
                nc.vector.tensor_scalar(a, a, -1.0, None, ALU.mult)
                for n, (dst, _, rhs) in enumerate(jobs):
                    dve.wait_ge(S["ps"], n + 1)
                    nc.vector.tensor_copy(dst, ps[:, n % 4, 0:dst.shape[-1]]).then_inc(S["kept"], 1)
                dve.wait_ge(S["kept"], len(jobs))

            @block.tensor
            def _(pe):
                pe.wait_ge(S["scaled"], 1)
                for n, (dst, src, rhs) in enumerate(jobs):
                    at(pe, S["kept"], n - 3)
                    if rhs is None:
                        k = src.shape[0]
                        nc.tensor.transpose(ps[:, n % 4, 0:k], src, core.ident[0:k, 0:k]).then_inc(S["ps"], 1)
                    else:
                        nc.tensor.matmul(ps[:, n % 4, 0:P], src, rhs, start=True, stop=True).then_inc(S["ps"], 1)


def mixer(core, Hr, OD):
    nc, B, aps = core.nc, core.B, core.aps
    NP = B // G
    live = lambda i, lag: not isinstance(i, int) or 0 <= i - lag < NP
    on = ExitStack()
    with on:
        sb = lambda name, shape, dt=F32: core.sbuf("s_" + name, shape, dt, on=on)
        Wt = {"taps": sb("w_taps", [P, DIRS, C2, DC, P]), "z": sb("w_z", [P, C2, P]), "out": sb("w_out", [P, C2, P]),
              "bc": sb("w_bc", [P, DIRS, C2, BC]), "dt": sb("w_dt", [P, DIRS, C2, C2, P]), "sel": sb("w_sel", [PARTS * BC, BC, P], BF16),
              "A": sb("A", [P, DIRS, C2, DS]), "conv_b": sb("conv_b", [P, DIRS, C2, 1]), "dt_b": sb("dt_b", [P, DIRS, C2, 1]),
              "D": sb("D", [P, DIRS, C2, 1]), "ln1": sb("ln1", [P, 2]), "one": sb("one", [P, 1])}
        mixer_weights(core, Wt, on)
        PADW = T + 2 * (DC - 1)
        xn = sb("xn", [P, G * TC, P])
        xT = sb("xT", [P, G, PADW])
        xc = [sb(f"xc{n}", [P, DIRS, C2, W]) for n in range(2)]
        z = [sb(f"z{n}", [P, C2, W]) for n in range(2)]
        dt = [sb(f"dt{n}", [P, DIRS, C2, W]) for n in range(2)]
        ux = [sb(f"ux{n}", [P, DIRS, C2, W]) for n in range(2)]
        bcs = [sb(f"bc_parts{n}", [PARTS * BC, DIRS, W], BF16) for n in range(2)]
        rest, part2 = sb("bc_rest", [BC, W]), sb("bc_part2", [BC, W], BF16)
        e_abs, e_one, e_ln = sb("exp_abs", [P, DIRS, C2, W]), sb("exp_plus_1", [P, C2, W]), sb("ln", [P, C2, W])
        dA = [sb(f"dA{n}", [P, DIRS, C2, G, T]) for n in range(2)]
        bsb = [sb(f"B_rows{n}", [P, DIRS, W]) for n in range(2)]
        R = core.X[:, 0:8192].rearrange("p (n d c w) -> p n d c w", n=4, d=DIRS, c=C2)
        yg = sb("y_gated", [P, C2, W])
        o = sb("out", [P, G * TC, D])
        YP = core.psum("s_y", [P, C2, W], on=on)
        BP = core.psum("s_B", [P, DIRS, W], on=on)
        CP = core.psum("s_C", [P, DIRS, W], on=on)
        PR = core.psum("s_prep", [P, 2, 512], on=on)
        S = {n: core.sem("s_" + n) for n in (
            "xn_ready", "prep_ps", "prep_read0", "prep_read1", "silu_done", "bc_part1", "bc_rest", "bc_part2", "bc_ready", "abs_done", "z_done",
            "relu_done", "exp_done", "plus1_done", "ln_done", "corr_done", "ln_corr", "dt_ready", "u_ready", "B_ps", "C_ps",
            "B_ready", "dA_ready", "in_ready", "scanned", "part_ready", "summed", "y_read", "y_skip", "gated", "out_ps", "out_read",
            "stats_done", "out_stored", "pads", "x_saved")}
        flat = lambda t: t.rearrange("p c w -> p (c w)")
        read = lambda u: S[f"prep_read{u % 2}"]

        xsave = nc.dram_tensor("x_saved", [P, core.NT * D], F32, kind="Internal").ap()
        with nc.Block() as block:
            @block.sync
            def _(sp):
                sp.dma_start(xsave, core.X[:, 0:core.NT * D]).then_inc(S["x_saved"], 16)
                sp.wait_ge(S["x_saved"], 16)

            @block.vector
            def _(dve):
                nc.vector.memset(xT[:], 0.0)
                for n in range(2):
                    nc.vector.memset(dA[n][:, 0, :, :, 0:1], 0.0)
                    last = nc.vector.memset(dA[n][:, 1, :, :, T - 1:T], 0.0)
                last.then_inc(S["pads"], 1)
                dve.wait_ge(S["pads"], 1)

        with nc.Block() as block:
            @block.sync
            def _(sp):
                def emit(i, u):
                    if live(i, 2):
                        j = i - 2
                        sp.wait_ge(S["stats_done"], j + 1)
                        sp.dma_start(OD[ds(j * (G * TC), G * TC)].rearrange("n p d -> p n d"), o[:]).then_inc(S["out_stored"], 16)
                rolled(sp, NP, 2, 3, emit, ring=2)
                sp.wait_ge(S["out_stored"], 16 * NP)

            @block.gpsimd
            def _(pool):
                def inputs(j, par, s):
                    pool.wait_ge(S["B_ready"], j * DS + (s + 1))
                    if s == 0:
                        pool.wait_ge(S["u_ready"], DIRS * (j + 1))
                    at(pool, S["summed"], j * DS + (s - 3))
                    nc.gpsimd.tensor_tensor(R[:, s % 4], ux[par][:], bsb[s % 2][:].unsqueeze(2).broadcast_to([P, DIRS, C2, W]),
                                            ALU.mult).then_inc(S["in_ready"], 1)

                def emit(i, u):
                    for s in range(DS):
                        if live(i, 1) and s > 0:
                            inputs(i - 1, (u + 1) % 2, s)
                        if s == 1 and live(i, 2):
                            pool.wait_ge(S["y_skip"], i - 1)
                            nc.gpsimd.tensor_tensor(yg[:], yg[:], z[u][:], ALU.mult).then_inc(S["gated"], 1)
                        if s in (11, 14) and live(i, 0):
                            d = (s - 11) // 3
                            pool.wait_ge(S["dt_ready"], DIRS * i + (d + 1))
                            nc.gpsimd.tensor_tensor(ux[u][:, d], dt[u][:, d], xc[u][:, d], ALU.mult).then_inc(S["u_ready"], 1)
                    if live(i, 0):
                        inputs(i, u, 0)
                rolled(pool, NP, 2, 3, emit, ring=2)

            @block.scalar
            def _(act):
                def front(j, par, s):
                    act.wait_ge(S["B_ps"], j * DS + (s + 1))
                    at(act, S["in_ready"], j * DS + (s - 1))
                    nc.scalar.activation(bsb[s % 2][:].rearrange("p d w -> p (d w)"), BP[:].rearrange("p d w -> p (d w)"), ACT.Copy).then_inc(S["B_ready"], 1)
                    if s == 0:
                        act.wait_ge(S["dt_ready"], DIRS * (j + 1))
                    at(act, S["scanned"], DIRS * (j * DS + (s - 1)))
                    for d in range(DIRS):
                        lo = 1 - d
                        for c in range(C2):
                            last = nc.scalar.activation(dA[s % 2][:, d, c, :, lo:lo + T - 1], dt[par][:, d, c, :].rearrange("p (g t) -> p g t", t=T)[:, :, lo:lo + T - 1],
                                                        ACT.Exp, scale=Wt["A"][:, d, c, s:s + 1])
                    last.then_inc(S["dA_ready"], 1)

                def softplus(i, d):
                    act.wait_ge(S["abs_done"], C2 * (DIRS * i + d) + C2)
                    func(flat(e_abs[:, d]), flat(e_abs[:, d]), ACT.Exp, scale=-1.0).then_inc(S["exp_done"], 1)
                    act.wait_ge(S["exp_done"], DIRS * i + (d + 1))
                    at(act, S["dt_ready"], DIRS * i + d)
                    func(flat(e_one[:]), flat(e_abs[:, d]), ACT.Identity, bias=Wt["one"][:, 0:1]).then_inc(S["plus1_done"], 1)
                    act.wait_ge(S["plus1_done"], DIRS * i + (d + 1))
                    func(flat(e_ln[:]), flat(e_one[:]), ACT.Ln).then_inc(S["ln_done"], 1)

                func = nc.scalar.activation

                def take(i, what):
                    use = USE[what]
                    act.wait_ge(S["prep_ps"], USES * i + (use + 1))
                    return PR[:, use % 2, :], read(use)

                def conv(i, u, d, c):
                    bank, done = take(i, ("conv", d, c))
                    func(xc[u][:, d, c, :], bank, ACT.Identity, bias=Wt["conv_b"][:, d, c, :]).then_inc(done, 1)

                def gate(i, u, c):
                    bank, done = take(i, ("z", c))
                    func(z[u][:, c, :], bank, ACT.Identity).then_inc(done, 1)

                def step_size(i, u, d, c):
                    bank, done = take(i, ("dt", d, c))
                    at(act, S["corr_done"], DIRS * (i - 1) + d + 1)
                    bias = Wt["dt_b"][:, d, c, :]
                    func(e_abs[:, d, c, :], bank, ACT.Abs, bias=bias).then_inc(S["abs_done"], 1)
                    func(dt[u][:, d, c, :], bank, ACT.Relu, bias=bias).then_inc(done, 1)

                def all_read(i, use):
                    act.wait_ge(read(use), BANK_USES[use % 2] * i + (use // 2 + 1))

                def emit(i, u):
                    for s in range(DS):
                        if live(i, 1) and s < DS - 1:
                            front(i - 1, (u + 1) % 2, s + 1)
                        if live(i, 0):
                            if s == 0:
                                bank, done = take(i, ("x",))
                                func(xT[:, :, DC - 1:DC - 1 + T], bank.rearrange("p (g t) -> p g t", t=T), ACT.Identity,
                                     scale=Wt["ln1"][:, 0:1], bias=Wt["ln1"][:, 1:2]).then_inc(done, 1)
                            if s == 3:
                                at(act, S["y_skip"], i - 1)
                                conv(i, u, 0, 0)
                            if s == 4:
                                conv(i, u, 0, 1)
                            if s == 5:
                                conv(i, u, 1, 0)
                            if s == 8:
                                conv(i, u, 1, 1)
                            if s in (4, 8):
                                d = s // 4 - 1
                                for c in range(C2):
                                    all_read(i, USE["conv", d, c])
                                func(flat(xc[u][:, d]), flat(xc[u][:, d]), ACT.Silu).then_inc(S["silu_done"], 1)
                            if s == 6:
                                step_size(i, u, 0, 0)
                            if s == 8:
                                step_size(i, u, 0, 1)
                            if s == 9:
                                softplus(i, 0)
                            if s == 10:
                                step_size(i, u, 1, 0)
                            if s == 11:
                                step_size(i, u, 1, 1)
                            if s == 12:
                                softplus(i, 1)
                            if s == 13:
                                at(act, S["gated"], i - 1)
                                for c in range(C2):
                                    gate(i, u, c)
                                for c in range(C2):
                                    all_read(i, USE["z", c])
                                func(flat(z[u][:]), flat(z[u][:]), ACT.Silu).then_inc(S["z_done"], 1)
                        if s == 15 and live(i, 2):
                            j = i - 2
                            act.wait_ge(S["out_ps"], j + 1)
                            at(act, S["out_stored"], 16 * j)
                            func(o[:].rearrange("p n d -> p (n d)"), PR[:, 1, :], ACT.Copy).then_inc(S["out_read"], 1)
                        if s == DS - 1 and live(i, 0):
                            front(i, u, 0)
                rolled(act, NP, 2, 3, emit, ring=2)

            @block.vector
            def _(dve):
                tt, stt = nc.vector.tensor_tensor, nc.vector.scalar_tensor_tensor

                def scan(j, s):
                    n = j * DS + s
                    dve.wait_ge(S["dA_ready"], n + 1)
                    dve.wait_ge(S["in_ready"], n + 1)
                    for d in range(DIRS):
                        r, a = flat(R[:, s % 4, d]), dA[s % 2][:, d].rearrange("p c g t -> p (c g t)")
                        if d:
                            r, a = r[:, ::-1], a[:, ::-1]
                        nc.vector.tensor_tensor_scan(r, a, r, 0.0, ALU.mult, ALU.add).then_inc(S["scanned"], 1)
                    dve.wait_ge(S["C_ps"], n + 1)
                    for d in range(DIRS):
                        dve.wait_ge(S["scanned"], DIRS * n + (d + 1))
                        r = R[:, s % 4, d]
                        last = tt(r, r, CP[:, d, :].unsqueeze(1).broadcast_to([P, C2, W]), ALU.mult)
                    last.then_inc(S["part_ready"], 1)

                def emit(i, u):
                    for s in range(DS):
                        if s == 0 and live(i, 0):
                            at(dve, S["prep_ps"], USES * (i - 1) + 1)
                            for k in range(G * TC):
                                c = i * (G * TC) + k
                                last = nc.vector.tensor_scalar(xn[:, k, :], Hr[:, ds(c * D, D)], core.rstd[:, ds(c, 1)], core.nmr[:, ds(c, 1)],
                                                               ALU.mult, ALU.add)
                            last.then_inc(S["xn_ready"], 1)
                        if live(i, 1):
                            scan(i - 1, s)
                        if s == 0 and live(i, 2):
                            j, par = i - 2, u
                            dve.wait_ge(S["summed"], DS * (j + 1))
                            at(dve, S["out_ps"], j)
                            for c in range(C2):
                                last = stt(out=yg[:, c, :], in0=xc[par][:, 0, c, :], scalar=Wt["D"][:, 0, c, :], in1=YP[:, c, :], op0=ALU.mult, op1=ALU.add)
                            last.then_inc(S["y_read"], 1)
                            dve.wait_ge(S["y_read"], j + 1)
                            for c in range(C2):
                                last = stt(out=yg[:, c, :], in0=xc[par][:, 1, c, :], scalar=Wt["D"][:, 1, c, :], in1=yg[:, c, :], op0=ALU.mult, op1=ALU.add)
                            last.then_inc(S["y_skip"], 1)
                        if s in (9, 12) and live(i, 0):
                            d = (s - 9) // 3
                            use = USE["bc", d]
                            n = DIRS * i + d
                            dve.wait_ge(S["prep_ps"], USES * i + use + 1)
                            at(dve, S["C_ps"], DS * (i - 1))
                            psb = PR[0:BC, use % 2, :]
                            nc.vector.tensor_copy(bcs[u][0:BC, d, :], psb).then_inc(S["bc_part1"], 1)
                            dve.wait_ge(S["bc_part1"], n + 1)
                            tt(rest[:], psb, bcs[u][0:BC, d, :], ALU.subtract).then_inc(S["bc_rest"], 1)
                            dve.wait_ge(S["bc_rest"], n + 1)
                            nc.vector.tensor_copy(part2[:], rest[:]).then_inc(S["bc_part2"], 1)
                            dve.wait_ge(S["bc_part2"], n + 1)
                            nc.vector.tensor_copy(bcs[u][BC:2 * BC, d, :], part2[:]).then_inc(read(use), 1)
                            tt(bcs[u][2 * BC:3 * BC, d, :], rest[:], part2[:], ALU.subtract).then_inc(S["bc_ready"], 1)
                        if s in (10, 13) and live(i, 0):
                            d = (s - 10) // 3
                            n = DIRS * i + d
                            dve.wait_ge(S["ln_done"], n + 1)
                            stt(out=flat(e_one[:]), in0=flat(e_one[:]), scalar=-1.0, in1=flat(e_abs[:, d]), op0=ALU.add, op1=ALU.subtract).then_inc(S["corr_done"], 1)
                            dve.wait_ge(S["corr_done"], n + 1)
                            tt(flat(e_ln[:]), flat(e_ln[:]), flat(e_one[:]), ALU.subtract).then_inc(S["ln_corr"], 1)
                            dve.wait_ge(S["ln_corr"], n + 1)
                            tt(flat(dt[u][:, d]), flat(dt[u][:, d]), flat(e_ln[:]), ALU.add).then_inc(S["dt_ready"], 1)
                        if s == 15 and live(i, 2):
                            j = i - 2
                            dve.wait_ge(S["out_read"], j + 1)
                            for k in range(G * TC):
                                c = j * (G * TC) + k
                                last = nc.vector.bn_stats(core.st[:, ds(c, 1), :].rearrange("p n k -> p (n k)"), o[:, k, :])
                            last.then_inc(S["stats_done"], 1)
                rolled(dve, NP, 2, 3, emit, ring=2)
                dve.wait_ge(S["stats_done"], NP)

            @block.tensor
            def _(pe):
                mm = nc.tensor.matmul

                def b_rows(j, par, s):
                    if s == 0:
                        pe.wait_ge(S["bc_ready"], DIRS * (j + 1))
                    at(pe, S["B_ready"], j * DS + s)
                    for d in range(DIRS):
                        last = mm(BP[:, d, :], Wt["sel"][:, s, :], bcs[par][:, d, :], start=True, stop=True)
                    last.then_inc(S["B_ps"], 1)

                def c_rows(j, par, s):
                    at(pe, S["part_ready"], j * DS + s)
                    for d in range(DIRS):
                        last = mm(CP[:, d, :], Wt["sel"][:, DS + s, :], bcs[par][:, d, :], start=True, stop=True)
                    last.then_inc(S["C_ps"], 1)

                def add_up(j, s):
                    at(pe, S["part_ready"], j * DS + (s + 1))
                    if s == 0:
                        at(pe, S["y_read"], j)
                    for c in range(C2):
                        for d in range(DIRS):
                            last = mm(YP[:, c, :], core.ident[:], R[:, s % 4, d, c, :], start=(s == 0 and d == 0), stop=(s == DS - 1 and d == 1))
                    last.then_inc(S["summed"], 1)

                def prep(i, u, what, first, end):
                    use = USE[what]
                    bank = PR[:, use % 2, :]
                    kind, of = what[0], what[1:]
                    if first == 0:
                        at(pe, read(use), BANK_USES[use % 2] * i + use // 2)
                        if use == 1:
                            pe.wait_ge(read(0), BANK_USES[0] * i + 1)
                            at(pe, S["out_read"], i - 2)
                        if kind == "x":
                            pe.wait_ge(S["xn_ready"], i + 1)
                        if kind in ("dt", "bc"):
                            pe.wait_ge(S["silu_done"], DIRS * i + (of[0] + 1))
                    for k in range(first, end):
                        if kind == "x":
                            for t in range(G * TC):
                                last = nc.tensor.transpose(bank[:, t * P:(t + 1) * P], xn[:, t, :], core.ident[:])
                        if kind == "conv":
                            d, c = of
                            off = k if d == 0 else 2 * (DC - 1) - k
                            last = mm(bank, Wt["taps"][:, d, c, k, :], xT[:, :, off:off + T], start=(k == 0), stop=(k == DC - 1))
                        if kind == "z":
                            last = mm(bank, Wt["z"][:, of[0], :], xT[:, :, DC - 1:DC - 1 + T], start=True, stop=True)
                        if kind == "bc":
                            last = mm(bank[0:BC], Wt["bc"][:, of[0], k, :], xc[u][:, of[0], k, :], start=(k == 0), stop=(k == C2 - 1))
                        if kind == "dt":
                            d, c2 = of
                            last = mm(bank, Wt["dt"][:, d, k, c2, :], xc[u][:, d, k, :], start=(k == 0), stop=(k == C2 - 1))
                    if end == {"x": 1, "conv": DC, "z": 1, "bc": C2, "dt": C2}[kind]:
                        last.then_inc(S["prep_ps"], 1)

                def emit(i, u):
                    for s in range(DS):
                        if live(i, 1):
                            if s < DS - 1:
                                b_rows(i - 1, (u + 1) % 2, s + 1)
                            c_rows(i - 1, (u + 1) % 2, s)
                            if s > 0:
                                add_up(i - 1, s - 1)
                        if s == 0 and live(i, 2):
                            add_up(i - 2, DS - 1)
                        if live(i, 0):
                            for part in PREP_AT.get(s, ()):
                                prep(i, u, part[:-2], *part[-2:])
                        if s == 14 and live(i, 2):
                            j = i - 2
                            pe.wait_ge(S["gated"], j + 1)
                            if live(i, 0):
                                pe.wait_ge(read(1), BANK_USES[1] * (i + 1))
                            for k in range(G * TC):
                                for c in range(C2):
                                    last = mm(PR[:, 1, k * D:(k + 1) * D], yg[:, c, k * P:(k + 1) * P], Wt["out"][:, c, :], start=(c == 0), stop=(c == C2 - 1))
                            last.then_inc(S["out_ps"], 1)
                        if s == DS - 1 and live(i, 0):
                            b_rows(i, u, 0)
                rolled(pe, NP, 2, 3, emit, ring=2)

        s_back = core.sem("s_x_back")
        with nc.Block() as block:
            @block.sync
            def _(sp):
                sp.dma_start(core.X[:, 0:core.NT * D], xsave).then_inc(s_back, 16)
                sp.wait_ge(s_back, 16)


GRID = 8
KT = 4
KB = KT // TC
TURN = float(np.nextafter(np.float32(2 * np.pi), np.float32(0)))
MAGIC = 1.5 * 2.0 ** 23
NBASIS = 16
B_S1, B_C1, B_S2, B_D, B_DS1, B_DC1, B_DS2, B_E, B_ES1, B_EC1, B_ES2, B_ED, B_EDS1, B_EDC1, B_EDS2, B_EE = range(NBASIS)
COS, SIN = 0, 1
KAN_TERMS = {
    B_S1: (1.0, [(1, SIN, 1), (1, SIN, 3), (1, SIN, 5), (1, SIN, 7)]), B_DS1: (1.0, [(1, SIN, 3), (1, SIN, 5)]),
    B_ES1: (1.0, [(1, SIN, 5), (1, SIN, 7)]), B_EDS1: (1.0, [(1, SIN, 7)]),
    B_C1: (1.0, [(1, COS, 1), (-1, COS, 3), (1, COS, 5), (-1, COS, 7)]), B_DC1: (1.0, [(1, COS, 3), (-1, COS, 5)]),
    B_EC1: (1.0, [(1, COS, 5), (-1, COS, 7)]), B_EDC1: (1.0, [(1, COS, 7)]),
    B_S2: (2.0, [(1, SIN, 2), (1, SIN, 6)]), B_ES2: (2.0, [(1, SIN, 6)]), B_DS2: (2.0, [(1, SIN, 4)]), B_EDS2: (2.0, [(1, SIN, 8)]),
    B_D: (0.5, [(1, COS, 2), (-1, COS, 6)]), B_ED: (0.5, [(1, COS, 6)]), B_E: (0.5, [(1, COS, 4)]), B_EE: (0.5, [(1, COS, 8)]),
}


def kan_weights(core, WT, const):
    nc, aps = core.nc, core.aps
    tmp = ExitStack()
    with tmp:
        coef = core.sbuf("kw_coef", [P, 2, D * GRID], on=tmp)
        comb = core.sbuf("kw_combined", [P, NBASIS, D], on=tmp)
        minus2 = core.sbuf("kw_minus_two", [P, P], on=tmp)
        ps = core.psum("kw_ps", [P, NBASIS // 4 + 1, 512], on=tmp)
        s_in, s_comb, s_ps, s_wt, s_const = (core.sem(f"kw_{n}") for n in ("loaded", "combined", "ps", "kept", "const"))
        with nc.Block() as block:
            @block.sync
            def _(sp):
                sp.dma_start(coef[:], aps["L1_attn_kan_coef"].rearrange("p j i k -> j p (i k)")).then_inc(s_in, 16)

            @block.vector
            def _(dve):
                chain = Chain(core, dve, "kw_dve_chain")
                raw = lambda kind, k: coef[:, kind, :].rearrange("p (i k) -> p i k", k=GRID)[:, :, k - 1]
                nc.vector.memset(minus2[:], -2.0)
                dve.wait_ge(s_in, 16)
                depth = max(len(terms) for _, terms in KAN_TERMS.values())
                for n in range(depth):
                    for m, (factor, terms) in KAN_TERMS.items():
                        if n == 0:
                            last = nc.vector.tensor_scalar(comb[:, m, :], raw(*terms[0][1:]), factor, None, ALU.mult)
                        elif n < len(terms):
                            sign, kind, k = terms[n]
                            last = nc.vector.scalar_tensor_tensor(out=comb[:, m, :], in0=raw(kind, k), scalar=sign * factor, in1=comb[:, m, :],
                                                                  op0=ALU.mult, op1=ALU.add)
                    chain.step(last)
                nc.vector.tensor_copy(minus2[0:1, 0:1], minus2[0:1, 0:1]).then_inc(s_comb, 1)
                dve.wait_ge(s_ps, 1)
                nc.vector.tensor_copy(WT[:].rearrange("p m j -> p (m j)"), ps[:, 0:NBASIS // 4, :].rearrange("p m j -> p (m j)")).then_inc(s_wt, 1)
                dve.wait_ge(s_const, 1)
                chain.step(nc.vector.tensor_copy(const[:], ps[:, NBASIS // 4, 0:D]))

            @block.tensor
            def _(pe):
                pe.wait_ge(s_comb, 1)
                for m in range(NBASIS):
                    last = nc.tensor.transpose(ps[:, m // 4, (m % 4) * P:(m % 4 + 1) * P], comb[:, m, :], core.ident[:])
                last.then_inc(s_ps, 1)
                pe.wait_ge(s_wt, 1)
                nc.tensor.matmul(ps[:, NBASIS // 4, 0:D], minus2[:], WT[:, B_EE, :], start=True, stop=True).then_inc(s_const, 1)


def kan(core, Hr, OD):
    nc, NT, X, aps = core.nc, core.NT, core.X, core.aps
    NG, W4 = NT // KT, KT * P
    live = lambda i, lag: not isinstance(i, int) or 0 <= i - lag < NG
    on = ExitStack()
    with on:
        sb = lambda name, shape, dt=F32: core.sbuf("k_" + name, shape, dt, on=on)
        WT, const = sb("coef_T", [P, NBASIS, D]), sb("constant", [P, D])
        kan_weights(core, WT, const)
        ln = sb("ln_cols", [P, 2])
        quarter = sb("half_pi", [P, 1])
        od = [sb(f"od{n}", [P, KT, D]) for n in range(2)]
        xn = sb("xn", [P, KT, D])
        f, whole, t, at_ = sb("turns", [P, W4]), sb("whole", [P, W4]), sb("angle", [P, W4]), sb("abs_angle", [P, W4])
        q = sb("squares", [P, W4])
        basis = [sb(f"basis{n}", [P, NBASIS, W4]) for n in range(2)]
        gate = [sb(f"gate{n}", [P, KB, D]) for n in range(2)]
        hb, y1, y2 = (sb(n, [P, W4]) for n in ("h_const", "y_plus_h", "y_gated"))
        psT = core.psum("k_psT", [P, W4], on=on)
        psY = core.psum("k_psY", [P, 2, W4], on=on)
        S = {n: core.sem("k_" + n) for n in (
            "ln_loaded", "ln_ready", "od_loaded", "gate_loaded", "xn_ready", "xT_ps", "f_ready", "rounded", "reduced", "sin_done", "abs_done",
            "cos_done", "q_ready", "s2_done", "D_ready", "D_products", "D_square", "E_ready", "E_products", "E_square",
            "products", "hb_ready", "y1_ready", "gated", "x_updated", "passed")}
        with nc.Block() as block:
            @block.sync
            def _(sp):
                for n, name in enumerate(("g", "b")):
                    sp.dma_start(ln[:, n:n + 1], aps[f"L1_attn_ln_{name}"].rearrange("(p n) -> p n", n=1)).then_inc(S["ln_loaded"], 16)

                def emit(i, u):
                    if live(i, 0):
                        at_alone(sp, S["od_loaded"], 16 * i, S["passed"])
                        at(sp, S["xn_ready"], i - 1)
                        sp.dma_start(od[u][:], OD[ds(i * KT, KT)].rearrange("n p d -> p n d")).then_inc(S["od_loaded"], 16)
                        at(sp, S["gate_loaded"], 16 * i)
                        at(sp, S["gated"], i - 1)
                        sp.dma_start(gate[u][:], core.modrow[2, ds(i * KB, KB), :].partition_broadcast(P)).then_inc(S["gate_loaded"], 16)
                rolled(sp, NG, 1, 3, emit, ring=2)

            @block.vector
            def _(dve):
                tt, ts = nc.vector.tensor_tensor, nc.vector.tensor_scalar
                nc.vector.memset(quarter[:], float(np.pi / 2))
                dve.wait_ge(S["ln_loaded"], 32)
                ts(ln[:], ln[:], float(1 / (2 * np.pi)), None, ALU.mult).then_inc(S["ln_ready"], 1)

                def emit(i, u):
                    if live(i, 0):
                        bs = basis[u]
                        dve.wait_ge(S["od_loaded"], 16 * (i + 1))
                        at(dve, S["xT_ps"], i)
                        for k in range(KT):
                            c = i * KT + k
                            last = ts(xn[:, k, :], od[u][:, k, :], core.rstd[:, ds(c, 1)], core.nmr[:, ds(c, 1)], ALU.mult, ALU.add)
                        last.then_inc(S["xn_ready"], 1)
                        dve.wait_ge(S["f_ready"], i + 1)
                        ts(whole[:], f[:], MAGIC, MAGIC, ALU.add, ALU.subtract).then_inc(S["rounded"], 1)
                        dve.wait_ge(S["rounded"], i + 1)
                        tt(t[:], f[:], whole[:], ALU.subtract).then_inc(S["reduced"], 1)
                        dve.wait_ge(S["cos_done"], i + 1)
                        tt(bs[:, B_S2, :], bs[:, B_S1, :], bs[:, B_C1, :], ALU.mult).then_inc(S["s2_done"], 1)
                        dve.wait_ge(S["q_ready"], i + 1)
                        ts(bs[:, B_D, :], q[:], -2.0, 2.0, ALU.mult, ALU.add).then_inc(S["D_ready"], 1)
                        dve.wait_ge(S["s2_done"], i + 1)
                        dve.wait_ge(S["D_ready"], i + 1)
                        tt(bs[:, B_DS1:B_DS2 + 1, :], bs[:, B_S1:B_S2 + 1, :], bs[:, B_D, :].unsqueeze(1).broadcast_to([P, 3, W4]), ALU.mult)\
                            .then_inc(S["D_products"], 1)
                        dve.wait_ge(S["D_square"], i + 1)
                        ts(bs[:, B_E, :], q[:], -2.0, None, ALU.add).then_inc(S["E_ready"], 1)
                        dve.wait_ge(S["E_ready"], i + 1)
                        dve.wait_ge(S["D_products"], i + 1)
                        tt(bs[:, B_ES1:B_EDS2 + 1, :], bs[:, B_S1:B_DS2 + 1, :], bs[:, B_E, :].unsqueeze(1).broadcast_to([P, 7, W4]), ALU.mult)\
                            .then_inc(S["E_products"], 1)
                    if live(i, 1):
                        j = i - 1
                        dve.wait_ge(S["products"], j + 1)
                        dve.wait_ge(S["hb_ready"], j + 1)
                        at(dve, S["gated"], j)
                        tt(y1[:], psY[:, (u + 1) % 2, :], hb[:], ALU.add).then_inc(S["y1_ready"], 1)
                rolled(dve, NG, 1, 3, emit, ring=2)

            @block.scalar
            def _(act):
                func = nc.scalar.activation
                act.wait_ge(S["ln_ready"], 1)

                def emit(i, u):
                    if live(i, 0):
                        bs = basis[u]
                        act.wait_ge(S["xT_ps"], i + 1)
                        at(act, S["reduced"], i)
                        func(f[:], psT[:], ACT.Identity, scale=ln[:, 0:1], bias=ln[:, 1:2]).then_inc(S["f_ready"], 1)
                        act.wait_ge(S["reduced"], i + 1)
                        at(act, S["products"], i - 1)
                        func(bs[:, B_S1, :], t[:], ACT.Sin, scale=TURN).then_inc(S["sin_done"], 1)
                        at(act, S["cos_done"], i)
                        func(at_[:], t[:], ACT.Abs).then_inc(S["abs_done"], 1)
                        act.wait_ge(S["abs_done"], i + 1)
                        func(bs[:, B_C1, :], at_[:], ACT.Sin, scale=-TURN, bias=quarter[:, 0:1]).then_inc(S["cos_done"], 1)
                        act.wait_ge(S["sin_done"], i + 1)
                        at(act, S["E_ready"], i)
                        func(q[:], bs[:, B_S1, :], ACT.Square, scale=float(np.sqrt(2))).then_inc(S["q_ready"], 1)
                        act.wait_ge(S["D_ready"], i + 1)
                        func(q[:], bs[:, B_D, :], ACT.Square).then_inc(S["D_square"], 1)
                        act.wait_ge(S["E_ready"], i + 1)
                        func(bs[:, B_EE, :], bs[:, B_E, :], ACT.Square).then_inc(S["E_square"], 1)
                rolled(act, NG, 1, 3, emit, ring=2)

            @block.tensor
            def _(pe):
                def emit(i, u):
                    if live(i, 0):
                        pe.wait_ge(S["xn_ready"], i + 1)
                        at(pe, S["f_ready"], i)
                        for k in range(KT):
                            last = nc.tensor.transpose(psT[:, k * P:(k + 1) * P], xn[:, k, :], core.ident[:])
                        last.then_inc(S["xT_ps"], 1)
                    if live(i, 1):
                        j, n = i - 1, (u + 1) % 2
                        pe.wait_ge(S["E_products"], j + 1)
                        pe.wait_ge(S["E_square"], j + 1)
                        at(pe, S["y1_ready"], j - 1)
                        for k in range(KT):
                            for m in range(NBASIS):
                                last = nc.tensor.matmul(psY[:, n, k * D:(k + 1) * D], basis[n][:, m, k * P:(k + 1) * P], WT[:, m, :],
                                                        start=(m == 0), stop=(m == NBASIS - 1))
                        last.then_inc(S["products"], 1)
                rolled(pe, NG, 1, 3, emit, ring=2)

            @block.gpsimd
            def _(pool):
                tt = nc.gpsimd.tensor_tensor

                def emit(i, u):
                    if live(i, 1):
                        j, n = i - 1, (u + 1) % 2
                        at(pool, S["y1_ready"], j)
                        tt(hb[:].rearrange("p (n d) -> p n d", d=D), Hr[:, ds(j * W4, W4)].rearrange("p (n d) -> p n d", d=D),
                           const[:].unsqueeze(1).broadcast_to([P, KT, D]), ALU.add).then_inc(S["hb_ready"], 1)
                        pool.wait_ge(S["gate_loaded"], 16 * (j + 1))
                        pool.wait_ge(S["y1_ready"], j + 1)
                        at(pool, S["x_updated"], j)
                        tt(y2[:].rearrange("p (b n d) -> p b n d", b=KB, d=D), y1[:].rearrange("p (b n d) -> p b n d", b=KB, d=D),
                           gate[n][:].unsqueeze(2).broadcast_to([P, KB, TC, D]), ALU.mult).then_inc(S["gated"], 1)
                        pool.wait_ge(S["gated"], j + 1)
                        x = X[:, ds(j * W4, W4)]
                        tt(x, x, y2[:], ALU.add).then_inc(S["x_updated"], 1)
                rolled(pool, NG, 1, 3, emit, ring=2)


def layer1_attention(core):
    OD = core.nc.dram_tensor("mixer_out", [core.NT, P, D], F32, kind="Internal").ap()
    on = ExitStack()
    with on:
        Hr = core.sbuf("h_rows1", [P, core.NT * D], on=on)
        ln_stats(core, "lnC")
        modulated(core, 1, Hr, None, 8)
        ln_stats(core, "lnC1", Hr, 1e-12)
        mixer(core, Hr, OD)
        with core.nc.Block() as block:
            ln_finish(core, "lnC2", core.st, 1e-12, block)
        kan(core, Hr, OD)


def experts1(core, XS, YS):
    nc, aps = core.nc, core.aps
    on = ExitStack()
    with on:
        sb = lambda name, shape, dt=F32: core.sbuf("e1_" + name, shape, dt, on=on)
        w1, w2 = sb("w1", [P, E, F]), sb("w2", [P, E, FC, D])
        b1, b2 = sb("b1", [P, E, F]), sb("b2", [P, E, D])
        x = [sb(f"x{n}", [CAP, D]) for n in range(2)]
        xT = sb("xT", [P, CAP])
        h1, g = sb("h1", [CAP, F]), sb("gelu", [CAP, F])
        gT = sb("gelu_T", [P, FC, CAP])
        y = [sb(f"y{n}", [CAP, D]) for n in range(2)]
        psX, ps1, psY = (core.psum("e1_ps" + n, [P, 512], on=on) for n in "X1Y")
        psG = core.psum("e1_psG", [P, FC, P], on=on)
        S = start_counts(core, "e1", ["w_loaded", "x_loaded", "xT_ps", "xT_ready", "h1_ps", "h1_ready", "gelu_ready", "gT_ps", "gT_ready",
                                      "y_ps", "y_ready", "y_stored"])
        live = lambda i, lag: not isinstance(i, int) or 0 <= i - lag < E
        slots_of = lambda table, e: table[ds(e * CAP, CAP), :]
        of = lambda t, e: t[:, ds(e, 1)].rearrange("p n f -> p (n f)")

        with nc.Block() as block:
            @block.sync
            def _(sp):
                sp.dma_start(w1[:], aps["L1_ffn_w1"].rearrange("e d f -> d e f")).then_inc(S["w_loaded"], 16)
                sp.dma_start(b1[:], aps["L1_ffn_b1"].partition_broadcast(P)).then_inc(S["w_loaded"], 16)
                sp.dma_start(w2[:].rearrange("p e c d -> p (e c) d"), aps["L1_ffn_w2"].rearrange("e (c f) d -> f (e c) d", f=P)).then_inc(S["w_loaded"], 16)
                sp.dma_start(b2[:], aps["L1_ffn_b2"].partition_broadcast(P)).then_inc(S["w_loaded"], 16)

                def emit(i, u):
                    if live(i, 0):
                        upto(sp, S["x_loaded"], 16 * i)
                        upto(sp, S["xT_ps"], i - 1)
                        sp.dma_start(x[u][:], slots_of(XS, i)).then_inc(S["x_loaded"], 16)
                    if live(i, 1):
                        j = i - 1
                        upto(sp, S["y_ready"], j + 1)
                        upto(sp, S["y_stored"], 16 * j)
                        sp.dma_start(slots_of(YS, j), y[(u + 1) % 2][:]).then_inc(S["y_stored"], 16)
                rolled(sp, E, 1, 2, emit, ring=2)
                upto(sp, S["y_stored"], 16 * E)

            @block.tensor
            def _(pe):
                mm = nc.tensor.matmul
                upto(pe, S["w_loaded"], 64)

                def emit(i, u):
                    if live(i, 0):
                        upto(pe, S["x_loaded"], 16 * (i + 1))
                        upto(pe, S["xT_ready"], i)
                        nc.tensor.transpose(psX[:, 0:CAP], x[u][:], core.ident[0:CAP, 0:CAP]).then_inc(S["xT_ps"], 1)
                    if live(i, 1):
                        j = i - 1
                        upto(pe, S["gelu_ready"], j + 1)
                        upto(pe, S["gT_ready"], j)
                        for c in range(FC):
                            last = nc.tensor.transpose(psG[:, c, 0:CAP], g[:, c * P:(c + 1) * P], core.ident[0:CAP, 0:CAP])
                        last.then_inc(S["gT_ps"], 1)
                    if live(i, 0):
                        upto(pe, S["xT_ready"], i + 1)
                        upto(pe, S["h1_ready"], i)
                        mm(ps1[0:CAP, :], xT[:], of(w1, i), start=True, stop=True).then_inc(S["h1_ps"], 1)
                    if live(i, 1):
                        upto(pe, S["gT_ready"], j + 1)
                        upto(pe, S["y_ready"], j)
                        for c in range(FC):
                            last = mm(psY[0:CAP, 0:D], gT[:, c, :], w2[:, ds(j, 1), c, :].rearrange("p n d -> p (n d)"), start=(c == 0), stop=(c == FC - 1))
                        last.then_inc(S["y_ps"], 1)
                rolled(pe, E, 1, 2, emit, ring=2)

            @block.scalar
            def _(act):
                def emit(i, u):
                    if live(i, 1):
                        j = i - 1
                        upto(act, S["gT_ps"], j + 1)
                        upto(act, S["y_ps"], j)
                        nc.scalar.activation(gT[:], psG[:, :, 0:CAP], ACT.Copy).then_inc(S["gT_ready"], 1)
                    if live(i, 0):
                        upto(act, S["h1_ready"], i + 1)
                        upto(act, S["gT_ps"], i)
                        nc.scalar.activation(g[:], h1[:], ACT.Gelu_apprx_tanh).then_inc(S["gelu_ready"], 1)
                rolled(act, E, 1, 2, emit, ring=2)

            @block.vector
            def _(dve):
                upto(dve, S["w_loaded"], 64)

                def emit(i, u):
                    if live(i, 0):
                        upto(dve, S["xT_ps"], i + 1)
                        upto(dve, S["h1_ps"], i)
                        nc.vector.tensor_copy(xT[:], psX[:, 0:CAP]).then_inc(S["xT_ready"], 1)
                        upto(dve, S["h1_ps"], i + 1)
                        upto(dve, S["gelu_ready"], i)
                        nc.vector.tensor_tensor(h1[:], ps1[0:CAP, :], of(b1, i)[0:CAP], ALU.add).then_inc(S["h1_ready"], 1)
                    if live(i, 1):
                        j = i - 1
                        upto(dve, S["y_ps"], j + 1)
                        upto(dve, S["y_stored"], 16 * (j - 1))
                        nc.vector.tensor_tensor(y[(u + 1) % 2][:], psY[0:CAP, 0:D], of(b2, j)[0:CAP], ALU.add).then_inc(S["y_ready"], 1)
                rolled(dve, E, 1, 2, emit, ring=2)


def ffn1(core):
    nc, NT = core.nc, core.NT
    rows = E * CAP
    XS = nc.dram_tensor("slot_inputs1", [rows, D], F32, kind="Internal").ap()
    YS = nc.dram_tensor("slot_outputs1", [(rows // P + 1) * P, D], F32, kind="Internal").ap()
    on = ExitStack()
    with on:
        slots, weights = [core.sbuf("slots1", [P, NT], U32, on=on)], [core.sbuf("weights1", [P, NT], on=on)]
        scratch = ExitStack()
        with scratch:
            Hr = core.sbuf("h_rows2", [P, NT * D], on=scratch)
            L = core.sbuf("logits1", [P, NT * E], on=scratch)
            fill_zero(core, "xs1", XS, rows // P)
            fill_zero(core, "ys1", YS, rows // P + 1)
            ln_stats(core, "lnD")
            modulated(core, 1, Hr, L, 6)
            moe_route(core, 1, L, slots, weights)
            scatter_rows(core, "sc1", Hr, slots, XS, rows)
        experts1(core, XS, YS[0:rows, :])
        gather_and_add(core, "ga1", 1, slots, weights, YS)


def store_x(core):
    with core.nc.Block() as block:
        s_stored = core.sem("out_stored")

        @block.sync
        def _(sp):
            sp.dma_start(core.aps["out_tiles"].rearrange("n p d -> p n d"), core.X[:, 0:core.NT * D].rearrange("p (n d) -> p n d", d=D))\
                .then_inc(s_stored, 16)
            sp.wait_ge(s_stored, 16)


def adaln_two_layers(nc, aps, B):
    core = Core(nc, aps, B)
    with core.stack:
        load_and_modulate(core)
        ln_stats(core, "lnA")
        attention(core)
        ln_stats(core, "lnB")
        ffn0(core)
        core.next_stage()
        layer1_attention(core)
        core.next_stage()
        ffn1(core)
        store_x(core)


def shape_constants():
    out = {"ident": np.eye(P, dtype=np.float32)}
    inv_freq = (1.0 / (np.float32(10000.0) ** (np.arange(0, DH, 2, dtype=np.float32) / np.float32(DH)))).astype(np.float32)
    freqs = np.arange(T, dtype=np.float32)[:, None] * inv_freq[None, :]
    emb = np.concatenate([freqs, freqs], -1)
    out["rope_cos"] = np.tile(np.cos(emb).astype(np.float32).T, (H, 1))
    out["rope_sin"] = np.tile(np.sin(emb).astype(np.float32).T, (H, 1))
    rot = np.zeros((D, D), np.float32)
    for m in range(D):
        half = DH // 2
        rot[m + half if m % DH < half else m - half, m] = -1 if m % DH < half else 1
    out["rope_rot"] = rot
    out["selector"] = np.tile(np.eye(BC, dtype=np.float32), (PARTS, 1))
    out["rev_rank"] = np.tile(np.arange(E, 0, -1, dtype=np.float32), (P, 1))
    out["tri"] = np.triu(np.ones((P, P), np.float32))
    return out


def kernel(**inputs):
    import concourse.bacc as bacc
    from concourse.bass_utils import run_bass_kernel_spmd

    arrays = {name: np.ascontiguousarray(a) for name, a in inputs.items()}
    x = arrays.pop("L0_attn_x")
    B = x.shape[0]
    arrays["x_tiles"] = x.reshape(B * TC, P, D)
    arrays.update({name: np.ascontiguousarray(a) for name, a in shape_constants().items()})
    nc = bacc.Bacc("TRN2", target_bir_lowering=False, num_devices=1)
    aps = {name: nc.dram_tensor(name, a.shape, mybir.dt.from_np(a.dtype), kind="ExternalInput").ap() for name, a in arrays.items()}
    aps["out_tiles"] = nc.dram_tensor("out_tiles", [B * TC, P, D], F32, kind="ExternalOutput").ap()
    adaln_two_layers(nc, aps, B)
    r = run_bass_kernel_spmd(nc, [arrays], core_ids=[0])
    return np.asarray(r.results[0]["out_tiles"]).reshape(x.shape)
```

```python
import numpy as np

import concourse.bass as bass
from concourse import mybir
from contextlib import ExitStack

P = 128
F32 = mybir.dt.float32
BF16 = mybir.dt.bfloat16
U32 = mybir.dt.uint32
I32 = mybir.dt.int32
ALU = mybir.AluOpType
ACT = mybir.ActivationFunctionType
AX = mybir.AxisListType
ds = bass.ds

T, D = 256, 128
TC = T // P
SHIFT_A, SCALE_A, GATE_A, SHIFT_B, SCALE_B, GATE_B = range(6)
LN_EPS = 1e-5


def at(eng, sem, count):
    if isinstance(count, int) and count <= 0:
        return
    eng.wait_ge(sem, count)


def at_alone(eng, sem, count, passed):
    at(eng, sem, count)
    if not isinstance(count, int):
        eng.sem_inc(passed, 1)


class Core:

    def __init__(self, nc, aps, B):
        self.nc, self.aps, self.B = nc, aps, B
        self.NT = B * TC
        self.stack = ExitStack()
        self.sems = []
        self.X = self.sbuf("resid_x", [P, max(self.NT * D, 8192)])
        self.mod = self.sbuf("mod_cols", [P, 2 * 6 * B])
        self.ident = self.sbuf("identity", [P, P])
        self.rstd = self.sbuf("rstd", [P, self.NT])
        self.nmr = self.sbuf("neg_mean_rstd", [P, self.NT])
        self.st = self.sbuf("bn_stats", [P, self.NT, 6])
        self.ln_tmp = [self.sbuf(f"ln_{n}", [P, self.NT]) for n in ("mean", "dmean", "var", "std")]
        self.modrow = nc.dram_tensor("mod_rows", [10, B, D], F32, kind="Internal").ap()

    def sbuf(self, name, shape, dt=F32, on=None):
        return (on or self.stack).enter_context(self.nc.sbuf_tensor(name, shape, dt))

    def psum(self, name, shape, dt=F32, on=None):
        return (on or self.stack).enter_context(self.nc.psum_tensor(name, shape, dt))

    def sem(self, name):
        self.sems.append(self.nc.alloc_semaphore(name=name))
        return self.sems[-1]

    def next_stage(self):
        self.nc.all_engine_barrier()
        self.nc.clear_and_free_semaphores(self.sems)
        self.nc.all_engine_barrier()
        self.sems = []

    def modcol(self, layer, kind, b):
        o = (layer * 6 + kind) * self.B
        return self.mod[:, ds(b + o, 1)]


class Chain:

    def __init__(self, core, eng, name):
        self.eng, self.sem, self.n = eng, core.sem(name), 0

    def step(self, ins):
        ins.then_inc(self.sem, 1)
        self.n += 1
        self.eng.wait_ge(self.sem, self.n)


def load_and_modulate(core):
    nc, B, aps = core.nc, core.B, core.aps
    on = ExitStack()
    with on:
        c = core.sbuf("c_rows", [2 * B, D], on=on)
        cs = core.sbuf("c_silu", [2 * B, D], on=on)
        cT = core.sbuf("c_silu_T", [P, 2 * B], on=on)
        w = core.sbuf("wmod", [P, 2, 6 * D], on=on)
        rows = core.sbuf("mod_rows_sb", [B, 10, D], on=on)
        sgn = core.sbuf("gate_sign", [P, 4 * D], on=on)
        psT = core.psum("m_psT", [P, 512], on=on)
        psC = core.psum("m_psC", [P, 512], on=on)
        psR = core.psum("m_psR", [P, 3, 512], on=on)
        LOTS = 4
        lot = core.NT // LOTS
        s_x = [core.sem(f"x_loaded{k}") for k in range(LOTS)]
        s_stats, s_in, s_silu = core.sem("x_stats"), core.sem("mod_in_loaded"), core.sem("c_silu_ready")
        s_T, s_cT, s_mm, s_rows, s_out = core.sem("cT_ps"), core.sem("cT_ready"), core.sem("mod_ps"), core.sem("modrows_ready"), core.sem("modrows_stored")
        with nc.Block() as block:
            @block.sync
            def _(sp):
                for l, (cn, wn) in enumerate((("L0_c", "L0_wmod"), ("L1_c", "L1_wmod"))):
                    sp.dma_start(c[l * B:(l + 1) * B, :], aps[cn][0:B]).then_inc(s_in, 16)
                    sp.dma_start(w[:, l, :], aps[wn]).then_inc(s_in, 16)
                sp.dma_start(core.ident[:], aps["ident"]).then_inc(s_in, 16)
                for k in range(LOTS):
                    sp.dma_start(core.X[:, k * lot * D:(k + 1) * lot * D].rearrange("p (n d) -> p n d", d=D),
                                 aps["x_tiles"][k * lot:(k + 1) * lot].rearrange("n p d -> p n d")).then_inc(s_x[k], 16)
                sp.wait_ge(s_rows, 1)
                sp.dma_start(core.modrow.rearrange("k b d -> b k d"), rows[:]).then_inc(s_out, 16)
                sp.wait_ge(s_out, 16)

            @block.scalar
            def _(act):
                act.wait_ge(s_in, 80)
                nc.scalar.activation(cs[:], c[:], ACT.Silu).then_inc(s_silu, 1)

            @block.tensor
            def _(pe):
                pe.wait_ge(s_silu, 1)
                nc.tensor.transpose(psT[:, 0:2 * B], cs[:], core.ident[0:2 * B, 0:2 * B]).then_inc(s_T, 1)
                pe.wait_ge(s_cT, 1)
                for l in range(2):
                    for k in range(6):
                        o = (l * 6 + k) * B
                        nc.tensor.matmul(psC[:, o:o + B], w[:, l, k * D:(k + 1) * D], cT[:, l * B:(l + 1) * B],
                                         start=True, stop=True)
                for n, (l, k) in enumerate(((0, GATE_A), (0, GATE_B), (1, GATE_A), (1, GATE_B), (0, SHIFT_B), (0, SCALE_B), (1, SHIFT_B), (1, SCALE_B),
                                             (1, SHIFT_A), (1, SCALE_A))):
                    last = nc.tensor.matmul(psR[0:B, n // 4, (n % 4) * D:(n % 4 + 1) * D], cT[:, l * B:(l + 1) * B],
                                            w[:, l, k * D:(k + 1) * D], start=True, stop=True)
                last.then_inc(s_mm, 1)

            @block.vector
            def _(dve):
                chain = Chain(core, dve, "mod_dve_chain")
                dve.wait_ge(s_T, 1)
                nc.vector.tensor_copy(cT[:], psT[:, 0:2 * B]).then_inc(s_cT, 1)
                dve.wait_ge(s_mm, 1)
                chain.step(nc.vector.tensor_copy(core.mod[:], psC[:, 0:12 * B]))
                for l in range(2):
                    for k in (SCALE_A, SCALE_B):
                        o = (l * 6 + k) * B
                        nc.vector.tensor_scalar(core.mod[:, o:o + B], core.mod[:, o:o + B], 1.0, None, ALU.add)
                chain.step(nc.vector.tensor_scalar(sgn[0:B, :], psR[0:B, 0, :], 0.0, None, ALU.is_ge))
                chain.step(nc.vector.tensor_scalar(sgn[0:B, :], sgn[0:B, :], 2.0, -1.0, ALU.mult, ALU.add))
                for k in range(3):
                    pair = psR[0:B, 1 + k // 2, (k % 2) * 2 * D:(k % 2 + 1) * 2 * D]
                    nc.vector.tensor_copy(rows[:, 4 + 2 * k, :], pair[:, 0:D])
                    nc.vector.tensor_scalar(rows[:, 5 + 2 * k, :], pair[:, D:2 * D], 1.0, None, ALU.add)
                gates = rows[:, 0:4, :].rearrange("b k d -> b (k d)")
                chain.step(nc.vector.tensor_copy(gates, psR[0:B, 0, :]))
                chain.step(nc.vector.scalar_tensor_tensor(out=gates, in0=gates, scalar=-1.0, in1=gates,
                                                          op0=ALU.mult, op1=ALU.max))
                chain.step(nc.vector.tensor_scalar(gates, gates, 0.25, None, ALU.max))
                nc.vector.tensor_tensor(gates, gates, sgn[0:B, :], ALU.mult).then_inc(s_rows, 1)
                for k in range(LOTS):
                    dve.wait_ge(s_x[k], 16)
                    for t in range(k * lot, (k + 1) * lot):
                        last = nc.vector.bn_stats(core.st[:, t, :], core.X[:, t * D:(t + 1) * D])
                last.then_inc(s_stats, 1)
                dve.wait_ge(s_stats, 1)


def ln_finish(core, tag, st, eps, block):
    nc = core.nc
    m, dm, v, sd = core.ln_tmp
    s_v, s_sd = core.sem(f"{tag}_var_ready"), core.sem(f"{tag}_std_ready")

    @block.vector
    def _(dve):
        chain = Chain(core, dve, f"{tag}_dve_chain")
        chain.step(nc.vector.tensor_tensor(m[:], st[:, :, 1], st[:, :, 4], ALU.add))
        nc.vector.tensor_tensor(dm[:], st[:, :, 1], st[:, :, 4], ALU.subtract)
        chain.step(nc.vector.tensor_tensor(v[:], st[:, :, 2], st[:, :, 5], ALU.add))
        chain.step(nc.vector.tensor_tensor(dm[:], dm[:], dm[:], ALU.mult))
        chain.step(nc.vector.tensor_scalar(dm[:], dm[:], 0.25, eps, ALU.mult, ALU.add))
        nc.vector.scalar_tensor_tensor(out=v[:], in0=v[:], scalar=1.0 / D, in1=dm[:],
                                       op0=ALU.mult, op1=ALU.add).then_inc(s_v, 1)
        dve.wait_ge(s_sd, 1)
        chain.step(nc.vector.reciprocal(core.rstd[:], sd[:]))
        chain.step(nc.vector.scalar_tensor_tensor(out=core.nmr[:], in0=m[:], scalar=-0.5, in1=core.rstd[:],
                                                  op0=ALU.mult, op1=ALU.mult))

    @block.scalar
    def _(act):
        act.wait_ge(s_v, 1)
        nc.scalar.activation(sd[:], v[:], ACT.Sqrt).then_inc(s_sd, 1)


def tile_stats(core, src, tile):
    return core.nc.vector.bn_stats(core.st[:, ds(tile, 1), :].rearrange("p n k -> p (n k)"), src[:, ds(tile * D, D)])


def norm_stats(core, tag, eps=LN_EPS):
    with core.nc.Block() as block:
        ln_finish(core, tag, core.st, eps, block)
H, DH = 16, 8
HQ = 4
PARTS = 3
KROWS = PARTS * PARTS * DH
RING = 4
PAIRS = H // 2
MAXHEADS = (2, 4, 0, 4, 2, 4, 0, 0)
MAXFROM = [sum(MAXHEADS[:p]) for p in range(PAIRS)]


def pair_heads(p):
    r, q = p // 2, 2 * (p % 2)
    return [HQ * q + r, HQ * (q + 1) + r]


def rolled(eng, n, lag, first, emit, ring=RING):
    turns = max(0, (n - first) // ring)
    for i in range(first):
        emit(i, i % ring)
    if turns:
        with eng.Fori(0, turns) as turn:
            for u in range(ring):
                emit(turn * ring + (first + u), (first + u) % ring)
    for i in range(first + turns * ring, n + lag):
        emit(i, i % ring)


def attention(core):
    nc, B, X, aps = core.nc, core.B, core.X, core.aps
    SCALE = float(DH) ** -0.5
    live = lambda i, lag: not isinstance(i, int) or 0 <= i - lag < B
    MAX, SCORES, LAG = 2, 3, 4
    on = ExitStack()
    with on:
        sb = lambda name, shape, dt=F32: core.sbuf("a_" + name, shape, dt, on=on)
        w_dk, w_dv, w_uk, w_uv, w_o, rot = (sb(n, [P, D]) for n in ("w_dk", "w_dv", "w_uk", "w_uv", "w_o", "rot"))
        bias = sb("bias_cols", [P, 4])
        bo = sb("bias_out", [P, TC * D])
        bo_row = sb("bias_out_row", [1, D])
        bo_in = sb("b_o_row", [1, D])
        ones1 = sb("ones_row", [1, P])
        cos, sin = sb("cos", [P, 2 * T]), sb("sin", [P, 2 * T])
        xn = sb("xn", [P, TC, D])
        qk = sb("qk", [P, 2, T])
        ckv = sb("ckv", [P, 2, T])
        qcos, qsin = sb("qk_cos", [P, 2 * T]), sb("qk_sin", [P, 2 * T])
        roped, left = sb("roped", [P, 2 * T]), sb("left", [P, 2 * T])
        parts = sb("parts", [P, PARTS, 2, T], BF16)
        Q9 = [sb(f"Q9_{n}", [KROWS + 2, H, T], BF16) for n in range(RING)]
        K9 = [sb(f"K9_{n}", [KROWS + 2, H, T], BF16) for n in range(RING)]
        V = [sb(f"V_{n}", [P, TC, HQ, HQ, 32]) for n in range(RING)]
        ones = sb("ones_pad", [P, HQ, 32])
        mx = sb("row_max", [P, H, TC])
        mhi, mlo = sb("max_hi", [2 * H, P], BF16), sb("max_lo", [2 * H, P], BF16)
        PT = sb("probs", [P, 4, 2, TC, T])
        rden, oT = sb("rden", [P, T]), sb("oT", [P, T])
        ga = sb("gate_rows", [P, D])
        minus = sb("minus_one", [2, H * T], BF16)
        y1, y2 = sb("y1", [P, TC * D]), sb("y2", [P, TC * D])
        ST = core.psum("a_scores", [P, 2, 2, TC, T], on=on)
        MX = core.psum("a_maxscores", [P, 2, TC, T], on=on)
        O = core.psum("a_out", [P, 2, T], on=on)
        PP = core.psum("a_proj", [P, 512], on=on)
        split = [nc.dram_tensor(f"split_qk_{n}", [P, PARTS, 2, T], BF16, kind="Internal").ap() for n in range(RING)]

        S = {n: core.sem("a_" + n) for n in (
            "w_loaded", "const_ready", "mrow_const", "bo_ps", "bo_row", "bo_ready", "gate_loaded", "xn_ready", "hT_ps", "hT_ready", "ckv_ps",
            "ckv_ready", "kv_ps", "k_ready", "v_ready", "rot_ps", "cos_done", "sin_done", "roped_ready", "part0",
            "left1", "part1", "part2", "stored", "loaded", "batch_loaded", "max_ps", "max_done", "maxT_ps", "max_hi", "max_lo",
            "max_rows", "scores_ps", "exp_done", "av_done", "rden_ready", "oT_ready", "y_ps", "y_biased",
            "y_gated", "x_updated", "stats", "passed")}

        with nc.Block() as block:
            @block.sync
            def _(sp):
                for t, n in ((w_dk, "L0_attn_w_dk"), (w_dv, "L0_attn_w_dv"), (w_uk, "L0_attn_w_uk"), (w_uv, "L0_attn_w_uv"),
                             (w_o, "L0_attn_w_o"), (rot, "rope_rot")):
                    sp.dma_start(t[:], aps[n]).then_inc(S["w_loaded"], 16)
                for k, n in enumerate(("L0_attn_b_dk", "L0_attn_b_dv", "L0_attn_b_uk", "L0_attn_b_uv")):
                    sp.dma_start(bias[:, k:k + 1], aps[n].rearrange("(p n) -> p n", n=1)).then_inc(S["w_loaded"], 16)
                sp.dma_start(bo_in[:], aps["L0_attn_b_o"].rearrange("(n d) -> n d", n=1)).then_inc(S["w_loaded"], 16)
                for t, n in ((cos, "rope_cos"), (sin, "rope_sin")):
                    for k in range(2):
                        sp.dma_start(t[:, k * T:(k + 1) * T], aps[n]).then_inc(S["w_loaded"], 16)
                sp.wait_ge(S["const_ready"], 1)
                for n in range(RING):
                    sp.dma_start(K9[n][KROWS:KROWS + 2, :, :], minus[:].rearrange("p (h t) -> p h t", t=T)).then_inc(S["mrow_const"], 16)

                def emit(i, u):
                    if live(i, 1):
                        sp.wait_ge(S["loaded"], 16 * 2 * PARTS * PARTS * i)
                        sp.sem_inc(S["batch_loaded"], 1)
                    if live(i, LAG):
                        at(sp, S["y_gated"], i - LAG)
                        sp.dma_start(ga[:], core.modrow[0, ds(i - LAG, 1), :].rearrange("n d -> (n d)").partition_broadcast(P)).then_inc(S["gate_loaded"], 16)
                    if live(i, MAX):
                        n = (u - MAX) % RING
                        at_alone(sp, S["max_lo"], i - MAX + 1, S["passed"])
                        at(sp, S["scores_ps"], PAIRS * (i - MAX - RING + 1))
                        for k, m in enumerate((mhi, mlo)):
                            sp.dma_start(Q9[n][KROWS + k:KROWS + k + 1, :, :], m[:]).then_inc(S["max_rows"], 16)
                    if live(i, 0):
                        sp.wait_ge(S["part2"], i + 1)
                        sp.dma_start(split[u], parts[:]).then_inc(S["stored"], 16)
                        at_alone(sp, S["stored"], 16 * (i + 1), S["passed"])
                        at(sp, S["scores_ps"], PAIRS * (i - RING + 1))
                        view = split[u].rearrange("(h e) a w t -> a w e h t", e=DH)
                        for a in range(PARTS):
                            for b in range(PARTS):
                                row = (a * PARTS + b) * DH
                                sp.dma_start(Q9[u][row:row + DH, :, :], view[a, 0]).then_inc(S["loaded"], 16)
                                sp.dma_start(K9[u][row:row + DH, :, :], view[b, 1]).then_inc(S["loaded"], 16)
                rolled(sp, B, LAG, 6, emit)

            @block.gpsimd
            def _(pool):
                nc.gpsimd.memset(ones[:], 0.0)
                for n in range(RING):
                    last = nc.gpsimd.memset(V[n][:], 0.0)
                last.then_inc(S["bo_row"], 1)
                pool.wait_ge(S["bo_row"], 1)
                for r in range(HQ):
                    nc.gpsimd.memset(ones[:, r, r * DH:(r + 1) * DH], 1.0)
                nc.gpsimd.memset(minus[:], -1.0)
                nc.gpsimd.memset(ones1[:], 1.0).then_inc(S["const_ready"], 1)
                pool.wait_ge(S["w_loaded"], 15 * 16)
                pool.wait_ge(S["bo_ready"], 1)

                def emit(i, u):
                    if live(i, 0):
                        pool.wait_ge(S["k_ready"], i + 1)
                        at(pool, S["roped_ready"], i)
                        nc.gpsimd.tensor_tensor(qcos[:], qk[:].rearrange("p a t -> p (a t)"), cos[:], ALU.mult).then_inc(S["cos_done"], 1)
                    if live(i, LAG):
                        b = i - LAG
                        pool.wait_ge(S["y_biased"], b + 1)
                        pool.wait_ge(S["gate_loaded"], 16 * (b + 1))
                        at(pool, S["x_updated"], b)
                        g = ga[:].unsqueeze(1).broadcast_to([P, TC, D])
                        nc.gpsimd.tensor_tensor(y2[:].rearrange("p (n d) -> p n d", d=D), y1[:].rearrange("p (n d) -> p n d", d=D), g,
                                                ALU.mult).then_inc(S["y_gated"], 1)
                        pool.wait_ge(S["y_gated"], b + 1)
                        x = X[:, ds(b * (TC * D), TC * D)]
                        nc.gpsimd.tensor_tensor(x, x, y2[:], ALU.add).then_inc(S["x_updated"], 1)
                rolled(pool, B, LAG, 6, emit)

            @block.scalar
            def _(act):
                act.wait_ge(S["w_loaded"], 15 * 16)

                def emit(i, u):
                    for p in range(PAIRS):
                        if live(i, SCORES):
                            act.wait_ge(S["scores_ps"], PAIRS * (i - SCORES) + p + 1)
                            at(act, S["av_done"], 4 * (i - SCORES) + p // 2 - 1)
                            nc.scalar.activation(PT[:, p % 4].rearrange("p a b t -> p (a b t)"), ST[:, p % 2].rearrange("p a b t -> p (a b t)"),
                                                 ACT.Exp, scale=SCALE).then_inc(S["exp_done"], 1)
                        if p == 1 and live(i, 0):
                            act.wait_ge(S["hT_ps"], i + 1)
                            at(act, S["rot_ps"], i)
                            at(act, S["cos_done"], i)
                            nc.scalar.activation(qk[:, 0, :], PP[:, 0:T], ACT.Identity, scale=core.modcol(0, SCALE_A, i),
                                                 bias=core.modcol(0, SHIFT_A, i)).then_inc(S["hT_ready"], 1)
                        if p == 2 and live(i, 0):
                            act.wait_ge(S["ckv_ps"], i + 1)
                            at(act, S["kv_ps"], i)
                            for k in range(2):
                                last = nc.scalar.activation(ckv[:, k, :], PP[:, k * T:(k + 1) * T], ACT.Identity, bias=bias[:, k:k + 1])
                            last.then_inc(S["ckv_ready"], 1)
                        if p == 3 and live(i, 0):
                            act.wait_ge(S["v_ready"], i + 1)
                            nc.scalar.activation(qk[:, 1, :], PP[:, 0:T], ACT.Identity, bias=bias[:, 2:3]).then_inc(S["k_ready"], 1)
                        if p == 6 and live(i, 0):
                            act.wait_ge(S["roped_ready"], i + 1)
                            at(act, S["stored"], 16 * i)
                            nc.scalar.activation(parts[:, 0].rearrange("p a t -> p (a t)"), roped[:], ACT.Copy).then_inc(S["part0"], 1)
                            act.wait_ge(S["left1"], i + 1)
                            nc.scalar.activation(parts[:, 1].rearrange("p a t -> p (a t)"), left[:], ACT.Copy).then_inc(S["part1"], 1)
                rolled(act, B, LAG, 6, emit)

            @block.vector
            def _(dve):
                dve.wait_ge(S["bo_ps"], 1)
                nc.vector.tensor_tensor(bo_row[:], PP[0:1, 0:D], bo_in[:], ALU.add).then_inc(S["bo_ready"], 1)
                dve.wait_ge(S["bo_ps"], 2)
                for k in range(TC):
                    last = nc.vector.tensor_copy(bo[:, k * D:(k + 1) * D], PP[:, D:2 * D])
                last.then_inc(S["bo_ready"], 1)
                dve.wait_ge(S["bo_ready"], 2)

                def new_stats(b):
                    dve.wait_ge(S["x_updated"], b + 1)
                    for k in range(TC):
                        last = tile_stats(core, X, b * TC + k)
                    last.then_inc(S["stats"], 1)

                def emit(i, u):
                    for p in range(PAIRS):
                        if p == 1 and live(i, LAG + 1):
                            new_stats(i - LAG - 1)
                        if p == 0 and live(i, 0):
                            at(dve, S["hT_ps"], i)
                            for k in range(TC):
                                c = 2 * i + k
                                last = nc.vector.tensor_scalar(xn[:, k, :], X[:, ds(i * (TC * D) + k * D, D)], core.rstd[:, ds(c, 1)],
                                                               core.nmr[:, ds(c, 1)], ALU.mult, ALU.add)
                            last.then_inc(S["xn_ready"], 1)
                        if p == 2 and live(i, LAG):
                            b = i - LAG
                            dve.wait_ge(S["av_done"], 4 * (b + 1))
                            nc.vector.reciprocal(rden[:], O[:, 1, :]).then_inc(S["rden_ready"], 1)
                            dve.wait_ge(S["rden_ready"], b + 1)
                            at(dve, S["y_ps"], b)
                            nc.vector.tensor_tensor(oT[:], O[:, 0, :], rden[:], ALU.mult).then_inc(S["oT_ready"], 1)
                        if live(i, MAX):
                            b = i - MAX
                            for h in range(MAXFROM[p], MAXFROM[p] + MAXHEADS[p]):
                                dve.wait_ge(S["max_ps"], H * b + h + 1)
                                if h == 0:
                                    at(dve, S["maxT_ps"], b)
                                nc.vector.tensor_reduce(mx[:, h, :], MX[:, h % 2], AX.X, ALU.max).then_inc(S["max_done"], 1)
                        if p == 3 and live(i, 0):
                            dve.wait_ge(S["kv_ps"], i + 1)
                            at(dve, S["av_done"], 4 * (i - RING + 1))
                            for k in range(TC):
                                v = V[u][:, k]
                                heads = bass.AP(tensor=v.tensor, offset=v.offset, ap=[list(v.ap[0]), [HQ * 32, HQ], [32 + DH, HQ], [1, DH]])
                                last = nc.vector.tensor_copy(heads, PP[:, T + k * D:T + (k + 1) * D].rearrange("p (q r e) -> p q r e", q=HQ, r=HQ))
                            last.then_inc(S["v_ready"], 1)
                        if p == 5 and live(i, 0):
                            dve.wait_ge(S["rot_ps"], i + 1)
                            nc.vector.tensor_tensor(qsin[:], PP[:], sin[:], ALU.mult).then_inc(S["sin_done"], 1)
                            dve.wait_ge(S["sin_done"], i + 1)
                            dve.wait_ge(S["cos_done"], i + 1)
                            nc.vector.tensor_tensor(roped[:], qcos[:], qsin[:], ALU.add).then_inc(S["roped_ready"], 1)
                        if p == 7 and live(i, LAG):
                            b = i - LAG
                            dve.wait_ge(S["y_ps"], b + 1)
                            at(dve, S["y_gated"], b)
                            nc.vector.tensor_tensor(y1[:], PP[:, 0:TC * D], bo[:], ALU.add).then_inc(S["y_biased"], 1)
                        if p == 6 and live(i, 0):
                            dve.wait_ge(S["part0"], i + 1)
                            nc.vector.tensor_tensor(left[:], roped[:], parts[:, 0].rearrange("p a t -> p (a t)"), ALU.subtract).then_inc(S["left1"], 1)
                        if p == 6 and live(i, MAX):
                            b = i - MAX
                            dve.wait_ge(S["maxT_ps"], b + 1)
                            at(dve, S["max_rows"], 32 * b)
                            nc.vector.tensor_copy(mhi[:], PP[0:2 * H, 0:P]).then_inc(S["max_hi"], 1)
                            dve.wait_ge(S["max_hi"], b + 1)
                            nc.vector.tensor_tensor(mlo[:], PP[0:2 * H, 0:P], mhi[:], ALU.subtract).then_inc(S["max_lo"], 1)
                        if p == 7 and live(i, 0):
                            dve.wait_ge(S["part1"], i + 1)
                            nc.vector.tensor_tensor(parts[:, 2].rearrange("p a t -> p (a t)"), left[:], parts[:, 1].rearrange("p a t -> p (a t)"),
                                                    ALU.subtract).then_inc(S["part2"], 1)
                rolled(dve, B, LAG, 6, emit)
                new_stats(B - 1)
                dve.wait_ge(S["stats"], B)

            @block.tensor
            def _(pe):
                mm = nc.tensor.matmul
                pe.wait_ge(S["w_loaded"], 15 * 16)
                pe.wait_ge(S["const_ready"], 1)
                pe.wait_ge(S["mrow_const"], 16 * RING)
                mm(PP[0:1, 0:D], bias[:, 3:4], w_o[:], start=True, stop=True).then_inc(S["bo_ps"], 1)
                pe.wait_ge(S["bo_ready"], 1)
                mm(PP[:, D:2 * D], ones1[:], bo_row[:], start=True, stop=True).then_inc(S["bo_ps"], 1)
                pe.wait_ge(S["bo_ready"], 2)

                def values(b, u, g, k):
                    if k == 0:
                        pe.wait_ge(S["exp_done"], PAIRS * b + 2 * g + 2)
                        if g == 0:
                            at(pe, S["oT_ready"], b)
                    for kind in range(2):
                        for q in range(HQ):
                            w = V[u][:, k, q, g, :] if kind == 0 else ones[:, g, :]
                            pr = PT[:, (2 * g + q // 2) % 4, q % 2, k, :]
                            last = mm(O[32 * q:32 * q + 32, kind, :], w, pr, start=(g == 0 and k == 0 and kind == 0),
                                      stop=(g == 3 and k == TC - 1 and kind == 1), skip_group_check=True)
                    if k == TC - 1:
                        last.then_inc(S["av_done"], 1)

                def values_at(i, u, p, k):
                    if p == 1 and live(i, LAG):
                        values(i - LAG, u, 3, k)
                    if p % 2 == 1 and p >= 3 and live(i, SCORES):
                        if p == 3 and k == 0:
                            pe.wait_ge(S["v_ready"], i - SCORES + 1)
                        values(i - SCORES, (u - SCORES) % RING, p // 2 - 1, k)

                def max_scores(i, u, heads):
                    b, n = i - MAX, (u - MAX) % RING
                    for h in heads:
                        if h == 0:
                            pe.wait_ge(S["batch_loaded"], b + 1)
                        at(pe, S["max_done"], H * b + h - 1)
                        for k in range(TC):
                            last = mm(MX[:, h % 2, k, :], Q9[n][0:KROWS, h, k * P:(k + 1) * P], K9[n][0:KROWS, h, :], start=True, stop=True)
                        last.then_inc(S["max_ps"], 1)

                def emit(i, u):
                    for p in range(PAIRS):
                        heads = range(MAXFROM[p], MAXFROM[p] + MAXHEADS[p])
                        if live(i, MAX):
                            max_scores(i, u, heads[:2])
                        if live(i, SCORES):
                            b, n = i - SCORES, (u - SCORES) % RING
                            if p == 0:
                                pe.wait_ge(S["max_rows"], 32 * (b + 1))
                            at(pe, S["exp_done"], PAIRS * b + p - 1)
                            for j, h in enumerate(pair_heads(p)):
                                for k in range(TC):
                                    last = mm(ST[:, p % 2, j, k, :], K9[n][:, h, k * P:(k + 1) * P], Q9[n][:, h, :], start=True, stop=True)
                            last.then_inc(S["scores_ps"], 1)
                        values_at(i, u, p, 0)
                        if p == 1 and live(i, 0):
                            pe.wait_ge(S["xn_ready"], i + 1)
                            at(pe, S["max_lo"], i - MAX)
                            at(pe, S["y_biased"], i - LAG)
                            for k in range(TC):
                                last = nc.tensor.transpose(PP[:, k * P:(k + 1) * P], xn[:, k, :], core.ident[:])
                            last.then_inc(S["hT_ps"], 1)
                        if p == 2 and live(i, 0):
                            pe.wait_ge(S["hT_ready"], i + 1)
                            mm(PP[:, 0:T], w_dk[:], qk[:, 0, :], start=True, stop=True)
                            mm(PP[:, T:2 * T], w_dv[:], qk[:, 0, :], start=True, stop=True).then_inc(S["ckv_ps"], 1)
                        if p == 3 and live(i, 0):
                            pe.wait_ge(S["ckv_ready"], i + 1)
                            mm(PP[:, 0:T], w_uk[:], ckv[:, 0, :], start=True, stop=True)
                            for k in range(TC):
                                last = mm(PP[:, T + k * D:T + (k + 1) * D], ckv[:, 1, k * P:(k + 1) * P], w_uv[:], start=True, stop=True)
                            last.then_inc(S["kv_ps"], 1)
                        if p == 4 and live(i, 0):
                            pe.wait_ge(S["k_ready"], i + 1)
                            pe.wait_ge(S["v_ready"], i + 1)
                            mm(PP[:], rot[:], qk[:].rearrange("p a t -> p (a t)"), start=True, stop=True).then_inc(S["rot_ps"], 1)
                        if live(i, MAX):
                            max_scores(i, u, heads[2:])
                        values_at(i, u, p, 1)
                        if p == 6 and live(i, MAX):
                            b = i - MAX
                            pe.wait_ge(S["max_done"], H * (b + 1))
                            if live(i, 0):
                                pe.wait_ge(S["sin_done"], i + 1)
                            else:
                                at(pe, S["y_biased"], i - LAG)
                            nc.tensor.transpose(PP[0:2 * H, 0:P], mx[:].rearrange("p h k -> p (h k)"), core.ident[:]).then_inc(S["maxT_ps"], 1)
                        if p == 7 and live(i, LAG):
                            b = i - LAG
                            if live(i, MAX):
                                pe.wait_ge(S["max_lo"], i - MAX + 1)
                            else:
                                pe.wait_ge(S["y_biased"], b)
                            pe.wait_ge(S["oT_ready"], b + 1)
                            for k in range(TC):
                                last = mm(PP[:, k * D:(k + 1) * D], oT[:, k * P:(k + 1) * P], w_o[:], start=True, stop=True)
                            last.then_inc(S["y_ps"], 1)
                rolled(pe, B, LAG, 6, emit)
E, F = 8, 512
FC = F // P
STAGES = 4
CAP = 80


def start_counts(core, tag, names):
    S = {n: core.sem(f"{tag}_{n}") for n in names}
    with core.nc.Block() as block:
        @block.sync
        def _(sp):
            for n in names:
                sp.sem_inc(S[n], 1)
    return S


def upto(eng, sem, count):
    if isinstance(count, int) and count < 0:
        return
    eng.wait_ge(sem, count + 1)


class Ahead:

    def __init__(self, core, tag, loads=(), fills=(), on=None):
        nc = core.nc
        self.loaded, self.zeroed = core.sem(f"{tag}_weights_loaded"), core.sem(f"{tag}_zeroed")
        self.loads, self.fills = 16 * len(loads), 16 * 8 * len(fills)
        width = max((tiles for _, tiles in fills), default=1) * D // 8
        zero = core.sbuf(f"{tag}_zero", [P, width], on=on)
        s_zero = core.sem(f"{tag}_zero_ready")
        with nc.Block() as block:
            @block.vector
            def _(dve):
                nc.vector.memset(zero[:], 0.0).then_inc(s_zero, 1)

            @block.sync
            def _(sp):
                for tile, array in loads:
                    sp.dma_start(tile, array).then_inc(self.loaded, 16)
                sp.wait_ge(s_zero, 1)
                for table, tiles in fills:
                    flat = table.rearrange("r d -> (r d)").rearrange("(k p w) -> k p w", k=8, p=P)
                    for k in range(8):
                        sp.dma_start(flat[k], zero[:, 0:tiles * D // 8]).then_inc(self.zeroed, 16)


def modulated(core, layer, Hr, L, row):
    nc, B, X, aps, tag = core.nc, core.B, core.X, core.aps, f"r{row}"
    on = ExitStack()
    with on:
        sb = lambda name, shape, dt=F32: core.sbuf(f"{tag}_{name}", shape, dt, on=on)
        gw = sb("gate_w", [P, E])
        mod = [sb(f"mod_rows{n}", [P, 2, D]) for n in range(STAGES)]
        xn = [sb(f"xn{n}", [P, TC, D]) for n in range(2)]
        scaled = [sb(f"scaled{n}", [P, TC, D]) for n in range(2)]
        if L is not None:
            h = [sb(f"h{n}", [P, TC, D]) for n in range(2)]
            hT = [sb(f"hT{n}", [P, TC, P]) for n in range(2)]
            psT = core.psum(f"{tag}_psT", [P, 2, 512], on=on)
            psL = core.psum(f"{tag}_psL", [P, 2, 512], on=on)
        S = start_counts(core, tag, ("w_loaded", "mod_loaded0", "mod_loaded1", "mod_loaded2", "mod_loaded3", "xn_ready", "scaled", "h_ready", "h_kept", "hT_ps", "hT_ready",
                                     "logits_ps", "logits_kept", "stats"))

        def loop(eng, emit):
            for u in range(STAGES):
                emit(u, u, u % 2, 0)
            with eng.Fori(0, B // STAGES - 1) as t:
                for u in range(STAGES):
                    emit(t * STAGES + (STAGES + u), u, u % 2, t + 1)

        with nc.Block() as block:
            @block.sync
            def _(sp):
                if L is not None:
                    sp.dma_start(gw[:], aps[f"L{layer}_ffn_gate_w"]).then_inc(S["w_loaded"], 16)

                def emit(b, v, u, turn):
                    upto(sp, S["h_ready"], b - STAGES + 1)
                    sp.dma_start(mod[v][:], core.modrow[row:row + 2, ds(b, 1), :].rearrange("k n d -> (k n) d").partition_broadcast(P))\
                        .then_inc(S[f"mod_loaded{v}"], 16)
                loop(sp, emit)

            @block.vector
            def _(dve):
                def keep_logits(b, u):
                    upto(dve, S["logits_ps"], b + 1)
                    nc.vector.tensor_copy(L[:, ds(b * (TC * E), TC * E)], psL[:, u, 0:TC * E]).then_inc(S["logits_kept"], 1)

                def stats(b, u):
                    upto(dve, S["h_ready"], b + 1)
                    for k in range(TC):
                        last = tile_stats(core, Hr, b * TC + k)
                    last.then_inc(S["stats"], 1)

                finish = stats if L is None else keep_logits

                def emit(b, v, u, turn):
                    for k in range(TC):
                        c = b * TC + k
                        last = nc.vector.tensor_scalar(xn[u][:, k, :], X[:, ds(b * (TC * D) + k * D, D)], core.rstd[:, ds(c, 1)],
                                                       core.nmr[:, ds(c, 1)], ALU.mult, ALU.add)
                    last.then_inc(S["xn_ready"], 1)
                    upto(dve, S[f"mod_loaded{v}"], 16 * (turn + 1))
                    upto(dve, S["h_ready"], b - 1)
                    upto(dve, S["xn_ready"], b + 1)
                    nc.vector.tensor_tensor(scaled[u][:], xn[u][:], mod[v][:, 1, :].unsqueeze(1).broadcast_to([P, TC, D]), ALU.mult).then_inc(S["scaled"], 1)
                    if not (isinstance(b, int) and b < 2):
                        finish(b - 2, u)
                loop(dve, emit)
                finish(B - 2, 0)
                finish(B - 1, 1)
                if L is None:
                    upto(dve, S["stats"], B)

            @block.gpsimd
            def _(pool):
                def emit(b, v, u, turn):
                    if L is None:
                        out = Hr[:, ds(b * (TC * D), TC * D)].rearrange("p (k d) -> p k d", d=D)
                    else:
                        out = h[u][:]
                        upto(pool, S["h_kept"], b - 1)
                        upto(pool, S["hT_ps"], b - 1)
                    upto(pool, S["scaled"], b + 1)
                    nc.gpsimd.tensor_tensor(out, scaled[u][:], mod[v][:, 0, :].unsqueeze(1).broadcast_to([P, TC, D]), ALU.add).then_inc(S["h_ready"], 1)
                loop(pool, emit)

            if L is not None:
                @block.tensor
                def _(pe):
                    upto(pe, S["w_loaded"], 16)

                    def logits(b, u):
                        upto(pe, S["hT_ready"], b + 1)
                        upto(pe, S["logits_kept"], b - 1)
                        for k in range(TC):
                            last = nc.tensor.matmul(psL[:, u, k * E:(k + 1) * E], hT[u][:, k, :], gw[:], start=True, stop=True)
                        last.then_inc(S["logits_ps"], 1)

                    def emit(b, v, u, turn):
                        if not (isinstance(b, int) and b == 0):
                            logits(b - 1, 1 - u)
                        upto(pe, S["h_ready"], b + 1)
                        upto(pe, S["hT_ready"], b - 1)
                        for k in range(TC):
                            last = nc.tensor.transpose(psT[:, u, k * P:(k + 1) * P], h[u][:, k, :], core.ident[:])
                        last.then_inc(S["hT_ps"], 1)
                    loop(pe, emit)
                    logits(B - 1, 1)

                @block.scalar
                def _(act):
                    def emit(b, v, u, turn):
                        upto(act, S["h_ready"], b + 1)
                        nc.scalar.activation(Hr[:, ds(b * (TC * D), TC * D)], h[u][:].rearrange("p k d -> p (k d)"), ACT.Copy).then_inc(S["h_kept"], 1)
                        upto(act, S["hT_ps"], b + 1)
                        upto(act, S["logits_ps"], b - 1)
                        nc.scalar.activation(hT[u][:].rearrange("p k t -> p (k t)"), psT[:, u, 0:TC * P], ACT.Copy).then_inc(S["hT_ready"], 1)
                    loop(act, emit)


def moe_route(core, layer, L, slots, weights, expert_of_tile=None, tiles=0):
    nc, NT, aps, tag = core.nc, core.NT, core.aps, f"q{layer}"
    K = 2 if layer == 0 else 1
    on = ExitStack()
    with on:
        sb = lambda name, shape, dt=F32: core.sbuf(f"{tag}_{name}", shape, dt, on=on)
        big = lambda name: sb(name, [P, NT, E])
        rev, tri, allone = sb("rev", [P, E]), sb("tri", [P, P]), sb("allone", [P, P])
        gb = sb("gate_b", [P, E])
        m = [big(f"choice{k}") for k in range(K)]
        L2, eq, cand, lim, dist, ex = big("masked_logits"), big("is_max"), big("candidates"), big("limit"), big("distance"), big("expd")
        both, before, within, place = big("chosen"), big("tiles_before"), big("within"), big("place")
        v, r = [sb(f"top{k}", [P, NT]) for k in range(K)], sb("rank", [P, NT])
        total = sb("sum", [P, NT])
        zero = sb("zeros", [P, NT])
        cnt, cnt_i = sb("counts", [P, E]), sb("counts_int", [P, E], I32)
        ends, base = sb("tile_ends", [P, E]), sb("base", [P, E])
        slot_f = sb("slot_f", [P, NT])
        ps = core.psum(f"{tag}_ps", [P, 2, 512], on=on)
        s_in, s_exp, s_exped = core.sem(f"{tag}_loaded"), core.sem(f"{tag}_exp_in"), core.sem(f"{tag}_exp_out")
        s_m, s_cum = core.sem(f"{tag}_chosen"), core.sem(f"{tag}_cum_ps")
        per_token = lambda t: t[:].unsqueeze(2).broadcast_to([P, NT, E])
        per_expert = lambda t: t[:].unsqueeze(1).broadcast_to([P, NT, E])
        flat = lambda t: t[:].rearrange("p n e -> p (n e)")
        with nc.Block() as block:
            @block.sync
            def _(sp):
                sp.dma_start(rev[:], aps["rev_rank"]).then_inc(s_in, 16)
                sp.dma_start(tri[:], aps["tri"]).then_inc(s_in, 16)
                if layer:
                    sp.dma_start(gb[:], aps["L1_ffn_gate_b"].partition_broadcast(P)).then_inc(s_in, 16)

            @block.scalar
            def _(act):
                for k in range(K):
                    act.wait_ge(s_exp, k + 1)
                    nc.scalar.activation(flat(ex), flat(dist), ACT.Exp).then_inc(s_exped, 1)

            @block.tensor
            def _(pe):
                pe.wait_ge(s_m, 1)
                nc.tensor.matmul(ps[:, 0, 0:NT * E], tri[:], flat(both), start=True, stop=True)
                nc.tensor.matmul(ps[:, 1, 0:NT * E], allone[:], flat(both), start=True, stop=True).then_inc(s_cum, 1)

            @block.vector
            def _(dve):
                chain = Chain(core, dve, f"{tag}_dve_chain")
                step = chain.step
                tt, ts, stt, red = nc.vector.tensor_tensor, nc.vector.tensor_scalar, nc.vector.scalar_tensor_tensor, nc.vector.tensor_reduce
                L3 = L[:].rearrange("p (n e) -> p n e", e=E)
                dve.wait_ge(s_in, 32 + 16 * layer)
                nc.vector.memset(allone[:], 1.0)
                step(nc.vector.memset(zero[:], 0.0))
                if layer:
                    step(tt(L3, L3, per_expert(gb), ALU.add))

                def first_max(src, k):
                    step(red(v[k][:], src, AX.X, ALU.max))
                    step(tt(eq[:], src, per_token(v[k]), ALU.is_equal))
                    step(tt(cand[:], eq[:], per_expert(rev), ALU.mult))
                    step(red(r[:], cand[:], AX.X, ALU.max))
                    step(tt(m[k][:], cand[:], per_token(r), ALU.is_equal))

                first_max(L3, 0)
                if K == 2:
                    step(ts(flat(L2), flat(m[0]), -2e38, 1e38, ALU.mult, ALU.add))
                    step(tt(L2[:], L2[:], L3, ALU.min))
                    first_max(L2[:], 1)
                for k in range(K):
                    src = L3 if k == 0 else L2[:]
                    step(tt(dist[:], src, per_token(v[k]), ALU.subtract))
                    dist_ready = nc.vector.tensor_copy(total[:], zero[:])
                    dist_ready.then_inc(s_exp, 1)
                    dve.wait_ge(s_exp, k + 1)
                    if layer == 0:
                        step(stt(out=lim[:], in0=L3, scalar=-1.0, in1=L3, op0=ALU.mult, op1=ALU.max))
                        step(tt(lim[:], lim[:], per_token(v[k]), ALU.max))
                        step(stt(out=flat(lim), in0=flat(lim), scalar=0.02, in1=flat(dist), op0=ALU.mult, op1=ALU.add))
                        step(ts(flat(lim), flat(lim), 0.0, None, ALU.is_ge))
                        dve.wait_ge(s_exped, k + 1)
                        step(tt(flat(ex), flat(ex), flat(lim), ALU.mult))
                    else:
                        dve.wait_ge(s_exped, k + 1)
                    step(red(total[:], ex[:], AX.X, ALU.add))
                    step(nc.vector.reciprocal(weights[k][:], total[:]))
                if K == 2:
                    tt(both[:], m[0][:], m[1][:], ALU.add).then_inc(s_m, 1)
                else:
                    nc.vector.tensor_copy(flat(both), flat(m[0])).then_inc(s_m, 1)
                dve.wait_ge(s_cum, 1)
                tot = ps[:, 1, 0:NT * E].rearrange("p (n e) -> p n e", e=E)
                step(nc.vector.tensor_copy(within[:], tot))
                for e in range(E):
                    last = nc.vector.tensor_tensor_scan(before[:, :, e], within[:, :, e], zero[:], 0.0, ALU.add, ALU.add)
                step(last)
                step(nc.vector.tensor_copy(cnt[:], before[:, NT - 1, :]))
                step(tt(before[:], before[:], within[:], ALU.subtract))
                step(tt(place[:], before[:], ps[:, 0, 0:NT * E].rearrange("p (n e) -> p n e", e=E), ALU.add))
                if layer == 0:
                    step(ts(cnt_i[:], cnt[:], float(P - 1), None, ALU.add))
                    step(ts(cnt_i[:], cnt_i[:], 7, None, ALU.arith_shift_right))
                    step(nc.vector.tensor_copy(cnt[:], cnt_i[:]))
                    step(nc.vector.tensor_tensor_scan(ends[:], cnt[:], zero[:, 0:E], 0.0, ALU.add, ALU.add))
                    step(tt(base[:], ends[:], cnt[:], ALU.subtract))
                    step(ts(base[:], base[:], float(P), -1.0, ALU.mult, ALU.add))
                    step(tt(place[:], place[:], per_expert(base), ALU.add))
                    for k in range(K):
                        step(tt(cand[:], m[k][:], place[:], ALU.mult))
                        step(red(slot_f[:], cand[:], AX.X, ALU.add))
                        step(nc.vector.tensor_copy(slots[k][:], slot_f[:]))
                    tile_no = sb("tile_no", [1, tiles])
                    acc = sb("tile_expert", [1, tiles])
                    step(nc.vector.memset(acc[:], 1.0))
                    step(nc.vector.tensor_tensor_scan(tile_no[:], acc[:], acc[:], -1.0, ALU.mult, ALU.add))
                    step(nc.vector.memset(acc[:], 0.0))
                    for e in range(E - 1):
                        step(stt(out=acc[:], in0=tile_no[:], scalar=ends[0:1, e:e + 1], in1=acc[:], op0=ALU.is_ge, op1=ALU.add))
                    step(nc.vector.tensor_copy(expert_of_tile[:], acc[:]))
                else:
                    step(tt(cand[:], m[0][:], place[:], ALU.mult))
                    step(red(r[:], cand[:], AX.X, ALU.add))
                    step(ts(base[:], rev[:], -float(CAP), float(E * CAP - 1), ALU.mult, ALU.add))
                    step(tt(place[:], place[:], per_expert(base), ALU.add))
                    step(tt(cand[:], m[0][:], place[:], ALU.mult))
                    step(red(slot_f[:], cand[:], AX.X, ALU.add))
                    step(ts(r[:], r[:], float(CAP), None, ALU.is_le))
                    nc.vector.tensor_tensor(weights[0][:], weights[0][:], r[:], ALU.mult)
                    step(ts(slot_f[:], slot_f[:], -float(E * CAP), None, ALU.add))
                    step(tt(slot_f[:], slot_f[:], r[:], ALU.mult))
                    step(ts(slot_f[:], slot_f[:], float(E * CAP), None, ALU.add))
                    step(nc.vector.tensor_copy(slots[0][:], slot_f[:]))


def scatter_rows(core, tag, Hr, slots, table, rows, ahead):
    nc, NT, K = core.nc, core.NT, len(slots)
    on = ExitStack()
    with on:
        row = [core.sbuf(f"{tag}_row{n}", [P, D], on=on) for n in range(STAGES)]
        idx = [[core.sbuf(f"{tag}_idx{n}_{k}", [P, 1], U32, on=on) for k in range(K)] for n in range(STAGES)]
        S = start_counts(core, tag, ["row_staged", "slot_staged", "passed"])
        scattered = [core.sem(f"{tag}_scattered{u}") for u in range(STAGES)]

        def loop(eng, emit):
            for u in range(STAGES):
                emit(u, u, 0)
            with eng.Fori(0, NT // STAGES - 1) as t:
                for u in range(STAGES):
                    emit((t + 1) * STAGES + u, u, t + 1)

        with nc.Block() as block:
            @block.scalar
            def _(act):
                def emit(t, u, turn):
                    at(act, scattered[u], turn * (16 * K))
                    nc.scalar.activation(row[u][:], Hr[:, ds(t * D, D)], ACT.Copy).then_inc(S["row_staged"], 1)
                loop(act, emit)

            @block.vector
            def _(dve):
                def emit(t, u, turn):
                    at(dve, scattered[u], turn * (16 * K))
                    for k in range(K):
                        last = nc.vector.tensor_copy(idx[u][k][:], slots[k][:, ds(t, 1)])
                    last.then_inc(S["slot_staged"], 1)
                loop(dve, emit)

            @block.gpsimd
            def _(pool):
                pool.wait_ge(ahead.zeroed, ahead.fills)

                def emit(t, u, turn):
                    upto(pool, S["row_staged"], t + 1)
                    at_alone(pool, S["slot_staged"], t + 2, S["passed"])
                    for k in range(K):
                        nc.gpsimd.indirect_dma_start(out=table, out_offset=bass.IndirectOffsetOnAxis(ap=idx[u][k][:, 0:1], axis=0),
                                                     in_=row[u][:], in_offset=None, bounds_check=rows - 1, oob_is_err=False)\
                            .then_inc(scattered[u], 16)
                loop(pool, emit)
                for u in range(STAGES):
                    pool.wait_ge(scattered[u], 16 * K * (NT // STAGES))


def experts0(core, W, ahead, XS, YS, expert_of_tile, tiles):
    nc, aps = core.nc, core.aps
    U = 3
    assert tiles % U == 0
    on = ExitStack()
    with on:
        sb = lambda name, shape, dt=F32: core.sbuf("e0_" + name, shape, dt, on=on)
        w1, w3, w2 = W
        x = [sb(f"x{n}", [P, D]) for n in range(U)]
        xT = [sb(f"xT{n}", [P, P]) for n in range(U)]
        act_h = [sb(f"silu{n}", [P, F]) for n in range(U)]
        g = [sb(f"g{n}", [P, FC, P]) for n in range(U)]
        gT = [sb(f"gT{n}", [P, FC, P]) for n in range(U)]
        y = [sb(f"y{n}", [P, D]) for n in range(U)]
        psX, ps1, ps3, psY = (core.psum("e0_ps" + n, [P, 512], on=on) for n in "X13Y")
        psG = core.psum("e0_psG", [P, FC, P], on=on)
        S = start_counts(core, "e0", ["xT_ps", "xT_ready", "h1_ps", "h3_ps", "silu_ready", "g_ready", "gT_ps", "gT_ready",
                                      "y_ps", "y_ready"] + [f"{n}{u}" for n in ("x_loaded", "y_stored") for u in range(U)])
        turns = tiles // U
        LAG = 4

        def loop(eng, emit):
            peeled = 2 * U
            for i in range(peeled):
                emit(i, i % U, i // U)
            with eng.Fori(0, turns - 2) as t:
                for u in range(U):
                    emit(t * U + (peeled + u), u, t + 2)
            for i in range(tiles, tiles + LAG):
                emit(i, i % U, i // U)

        live = lambda i, lag: not isinstance(i, int) or 0 <= i - lag < tiles
        buf = lambda u, lag: (u - lag) % U
        times = lambda u, turn, lag: turn + (u - lag) // U

        with nc.Block() as block:
            @block.sync
            def _(sp):
                def emit(i, u, turn):
                    if live(i, 0):
                        upto(sp, S["xT_ps"], i - U + 1)
                        sp.dma_start(x[u][:], XS[ds(i * P, P), :]).then_inc(S[f"x_loaded{u}"], 16)
                    if live(i, 4):
                        j, n = i - 4, buf(u, 4)
                        upto(sp, S["y_ready"], j + 1)
                        sp.dma_start(YS[ds(j * P, P), :], y[n][:]).then_inc(S[f"y_stored{n}"], 16)
                loop(sp, emit)
                for u in range(U):
                    upto(sp, S[f"y_stored{u}"], 16 * turns)

            @block.tensor
            def _(pe):
                mm = nc.tensor.matmul
                pe.wait_ge(ahead.loaded, ahead.loads)
                expert = lambda j: pe.value_load(expert_of_tile[0:1, ds(j, 1)], min_val=0, max_val=E - 1)

                def emit(i, u, turn):
                    up = expert(i - 1) if live(i, 1) else None
                    down = expert(i - 3) if live(i, 3) else None
                    if live(i, 0):
                        upto(pe, S[f"x_loaded{u}"], 16 * (turn + 1))
                        upto(pe, S["xT_ready"], i)
                        nc.tensor.transpose(psX[:, 0:P], x[u][:], core.ident[:]).then_inc(S["xT_ps"], 1)
                    if live(i, 2):
                        j, n = i - 2, buf(u, 2)
                        upto(pe, S["g_ready"], j + 1)
                        upto(pe, S["gT_ready"], j)
                        for c in range(FC):
                            last = nc.tensor.transpose(psG[:, c, :], g[n][:, c, :], core.ident[:])
                        last.then_inc(S["gT_ps"], 1)
                    if live(i, 1):
                        j, n = i - 1, buf(u, 1)
                        upto(pe, S["xT_ready"], j + 1)
                        upto(pe, S["silu_ready"], j)
                        mm(ps1[:], xT[n][:], w1[:, ds(up, 1), :].rearrange("p n f -> p (n f)"), start=True, stop=True).then_inc(S["h1_ps"], 1)
                        upto(pe, S["g_ready"], j)
                        mm(ps3[:], xT[n][:], w3[:, ds(up, 1), :].rearrange("p n f -> p (n f)"), start=True, stop=True).then_inc(S["h3_ps"], 1)
                    if live(i, 3):
                        j, n = i - 3, buf(u, 3)
                        upto(pe, S["gT_ready"], j + 1)
                        upto(pe, S["y_ready"], j)
                        for c in range(FC):
                            last = mm(psY[:, 0:D], gT[n][:, c, :], w2[:, ds(down, 1), c, :].rearrange("p n d -> p (n d)"), start=(c == 0), stop=(c == FC - 1))
                        last.then_inc(S["y_ps"], 1)
                loop(pe, emit)

            @block.scalar
            def _(act):
                def emit(i, u, turn):
                    if live(i, 2):
                        j, n = i - 2, buf(u, 2)
                        upto(act, S["gT_ps"], j + 1)
                        upto(act, S["y_ps"], j - U + 1)
                        nc.scalar.activation(gT[n][:].rearrange("p c t -> p (c t)"), psG[:].rearrange("p c t -> p (c t)"), ACT.Copy).then_inc(S["gT_ready"], 1)
                    if live(i, 1):
                        j, n = i - 1, buf(u, 1)
                        upto(act, S["h1_ps"], j + 1)
                        upto(act, S["g_ready"], j - U + 1)
                        nc.scalar.activation(act_h[n][:], ps1[:], ACT.Silu).then_inc(S["silu_ready"], 1)
                loop(act, emit)

            @block.vector
            def _(dve):
                def emit(i, u, turn):
                    if live(i, 0):
                        upto(dve, S["xT_ps"], i + 1)
                        upto(dve, S["h3_ps"], i - U + 1)
                        nc.vector.tensor_copy(xT[u][:], psX[:, 0:P]).then_inc(S["xT_ready"], 1)
                    if live(i, 1):
                        j, n = i - 1, buf(u, 1)
                        upto(dve, S["silu_ready"], j + 1)
                        upto(dve, S["h3_ps"], j + 1)
                        upto(dve, S["gT_ps"], j - U + 1)
                        nc.vector.tensor_tensor(g[n][:].rearrange("p c t -> p (c t)"), act_h[n][:], ps3[:], ALU.mult).then_inc(S["g_ready"], 1)
                    if live(i, 3):
                        j, n = i - 3, buf(u, 3)
                        upto(dve, S["y_ps"], j + 1)
                        upto(dve, S[f"y_stored{n}"], times(u, turn, 3) * 16)
                        nc.vector.tensor_copy(y[n][:], psY[:, 0:D]).then_inc(S["y_ready"], 1)
                loop(dve, emit)


def gather_and_add(core, tag, layer, slots, weights, table, stats):
    nc, NT, B, X, K = core.nc, core.NT, core.B, core.X, len(slots)
    GB = STAGES // TC
    on = ExitStack()
    with on:
        yg = [[core.sbuf(f"{tag}_y{n}_{k}", [P, D], on=on) for k in range(K)] for n in range(STAGES)]
        idx = [[core.sbuf(f"{tag}_idx{n}_{k}", [P, 1], U32, on=on) for k in range(K)] for n in range(STAGES)]
        acc = [core.sbuf(f"{tag}_acc{n}", [P, D], on=on) for n in range(STAGES)]
        gate = [core.sbuf(f"{tag}_gate{n}", [P, D], on=on) for n in range(GB)]
        S = start_counts(core, tag, ["slot_staged", "weighted", "summed", "gated", "x_updated", "stats", "passed"] + [f"gate_loaded{u}" for u in range(GB)])
        gathered = [core.sem(f"{tag}_gathered{u}") for u in range(STAGES)]
        turns = NT // STAGES

        with nc.Block() as block:
            @block.sync
            def _(sp):
                with sp.Fori(0, turns) as turn:
                    for n in range(GB):
                        upto(sp, S["gated"], turn * STAGES)
                        sp.dma_start(gate[n][:], core.modrow[1 + 2 * layer, ds(turn * GB + n, 1), :].rearrange("n d -> (n d)").partition_broadcast(P))\
                            .then_inc(S[f"gate_loaded{n}"], 16)

            @block.gpsimd
            def _(pool):
                with pool.Fori(0, turns) as turn:
                    for u in range(STAGES):
                        at_alone(pool, S["slot_staged"], turn * STAGES + (u + 1) + 1, S["passed"])
                        for k in range(K):
                            nc.gpsimd.indirect_dma_start(out=yg[u][k][:], out_offset=None, in_=table,
                                                         in_offset=bass.IndirectOffsetOnAxis(ap=idx[u][k][:, 0:1], axis=0))\
                                .then_inc(gathered[u], 16)

            @block.vector
            def _(dve):
                ahead = STAGES - 1

                def stage(t, u):
                    for k in range(K):
                        last = nc.vector.tensor_copy(idx[u][k][:], slots[k][:, ds(t, 1)])
                    last.then_inc(S["slot_staged"], 1)

                for t in range(ahead):
                    stage(t, t)

                def emit(t, u, turn):
                    if not isinstance(t, int) or t + ahead < NT:
                        stage(t + ahead, (u + ahead) % STAGES)
                    dve.wait_ge(gathered[u], (turn + 1) * (16 * K))
                    gate_rows = gate[u // TC][:]
                    w = lambda k: weights[k][:, ds(t, 1)]
                    stt = nc.vector.scalar_tensor_tensor
                    if K == 1:
                        upto(dve, S[f"gate_loaded{u // TC}"], (turn + 1) * 16)
                        stt(out=acc[u][:], in0=yg[u][0][:], scalar=w(0), in1=gate_rows, op0=ALU.mult, op1=ALU.mult).then_inc(S["gated"], 1)
                    else:
                        nc.vector.tensor_scalar(acc[u][:], yg[u][0][:], w(0), None, ALU.mult).then_inc(S["weighted"], 1)
                        upto(dve, S["weighted"], t + 1)
                        stt(out=acc[u][:], in0=yg[u][1][:], scalar=w(1), in1=acc[u][:], op0=ALU.mult, op1=ALU.add).then_inc(S["summed"], 1)
                        upto(dve, S["summed"], t + 1)
                        upto(dve, S[f"gate_loaded{u // TC}"], (turn + 1) * 16)
                        nc.vector.tensor_tensor(acc[u][:], acc[u][:], gate_rows, ALU.mult).then_inc(S["gated"], 1)
                    if stats and not (isinstance(t, int) and t == 0):
                        upto(dve, S["x_updated"], t)
                        tile_stats(core, X, t - 1)
                    upto(dve, S["gated"], t + 1)
                    x = X[:, ds(t * D, D)]
                    nc.vector.tensor_tensor(x, x, acc[u][:], ALU.add).then_inc(S["x_updated"], 1)

                for u in range(STAGES):
                    emit(u, u, 0)
                with dve.Fori(0, turns - 2) as turn:
                    for u in range(STAGES):
                        emit(turn * STAGES + (STAGES + u), u, turn + 1)
                for u in range(STAGES):
                    emit((turns - 1) * STAGES + u, u, turns - 1)
                upto(dve, S["x_updated"], NT)
                if stats:
                    tile_stats(core, X, NT - 1).then_inc(S["stats"], 1)
                    upto(dve, S["stats"], 1)


def ffn0(core):
    nc, aps, NT = core.nc, core.aps, core.NT
    tiles = 2 * NT + E - 1
    tiles += -tiles % 3
    XS = nc.dram_tensor("slot_inputs", [tiles * P, D], F32, kind="Internal").ap()
    YS = nc.dram_tensor("slot_outputs", [tiles * P, D], F32, kind="Internal").ap()
    on = ExitStack()
    with on:
        slots = [core.sbuf(f"slots0_{k}", [P, NT], U32, on=on) for k in range(2)]
        weights = [core.sbuf(f"weights0_{k}", [P, NT], on=on) for k in range(2)]
        expert_of_tile = core.sbuf("expert_of_tile", [1, tiles], I32, on=on)
        w1, w3, w2 = (core.sbuf(f"e0_{n}", [P, E, F], on=on) for n in ("w1", "w3", "w2"))
        up = lambda name: aps[name].rearrange("e d f -> d e f")
        ahead = Ahead(core, "e0", [(w1[:], up("L0_ffn_w1")), (w3[:], up("L0_ffn_w3")),
                                   (w2[:].rearrange("p e (c d) -> p (e c) d", d=D), aps["L0_ffn_w2"].rearrange("e (c f) d -> f (e c) d", f=P))],
                      [(XS, tiles)], on=on)
        w2 = w2[:].rearrange("p e (c d) -> p e c d", d=D)
        norm_stats(core, "lnB")
        scratch = ExitStack()
        with scratch:
            Hr = core.sbuf("h_rows0", [P, NT * D], on=scratch)
            L = core.sbuf("logits0", [P, NT * E], on=scratch)
            modulated(core, 0, Hr, L, 4)
            moe_route(core, 0, L, slots, weights, expert_of_tile, tiles)
            scatter_rows(core, "sc0", Hr, slots, XS, tiles * P, ahead)
        experts0(core, (w1, w3, w2), ahead, XS, YS, expert_of_tile, tiles)
        gather_and_add(core, "ga0", 0, slots, weights, YS, stats=True)
DI, DS, DC, DTR = 256, 16, 4, 8
C2 = DI // P
DIRS = 2
G = 2
W = G * T
BC = 2 * DS
PREP = [("x",), ("conv", 0, 0), ("conv", 0, 1), ("conv", 1, 0), ("dt", 0, 0), ("conv", 1, 1), ("dt", 0, 1), ("bc", 0),
        ("dt", 1, 0), ("dt", 1, 1), ("bc", 1), ("z", 0), ("z", 1)]
USES = len(PREP)
BANK_USES = ((USES + 1) // 2, USES // 2)
USE = {what: n for n, what in enumerate(PREP)}
PREP_AT = {0: [("x", 0, 1)], 1: [("conv", 0, 0, 0, 3)], 2: [("conv", 0, 0, 3, 4), ("conv", 0, 1, 0, 2)],
           3: [("conv", 0, 1, 2, 4), ("conv", 1, 0, 0, 1)], 4: [("conv", 1, 0, 1, 4)], 5: [("dt", 0, 0, 0, 2)],
           6: [("conv", 1, 1, 0, 3)], 7: [("conv", 1, 1, 3, 4), ("dt", 0, 1, 0, 2)], 8: [("bc", 0, 0, 2)], 9: [("dt", 1, 0, 0, 2)],
           10: [("dt", 1, 1, 0, 2)], 11: [("bc", 1, 0, 2)], 12: [("z", 0, 0, 1)], 13: [("z", 1, 0, 1)]}


def mixer_weights(core, Wt, on):
    nc, aps = core.nc, core.aps
    tmp = ExitStack()
    with tmp:
        sb = lambda name, shape, dt=F32: core.sbuf("w_" + name, shape, dt, on=tmp)
        win = sb("in_proj", [P, 4, D])
        taps = sb("conv_w", [P, DIRS, C2, DC])
        scaled = sb("in_taps", [P, DIRS, C2, DC, D])
        wout = sb("out_proj", [P, DI])
        xp = sb("x_proj", [BC + DTR, DIRS, DI])
        xdt = sb("x_proj_dt", [DTR, DIRS, DI])
        dtT = sb("dt_w_T", [DTR, DIRS, DI])
        sel = sb("selector", [PARTS * BC, BC])
        alog = sb("A_log", [P, DIRS, C2, DS])
        ps = core.psum("w_ps", [P, 4, 512], on=tmp)
        S = {n: core.sem("w_" + n) for n in ("loaded", "scaled", "ps", "kept", "exp_done", "done")}
        names = "fb"
        jobs = []
        for d in range(DIRS):
            for c in range(C2):
                for k in range(DC):
                    jobs.append((Wt["taps"][:, d, c, k, :], scaled[:, d, c, k, :], None))
        for c in range(C2):
            jobs.append((Wt["z"][:, c, :], win[:, C2 + c, :], None))
            jobs.append((Wt["out"][:, c, :], wout[:, c * P:(c + 1) * P], None))
        for d in range(DIRS):
            for c in range(C2):
                jobs.append((Wt["bc"][:, d, c, :], xp[0:BC, d, c * P:(c + 1) * P], None))
                for c2 in range(C2):
                    jobs.append((Wt["dt"][:, d, c, c2, :], xdt[:, d, c * P:(c + 1) * P], dtT[:, d, c2 * P:(c2 + 1) * P]))
        with nc.Block() as block:
            @block.sync
            def _(sp):
                n = 0

                def load(dst, src, **how):
                    sp.dma_start(dst, src, **how).then_inc(S["loaded"], 16)
                load(win[:], aps["L1_attn_in_proj_w"].rearrange("(c p) e -> p c e", p=P))
                load(wout[:], aps["L1_attn_out_proj_w"])
                load(sel[:], aps["selector"])
                for d, f in enumerate(names):
                    load(taps[:, d], aps[f"L1_attn_conv_w_{f}"].rearrange("(c p) k -> p c k", p=P))
                    x = aps[f"L1_attn_x_proj_w_{f}"]
                    load(xp[0:BC, d], x[DTR:DTR + BC])
                    load(xdt[:, d], x[0:DTR])
                    load(dtT[:, d], aps[f"L1_attn_dt_w_{f}"].rearrange("d r -> r d"), allow_slow_non_contiguous=True)
                    load(alog[:, d], aps[f"L1_attn_A_log_{f}"].rearrange("(c p) s -> p c s", p=P))
                    for name, key in (("conv_b", "conv_b"), ("dt_b", "dt_b"), ("D", "D")):
                        load(Wt[key][:, d], aps[f"L1_attn_{name}_{f}"].rearrange("(c p n) -> p c n", p=P, n=1), allow_slow_non_contiguous=True)
                load(Wt["ln1"][:, 0:1], aps["L1_attn_ln1_g"].rearrange("(p n) -> p n", n=1))
                load(Wt["ln1"][:, 1:2], aps["L1_attn_ln1_b"].rearrange("(p n) -> p n", n=1))

            loads = 16 * (3 + DIRS * 8 + 2)

            @block.scalar
            def _(act):
                act.wait_ge(S["loaded"], loads)
                nc.scalar.activation(Wt["A"][:].rearrange("p d c s -> p (d c s)"), alog[:].rearrange("p d c s -> p (d c s)"), ACT.Exp).then_inc(S["exp_done"], 1)

            @block.vector
            def _(dve):
                dve.wait_ge(S["loaded"], loads)
                for d in range(DIRS):
                    for c in range(C2):
                        for k in range(DC):
                            last = nc.vector.tensor_scalar(scaled[:, d, c, k, :], win[:, c, :], taps[:, d, c, k:k + 1], None, ALU.mult)
                last.then_inc(S["scaled"], 1)
                nc.vector.tensor_copy(Wt["sel"][:], sel[:].unsqueeze(2).broadcast_to([PARTS * BC, BC, P]))
                nc.vector.memset(Wt["one"][:], 1.0)
                dve.wait_ge(S["exp_done"], 1)
                a = Wt["A"][:].rearrange("p d c s -> p (d c s)")
                nc.vector.tensor_scalar(a, a, -1.0, None, ALU.mult)
                for n, (dst, _, rhs) in enumerate(jobs):
                    dve.wait_ge(S["ps"], n + 1)
                    nc.vector.tensor_copy(dst, ps[:, n % 4, 0:dst.shape[-1]]).then_inc(S["kept"], 1)
                dve.wait_ge(S["kept"], len(jobs))

            @block.tensor
            def _(pe):
                pe.wait_ge(S["scaled"], 1)
                for n, (dst, src, rhs) in enumerate(jobs):
                    at(pe, S["kept"], n - 3)
                    if rhs is None:
                        k = src.shape[0]
                        nc.tensor.transpose(ps[:, n % 4, 0:k], src, core.ident[0:k, 0:k]).then_inc(S["ps"], 1)
                    else:
                        nc.tensor.matmul(ps[:, n % 4, 0:P], src, rhs, start=True, stop=True).then_inc(S["ps"], 1)


def mixer(core, Hr, OD, x_saved):
    nc, B, aps = core.nc, core.B, core.aps
    NP = B // G
    live = lambda i, lag: not isinstance(i, int) or 0 <= i - lag < NP
    on = ExitStack()
    with on:
        sb = lambda name, shape, dt=F32: core.sbuf("s_" + name, shape, dt, on=on)
        Wt = {"taps": sb("w_taps", [P, DIRS, C2, DC, P]), "z": sb("w_z", [P, C2, P]), "out": sb("w_out", [P, C2, P]),
              "bc": sb("w_bc", [P, DIRS, C2, BC]), "dt": sb("w_dt", [P, DIRS, C2, C2, P]), "sel": sb("w_sel", [PARTS * BC, BC, P], BF16),
              "A": sb("A", [P, DIRS, C2, DS]), "conv_b": sb("conv_b", [P, DIRS, C2, 1]), "dt_b": sb("dt_b", [P, DIRS, C2, 1]),
              "D": sb("D", [P, DIRS, C2, 1]), "ln1": sb("ln1", [P, 2]), "one": sb("one", [P, 1])}
        mixer_weights(core, Wt, on)
        PADW = T + 2 * (DC - 1)
        xn = sb("xn", [P, G * TC, P])
        xT = sb("xT", [P, G, PADW])
        xc = [sb(f"xc{n}", [P, DIRS, C2, W]) for n in range(2)]
        z = [sb(f"z{n}", [P, C2, W]) for n in range(2)]
        dt = [sb(f"dt{n}", [P, DIRS, C2, W]) for n in range(2)]
        ux = [sb(f"ux{n}", [P, DIRS, C2, W]) for n in range(2)]
        bcs = [sb(f"bc_parts{n}", [PARTS * BC, DIRS, W], BF16) for n in range(2)]
        rest, part2 = sb("bc_rest", [BC, W]), sb("bc_part2", [BC, W], BF16)
        e_abs, e_one, e_ln = sb("exp_abs", [P, DIRS, C2, W]), sb("exp_plus_1", [P, C2, W]), sb("ln", [P, C2, W])
        dA = [sb(f"dA{n}", [P, DIRS, C2, G, T]) for n in range(2)]
        bsb = [sb(f"B_rows{n}", [P, DIRS, W]) for n in range(2)]
        R = core.X[:, 0:8192].rearrange("p (n d c w) -> p n d c w", n=4, d=DIRS, c=C2)
        yg = sb("y_gated", [P, C2, W])
        o = sb("out", [P, G * TC, D])
        YP = core.psum("s_y", [P, C2, W], on=on)
        BP = core.psum("s_B", [P, DIRS, W], on=on)
        CP = core.psum("s_C", [P, DIRS, W], on=on)
        PR = core.psum("s_prep", [P, 2, 512], on=on)
        S = {n: core.sem("s_" + n) for n in (
            "xn_ready", "prep_ps", "prep_read0", "prep_read1", "silu_done", "bc_part1", "bc_rest", "bc_part2", "bc_ready", "abs_done", "z_done",
            "relu_done", "exp_done", "plus1_done", "ln_done", "corr_done", "ln_corr", "dt_ready", "u_ready", "B_ps", "C_ps",
            "B_ready", "dA_ready", "in_ready", "scanned", "part_ready", "summed", "y_read", "y_skip", "gated", "out_ps", "out_read",
            "stats_done", "out_stored", "pads")}
        flat = lambda t: t.rearrange("p c w -> p (c w)")
        read = lambda u: S[f"prep_read{u % 2}"]

        def of(i, u, s):
            if s < DS:
                return (i - 1, (u + 1) % 2, s) if live(i, 1) else None
            return (i, u, s - DS) if live(i, 0) else None

        with nc.Block() as block:
            @block.sync
            def _(sp):
                sp.wait_ge(x_saved, 16)

            @block.vector
            def _(dve):
                nc.vector.memset(xT[:], 0.0)
                for n in range(2):
                    nc.vector.memset(dA[n][:, 0, :, :, 0:1], 0.0)
                    last = nc.vector.memset(dA[n][:, 1, :, :, T - 1:T], 0.0)
                last.then_inc(S["pads"], 1)
                dve.wait_ge(S["pads"], 1)

        with nc.Block() as block:
            @block.sync
            def _(sp):
                def emit(i, u):
                    if live(i, 2):
                        j = i - 2
                        sp.wait_ge(S["stats_done"], j + 1)
                        sp.dma_start(OD[ds(j * (G * TC), G * TC)].rearrange("n p d -> p n d"), o[:]).then_inc(S["out_stored"], 16)
                rolled(sp, NP, 2, 3, emit, ring=2)
                sp.wait_ge(S["out_stored"], 16 * NP)

            @block.gpsimd
            def _(pool):
                def inputs(j, par, s):
                    n = j * DS + s
                    at(pool, S["summed"], n - 3)
                    for d in range(DIRS):
                        pool.wait_ge(S["B_ready"], DIRS * n + (d + 1))
                        if s == 0:
                            pool.wait_ge(S["u_ready"], DIRS * j + (d + 1))
                        nc.gpsimd.tensor_tensor(R[:, s % 4, d], ux[par][:, d], bsb[s % 2][:, d].unsqueeze(1).broadcast_to([P, C2, W]),
                                                ALU.mult).then_inc(S["in_ready"], 1)

                def emit(i, u):
                    for s in range(DS):
                        if live(i, 1) and s > 0:
                            inputs(i - 1, (u + 1) % 2, s)
                        if s == 3 and live(i, 2):
                            pool.wait_ge(S["y_skip"], i - 1)
                            nc.gpsimd.tensor_tensor(yg[:], yg[:], z[u][:], ALU.mult).then_inc(S["gated"], 1)
                        if s in (13, 15) and live(i, 0):
                            d = (s - 13) // 2
                            pool.wait_ge(S["dt_ready"], DIRS * i + (d + 1))
                            nc.gpsimd.tensor_tensor(ux[u][:, d], dt[u][:, d], xc[u][:, d], ALU.mult).then_inc(S["u_ready"], 1)
                    if live(i, 0):
                        inputs(i, u, 0)
                rolled(pool, NP, 2, 3, emit, ring=2)

            @block.scalar
            def _(act):
                def b_copy(j, par, s, d):
                    n = j * DS + s
                    act.wait_ge(S["B_ps"], DIRS * n + (d + 1))
                    at(act, S["in_ready"], DIRS * (n - 2) + (d + 1))
                    nc.scalar.activation(bsb[s % 2][:, d, :], BP[:, d, :], ACT.Copy).then_inc(S["B_ready"], 1)

                def decays(j, par, s):
                    if s == 0:
                        act.wait_ge(S["dt_ready"], DIRS * (j + 1))
                    at(act, S["scanned"], DIRS * (j * DS + (s - 1)))
                    for d in range(DIRS):
                        lo = 1 - d
                        for c in range(C2):
                            last = nc.scalar.activation(dA[s % 2][:, d, c, :, lo:lo + T - 1], dt[par][:, d, c, :].rearrange("p (g t) -> p g t", t=T)[:, :, lo:lo + T - 1],
                                                        ACT.Exp, scale=Wt["A"][:, d, c, s:s + 1])
                    last.then_inc(S["dA_ready"], 1)

                def softplus(i, d):
                    act.wait_ge(S["abs_done"], C2 * (DIRS * i + d) + C2)
                    func(flat(e_abs[:, d]), flat(e_abs[:, d]), ACT.Exp, scale=-1.0).then_inc(S["exp_done"], 1)
                    act.wait_ge(S["exp_done"], DIRS * i + (d + 1))
                    at(act, S["dt_ready"], DIRS * i + d)
                    func(flat(e_one[:]), flat(e_abs[:, d]), ACT.Identity, bias=Wt["one"][:, 0:1]).then_inc(S["plus1_done"], 1)
                    act.wait_ge(S["plus1_done"], DIRS * i + (d + 1))
                    func(flat(e_ln[:]), flat(e_one[:]), ACT.Ln).then_inc(S["ln_done"], 1)

                func = nc.scalar.activation

                def take(i, what):
                    use = USE[what]
                    act.wait_ge(S["prep_ps"], USES * i + (use + 1))
                    return PR[:, use % 2, :], read(use)

                def conv(i, u, d, c):
                    bank, done = take(i, ("conv", d, c))
                    func(xc[u][:, d, c, :], bank, ACT.Identity, bias=Wt["conv_b"][:, d, c, :]).then_inc(done, 1)

                def gate(i, u, c):
                    bank, done = take(i, ("z", c))
                    func(z[u][:, c, :], bank, ACT.Identity).then_inc(done, 1)

                def step_size(i, u, d, c):
                    bank, done = take(i, ("dt", d, c))
                    at(act, S["corr_done"], DIRS * (i - 1) + d + 1)
                    bias = Wt["dt_b"][:, d, c, :]
                    func(e_abs[:, d, c, :], bank, ACT.Abs, bias=bias).then_inc(S["abs_done"], 1)
                    func(dt[u][:, d, c, :], bank, ACT.Relu, bias=bias).then_inc(done, 1)

                def all_read(i, use):
                    act.wait_ge(read(use), BANK_USES[use % 2] * i + (use // 2 + 1))

                def emit(i, u):
                    for s in range(DS):
                        if live(i, 1) and s < DS - 1:
                            decays(*of(i, u, s + 1))
                        if of(i, u, s + 2):
                            for d in range(DIRS):
                                b_copy(*of(i, u, s + 2), d)
                        if live(i, 0):
                            if s == 0:
                                bank, done = take(i, ("x",))
                                func(xT[:, :, DC - 1:DC - 1 + T], bank.rearrange("p (g t) -> p g t", t=T), ACT.Identity,
                                     scale=Wt["ln1"][:, 0:1], bias=Wt["ln1"][:, 1:2]).then_inc(done, 1)
                            if s == 3:
                                at(act, S["y_skip"], i - 1)
                                conv(i, u, 0, 0)
                            if s == 4:
                                conv(i, u, 0, 1)
                            if s == 5:
                                conv(i, u, 1, 0)
                            if s == 8:
                                conv(i, u, 1, 1)
                            if s in (4, 8):
                                d = s // 4 - 1
                                for c in range(C2):
                                    all_read(i, USE["conv", d, c])
                                func(flat(xc[u][:, d]), flat(xc[u][:, d]), ACT.Silu).then_inc(S["silu_done"], 1)
                            if s == 6:
                                step_size(i, u, 0, 0)
                            if s == 8:
                                step_size(i, u, 0, 1)
                            if s == 9:
                                softplus(i, 0)
                            if s == 10:
                                step_size(i, u, 1, 0)
                            if s == 11:
                                step_size(i, u, 1, 1)
                            if s == 12:
                                softplus(i, 1)
                            if s == 13:
                                at(act, S["gated"], i - 1)
                                for c in range(C2):
                                    gate(i, u, c)
                                for c in range(C2):
                                    all_read(i, USE["z", c])
                                func(flat(z[u][:]), flat(z[u][:]), ACT.Silu).then_inc(S["z_done"], 1)
                        if s == 15 and live(i, 2):
                            j = i - 2
                            act.wait_ge(S["out_ps"], j + 1)
                            at(act, S["out_stored"], 16 * j)
                            func(o[:].rearrange("p n d -> p (n d)"), PR[:, 1, :], ACT.Copy).then_inc(S["out_read"], 1)
                        if s == DS - 1 and live(i, 0):
                            decays(i, u, 0)
                rolled(act, NP, 2, 3, emit, ring=2)

            @block.vector
            def _(dve):
                tt, stt = nc.vector.tensor_tensor, nc.vector.scalar_tensor_tensor

                def scan(j, s):
                    n = j * DS + s
                    dve.wait_ge(S["dA_ready"], n + 1)
                    for d in range(DIRS):
                        dve.wait_ge(S["in_ready"], DIRS * n + (d + 1))
                        r, a = flat(R[:, s % 4, d]), dA[s % 2][:, d].rearrange("p c g t -> p (c g t)")
                        if d:
                            r, a = r[:, ::-1], a[:, ::-1]
                        nc.vector.tensor_tensor_scan(r, a, r, 0.0, ALU.mult, ALU.add).then_inc(S["scanned"], 1)
                    for d in range(DIRS):
                        dve.wait_ge(S["C_ps"], DIRS * n + (d + 1))
                        dve.wait_ge(S["scanned"], DIRS * n + (d + 1))
                        r = R[:, s % 4, d]
                        tt(r, r, CP[:, d, :].unsqueeze(1).broadcast_to([P, C2, W]), ALU.mult).then_inc(S["part_ready"], 1)

                def emit(i, u):
                    for s in range(DS):
                        if s == 0 and live(i, 0):
                            at(dve, S["prep_ps"], USES * (i - 1) + 1)
                            for k in range(G * TC):
                                c = i * (G * TC) + k
                                last = nc.vector.tensor_scalar(xn[:, k, :], Hr[:, ds(c * D, D)], core.rstd[:, ds(c, 1)], core.nmr[:, ds(c, 1)],
                                                               ALU.mult, ALU.add)
                            last.then_inc(S["xn_ready"], 1)
                        if live(i, 1):
                            scan(i - 1, s)
                        if s == 0 and live(i, 2):
                            j, par = i - 2, u
                            dve.wait_ge(S["summed"], DS * (j + 1))
                            at(dve, S["out_ps"], j)
                            for c in range(C2):
                                last = stt(out=yg[:, c, :], in0=xc[par][:, 0, c, :], scalar=Wt["D"][:, 0, c, :], in1=YP[:, c, :], op0=ALU.mult, op1=ALU.add)
                            last.then_inc(S["y_read"], 1)
                            dve.wait_ge(S["y_read"], j + 1)
                            for c in range(C2):
                                last = stt(out=yg[:, c, :], in0=xc[par][:, 1, c, :], scalar=Wt["D"][:, 1, c, :], in1=yg[:, c, :], op0=ALU.mult, op1=ALU.add)
                            last.then_inc(S["y_skip"], 1)
                        if s in (9, 12) and live(i, 0):
                            d = (s - 9) // 3
                            use = USE["bc", d]
                            n = DIRS * i + d
                            dve.wait_ge(S["prep_ps"], USES * i + use + 1)
                            at(dve, S["C_ps"], DIRS * DS * (i - 1))
                            psb = PR[0:BC, use % 2, :]
                            nc.vector.tensor_copy(bcs[u][0:BC, d, :], psb).then_inc(S["bc_part1"], 1)
                            dve.wait_ge(S["bc_part1"], n + 1)
                            tt(rest[:], psb, bcs[u][0:BC, d, :], ALU.subtract).then_inc(S["bc_rest"], 1)
                            dve.wait_ge(S["bc_rest"], n + 1)
                            nc.vector.tensor_copy(part2[:], rest[:]).then_inc(S["bc_part2"], 1)
                            dve.wait_ge(S["bc_part2"], n + 1)
                            nc.vector.tensor_copy(bcs[u][BC:2 * BC, d, :], part2[:]).then_inc(read(use), 1)
                            tt(bcs[u][2 * BC:3 * BC, d, :], rest[:], part2[:], ALU.subtract).then_inc(S["bc_ready"], 1)
                        if s in (10, 13) and live(i, 0):
                            d = (s - 10) // 3
                            n = DIRS * i + d
                            dve.wait_ge(S["ln_done"], n + 1)
                            stt(out=flat(e_one[:]), in0=flat(e_one[:]), scalar=-1.0, in1=flat(e_abs[:, d]), op0=ALU.add, op1=ALU.subtract).then_inc(S["corr_done"], 1)
                            dve.wait_ge(S["corr_done"], n + 1)
                            tt(flat(e_ln[:]), flat(e_ln[:]), flat(e_one[:]), ALU.subtract).then_inc(S["ln_corr"], 1)
                            dve.wait_ge(S["ln_corr"], n + 1)
                            tt(flat(dt[u][:, d]), flat(dt[u][:, d]), flat(e_ln[:]), ALU.add).then_inc(S["dt_ready"], 1)
                        if s == 15 and live(i, 2):
                            j = i - 2
                            dve.wait_ge(S["out_read"], j + 1)
                            for k in range(G * TC):
                                c = j * (G * TC) + k
                                last = nc.vector.bn_stats(core.st[:, ds(c, 1), :].rearrange("p n k -> p (n k)"), o[:, k, :])
                            last.then_inc(S["stats_done"], 1)
                rolled(dve, NP, 2, 3, emit, ring=2)
                dve.wait_ge(S["stats_done"], NP)

            @block.tensor
            def _(pe):
                mm = nc.tensor.matmul

                def b_rows(j, par, s, d):
                    if s == 0:
                        pe.wait_ge(S["bc_ready"], DIRS * j + (d + 1))
                    at(pe, S["B_ready"], DIRS * (j * DS + s - 1) + (d + 1))
                    mm(BP[:, d, :], Wt["sel"][:, s, :], bcs[par][:, d, :], start=True, stop=True).then_inc(S["B_ps"], 1)

                def c_rows(j, par, s, d):
                    n = j * DS + s
                    at(pe, S["part_ready"], DIRS * (n - 1) + (d + 1))
                    mm(CP[:, d, :], Wt["sel"][:, DS + s, :], bcs[par][:, d, :], start=True, stop=True).then_inc(S["C_ps"], 1)

                def add_up(j, s):
                    pe.wait_ge(S["part_ready"], DIRS * (j * DS + (s + 1)))
                    if s == 0:
                        at(pe, S["y_read"], j)
                    for c in range(C2):
                        for d in range(DIRS):
                            last = mm(YP[:, c, :], core.ident[:], R[:, s % 4, d, c, :], start=(s == 0 and d == 0), stop=(s == DS - 1 and d == 1))
                    last.then_inc(S["summed"], 1)

                def prep(i, u, what, first, end):
                    use = USE[what]
                    bank = PR[:, use % 2, :]
                    kind, of = what[0], what[1:]
                    if first == 0:
                        at(pe, read(use), BANK_USES[use % 2] * i + use // 2)
                        if use == 1:
                            pe.wait_ge(read(0), BANK_USES[0] * i + 1)
                            at(pe, S["out_read"], i - 2)
                        if kind == "x":
                            pe.wait_ge(S["xn_ready"], i + 1)
                        if kind in ("dt", "bc"):
                            pe.wait_ge(S["silu_done"], DIRS * i + (of[0] + 1))
                    for k in range(first, end):
                        if kind == "x":
                            for t in range(G * TC):
                                last = nc.tensor.transpose(bank[:, t * P:(t + 1) * P], xn[:, t, :], core.ident[:])
                        if kind == "conv":
                            d, c = of
                            off = k if d == 0 else 2 * (DC - 1) - k
                            last = mm(bank, Wt["taps"][:, d, c, k, :], xT[:, :, off:off + T], start=(k == 0), stop=(k == DC - 1))
                        if kind == "z":
                            last = mm(bank, Wt["z"][:, of[0], :], xT[:, :, DC - 1:DC - 1 + T], start=True, stop=True)
                        if kind == "bc":
                            last = mm(bank[0:BC], Wt["bc"][:, of[0], k, :], xc[u][:, of[0], k, :], start=(k == 0), stop=(k == C2 - 1))
                        if kind == "dt":
                            d, c2 = of
                            last = mm(bank, Wt["dt"][:, d, k, c2, :], xc[u][:, d, k, :], start=(k == 0), stop=(k == C2 - 1))
                    if end == {"x": 1, "conv": DC, "z": 1, "bc": C2, "dt": C2}[kind]:
                        last.then_inc(S["prep_ps"], 1)

                def emit(i, u):
                    for s in range(DS):
                        if live(i, 1):
                            for d in range(DIRS):
                                c_rows(i - 1, (u + 1) % 2, s, d)
                        if of(i, u, s + 2):
                            for d in range(DIRS):
                                b_rows(*of(i, u, s + 2), d)
                        if live(i, 1) and s > 0:
                            add_up(i - 1, s - 1)
                        if s == 0 and live(i, 2):
                            add_up(i - 2, DS - 1)
                        if live(i, 0):
                            for part in PREP_AT.get(s, ()):
                                prep(i, u, part[:-2], *part[-2:])
                        if s == 14 and live(i, 2):
                            j = i - 2
                            pe.wait_ge(S["gated"], j + 1)
                            if live(i, 0):
                                pe.wait_ge(read(1), BANK_USES[1] * (i + 1))
                            for k in range(G * TC):
                                for c in range(C2):
                                    last = mm(PR[:, 1, k * D:(k + 1) * D], yg[:, c, k * P:(k + 1) * P], Wt["out"][:, c, :], start=(c == 0), stop=(c == C2 - 1))
                            last.then_inc(S["out_ps"], 1)
                rolled(pe, NP, 2, 3, emit, ring=2)


GRID = 8
KT = 4
KB = KT // TC
TURN = float(np.nextafter(np.float32(2 * np.pi), np.float32(0)))
MAGIC = 1.5 * 2.0 ** 23
NBASIS = 16
B_S1, B_C1, B_S2, B_D, B_DS1, B_DC1, B_DS2, B_E, B_ES1, B_EC1, B_ES2, B_ED, B_EDS1, B_EDC1, B_EDS2, B_EE = range(NBASIS)
COS, SIN = 0, 1
KAN_TERMS = {
    B_S1: (1.0, [(1, SIN, 1), (1, SIN, 3), (1, SIN, 5), (1, SIN, 7)]), B_DS1: (1.0, [(1, SIN, 3), (1, SIN, 5)]),
    B_ES1: (1.0, [(1, SIN, 5), (1, SIN, 7)]), B_EDS1: (1.0, [(1, SIN, 7)]),
    B_C1: (1.0, [(1, COS, 1), (-1, COS, 3), (1, COS, 5), (-1, COS, 7)]), B_DC1: (1.0, [(1, COS, 3), (-1, COS, 5)]),
    B_EC1: (1.0, [(1, COS, 5), (-1, COS, 7)]), B_EDC1: (1.0, [(1, COS, 7)]),
    B_S2: (2.0, [(1, SIN, 2), (1, SIN, 6)]), B_ES2: (2.0, [(1, SIN, 6)]), B_DS2: (2.0, [(1, SIN, 4)]), B_EDS2: (2.0, [(1, SIN, 8)]),
    B_D: (0.5, [(1, COS, 2), (-1, COS, 6)]), B_ED: (0.5, [(1, COS, 6)]), B_E: (0.5, [(1, COS, 4)]), B_EE: (0.5, [(1, COS, 8)]),
}


def kan_weights(core, WT, const):
    nc, aps = core.nc, core.aps
    tmp = ExitStack()
    with tmp:
        coef = core.sbuf("kw_coef", [P, 2, D * GRID], on=tmp)
        comb = core.sbuf("kw_combined", [P, NBASIS, D], on=tmp)
        minus2 = core.sbuf("kw_minus_two", [P, P], on=tmp)
        ps = core.psum("kw_ps", [P, NBASIS // 4 + 1, 512], on=tmp)
        s_in, s_comb, s_ps, s_wt, s_const = (core.sem(f"kw_{n}") for n in ("loaded", "combined", "ps", "kept", "const"))
        with nc.Block() as block:
            @block.sync
            def _(sp):
                sp.dma_start(coef[:], aps["L1_attn_kan_coef"].rearrange("p j i k -> j p (i k)")).then_inc(s_in, 16)

            @block.vector
            def _(dve):
                chain = Chain(core, dve, "kw_dve_chain")
                raw = lambda kind, k: coef[:, kind, :].rearrange("p (i k) -> p i k", k=GRID)[:, :, k - 1]
                nc.vector.memset(minus2[:], -2.0)
                dve.wait_ge(s_in, 16)
                depth = max(len(terms) for _, terms in KAN_TERMS.values())
                for n in range(depth):
                    for m, (factor, terms) in KAN_TERMS.items():
                        if n == 0:
                            last = nc.vector.tensor_scalar(comb[:, m, :], raw(*terms[0][1:]), factor, None, ALU.mult)
                        elif n < len(terms):
                            sign, kind, k = terms[n]
                            last = nc.vector.scalar_tensor_tensor(out=comb[:, m, :], in0=raw(kind, k), scalar=sign * factor, in1=comb[:, m, :],
                                                                  op0=ALU.mult, op1=ALU.add)
                    chain.step(last)
                nc.vector.tensor_copy(minus2[0:1, 0:1], minus2[0:1, 0:1]).then_inc(s_comb, 1)
                dve.wait_ge(s_ps, 1)
                nc.vector.tensor_copy(WT[:].rearrange("p m j -> p (m j)"), ps[:, 0:NBASIS // 4, :].rearrange("p m j -> p (m j)")).then_inc(s_wt, 1)
                dve.wait_ge(s_const, 1)
                chain.step(nc.vector.tensor_copy(const[:], ps[:, NBASIS // 4, 0:D]))

            @block.tensor
            def _(pe):
                pe.wait_ge(s_comb, 1)
                for m in range(NBASIS):
                    last = nc.tensor.transpose(ps[:, m // 4, (m % 4) * P:(m % 4 + 1) * P], comb[:, m, :], core.ident[:])
                last.then_inc(s_ps, 1)
                pe.wait_ge(s_wt, 1)
                nc.tensor.matmul(ps[:, NBASIS // 4, 0:D], minus2[:], WT[:, B_EE, :], start=True, stop=True).then_inc(s_const, 1)


def kan(core, Hr, OD, x_back):
    nc, NT, X, aps = core.nc, core.NT, core.X, core.aps
    NG, W4 = NT // KT, KT * P
    live = lambda i, lag: not isinstance(i, int) or 0 <= i - lag < NG
    on = ExitStack()
    with on:
        sb = lambda name, shape, dt=F32: core.sbuf("k_" + name, shape, dt, on=on)
        WT, const = sb("coef_T", [P, NBASIS, D]), sb("constant", [P, D])
        kan_weights(core, WT, const)
        ln = sb("ln_cols", [P, 2])
        quarter = sb("half_pi", [P, 1])
        od = [sb(f"od{n}", [P, KT, D]) for n in range(2)]
        xn = sb("xn", [P, KT, D])
        f, whole, t, at_ = sb("turns", [P, W4]), sb("whole", [P, W4]), sb("angle", [P, W4]), sb("abs_angle", [P, W4])
        q = sb("squares", [P, W4])
        basis = [sb(f"basis{n}", [P, NBASIS, W4]) for n in range(2)]
        gate = [sb(f"gate{n}", [P, KB, D]) for n in range(2)]
        hb, y1, y2 = (sb(n, [P, W4]) for n in ("h_const", "y_plus_h", "y_gated"))
        psT = core.psum("k_psT", [P, W4], on=on)
        psY = core.psum("k_psY", [P, 2, W4], on=on)
        S = {n: core.sem("k_" + n) for n in (
            "ln_loaded", "ln_ready", "od_loaded", "gate_loaded", "xn_ready", "xT_ps", "f_ready", "rounded", "reduced", "sin_done", "abs_done",
            "cos_done", "q_ready", "s2_done", "D_ready", "D_products", "D_square", "E_ready", "E_products", "E_square",
            "products", "hb_ready", "y1_ready", "gated", "x_updated", "stats", "passed")}
        with nc.Block() as block:
            @block.sync
            def _(sp):
                for n, name in enumerate(("g", "b")):
                    sp.dma_start(ln[:, n:n + 1], aps[f"L1_attn_ln_{name}"].rearrange("(p n) -> p n", n=1)).then_inc(S["ln_loaded"], 16)

                def emit(i, u):
                    if live(i, 0):
                        at_alone(sp, S["od_loaded"], 16 * i, S["passed"])
                        at(sp, S["xn_ready"], i - 1)
                        sp.dma_start(od[u][:], OD[ds(i * KT, KT)].rearrange("n p d -> p n d")).then_inc(S["od_loaded"], 16)
                    if live(i, 1):
                        j = i - 1
                        at_alone(sp, S["gate_loaded"], 16 * j, S["passed"])
                        at(sp, S["gated"], j - 1)
                        sp.dma_start(gate[(u + 1) % 2][:], core.modrow[2, ds(j * KB, KB), :].partition_broadcast(P)).then_inc(S["gate_loaded"], 16)
                rolled(sp, NG, 2, 3, emit, ring=2)

            @block.vector
            def _(dve):
                tt, ts = nc.vector.tensor_tensor, nc.vector.tensor_scalar
                nc.vector.memset(quarter[:], float(np.pi / 2))
                dve.wait_ge(S["ln_loaded"], 32)
                ts(ln[:], ln[:], float(1 / (2 * np.pi)), None, ALU.mult).then_inc(S["ln_ready"], 1)

                def new_stats(j):
                    dve.wait_ge(S["x_updated"], j + 1)
                    for k in range(KT):
                        last = tile_stats(core, X, j * KT + k)
                    last.then_inc(S["stats"], 1)

                def emit(i, u):
                    if live(i, 0):
                        bs = basis[u]
                        dve.wait_ge(S["od_loaded"], 16 * (i + 1))
                        at(dve, S["xT_ps"], i)
                        for k in range(KT):
                            c = i * KT + k
                            last = ts(xn[:, k, :], od[u][:, k, :], core.rstd[:, ds(c, 1)], core.nmr[:, ds(c, 1)], ALU.mult, ALU.add)
                        last.then_inc(S["xn_ready"], 1)
                        dve.wait_ge(S["f_ready"], i + 1)
                        ts(whole[:], f[:], MAGIC, MAGIC, ALU.add, ALU.subtract).then_inc(S["rounded"], 1)
                        dve.wait_ge(S["rounded"], i + 1)
                        tt(t[:], f[:], whole[:], ALU.subtract).then_inc(S["reduced"], 1)
                        dve.wait_ge(S["cos_done"], i + 1)
                        tt(bs[:, B_S2, :], bs[:, B_S1, :], bs[:, B_C1, :], ALU.mult).then_inc(S["s2_done"], 1)
                        dve.wait_ge(S["q_ready"], i + 1)
                        ts(bs[:, B_D, :], q[:], -2.0, 2.0, ALU.mult, ALU.add).then_inc(S["D_ready"], 1)
                        dve.wait_ge(S["s2_done"], i + 1)
                        dve.wait_ge(S["D_ready"], i + 1)
                        tt(bs[:, B_DS1:B_DS2 + 1, :], bs[:, B_S1:B_S2 + 1, :], bs[:, B_D, :].unsqueeze(1).broadcast_to([P, 3, W4]), ALU.mult)\
                            .then_inc(S["D_products"], 1)
                        dve.wait_ge(S["D_square"], i + 1)
                        ts(bs[:, B_E, :], q[:], -2.0, None, ALU.add).then_inc(S["E_ready"], 1)
                        dve.wait_ge(S["E_ready"], i + 1)
                        dve.wait_ge(S["D_products"], i + 1)
                        tt(bs[:, B_ES1:B_EDS2 + 1, :], bs[:, B_S1:B_DS2 + 1, :], bs[:, B_E, :].unsqueeze(1).broadcast_to([P, 7, W4]), ALU.mult)\
                            .then_inc(S["E_products"], 1)
                    if live(i, 3):
                        new_stats(i - 3)
                    if live(i, 2):
                        j = i - 2
                        dve.wait_ge(S["products"], j + 1)
                        dve.wait_ge(S["hb_ready"], j + 1)
                        at(dve, S["gated"], j)
                        tt(y1[:], psY[:, u, :], hb[:], ALU.add).then_inc(S["y1_ready"], 1)
                rolled(dve, NG, 2, 3, emit, ring=2)
                new_stats(NG - 1)
                dve.wait_ge(S["stats"], NG)

            @block.scalar
            def _(act):
                func = nc.scalar.activation
                act.wait_ge(S["ln_ready"], 1)

                def emit(i, u):
                    if live(i, 0):
                        bs = basis[u]
                        act.wait_ge(S["xT_ps"], i + 1)
                        at(act, S["reduced"], i)
                        func(f[:], psT[:], ACT.Identity, scale=ln[:, 0:1], bias=ln[:, 1:2]).then_inc(S["f_ready"], 1)
                        act.wait_ge(S["reduced"], i + 1)
                        at(act, S["products"], i - 1)
                        func(bs[:, B_S1, :], t[:], ACT.Sin, scale=TURN).then_inc(S["sin_done"], 1)
                        at(act, S["cos_done"], i)
                        func(at_[:], t[:], ACT.Abs).then_inc(S["abs_done"], 1)
                        act.wait_ge(S["abs_done"], i + 1)
                        func(bs[:, B_C1, :], at_[:], ACT.Sin, scale=-TURN, bias=quarter[:, 0:1]).then_inc(S["cos_done"], 1)
                        act.wait_ge(S["sin_done"], i + 1)
                        at(act, S["E_ready"], i)
                        func(q[:], bs[:, B_S1, :], ACT.Square, scale=float(np.sqrt(2))).then_inc(S["q_ready"], 1)
                        act.wait_ge(S["D_ready"], i + 1)
                        func(q[:], bs[:, B_D, :], ACT.Square).then_inc(S["D_square"], 1)
                        act.wait_ge(S["E_ready"], i + 1)
                        func(bs[:, B_EE, :], bs[:, B_E, :], ACT.Square).then_inc(S["E_square"], 1)
                rolled(act, NG, 2, 3, emit, ring=2)

            @block.tensor
            def _(pe):
                def emit(i, u):
                    if live(i, 0):
                        pe.wait_ge(S["xn_ready"], i + 1)
                        at(pe, S["f_ready"], i)
                        for k in range(KT):
                            last = nc.tensor.transpose(psT[:, k * P:(k + 1) * P], xn[:, k, :], core.ident[:])
                        last.then_inc(S["xT_ps"], 1)
                    if live(i, 1):
                        j, n = i - 1, (u + 1) % 2
                        pe.wait_ge(S["E_products"], j + 1)
                        pe.wait_ge(S["E_square"], j + 1)
                        at(pe, S["y1_ready"], j - 1)
                        for k in range(KT):
                            for m in range(NBASIS):
                                last = nc.tensor.matmul(psY[:, n, k * D:(k + 1) * D], basis[n][:, m, k * P:(k + 1) * P], WT[:, m, :],
                                                        start=(m == 0), stop=(m == NBASIS - 1))
                        last.then_inc(S["products"], 1)
                rolled(pe, NG, 2, 3, emit, ring=2)

            @block.gpsimd
            def _(pool):
                tt = nc.gpsimd.tensor_tensor
                pool.wait_ge(x_back, 16)

                def emit(i, u):
                    if live(i, 2):
                        j, n = i - 2, u
                        at(pool, S["y1_ready"], j)
                        tt(hb[:].rearrange("p (n d) -> p n d", d=D), Hr[:, ds(j * W4, W4)].rearrange("p (n d) -> p n d", d=D),
                           const[:].unsqueeze(1).broadcast_to([P, KT, D]), ALU.add).then_inc(S["hb_ready"], 1)
                        pool.wait_ge(S["gate_loaded"], 16 * (j + 1))
                        pool.wait_ge(S["y1_ready"], j + 1)
                        at(pool, S["x_updated"], j)
                        tt(y2[:].rearrange("p (b n d) -> p b n d", b=KB, d=D), y1[:].rearrange("p (b n d) -> p b n d", b=KB, d=D),
                           gate[n][:].unsqueeze(2).broadcast_to([P, KB, TC, D]), ALU.mult).then_inc(S["gated"], 1)
                        pool.wait_ge(S["gated"], j + 1)
                        x = X[:, ds(j * W4, W4)]
                        tt(x, x, y2[:], ALU.add).then_inc(S["x_updated"], 1)
                rolled(pool, NG, 2, 3, emit, ring=2)


def layer1_attention(core):
    OD = core.nc.dram_tensor("mixer_out", [core.NT, P, D], F32, kind="Internal").ap()
    on = ExitStack()
    with on:
        Hr = core.sbuf("h_rows1", [P, core.NT * D], on=on)
        xsave = core.nc.dram_tensor("x_saved", [P, core.NT * D], F32, kind="Internal").ap()
        x_saved, x_back = core.sem("x_saved"), core.sem("x_back")
        with core.nc.Block() as block:
            @block.sync
            def _(sp):
                sp.dma_start(xsave, core.X[:, 0:core.NT * D]).then_inc(x_saved, 16)
        norm_stats(core, "lnC")
        modulated(core, 1, Hr, None, 8)
        norm_stats(core, "lnC1", 1e-12)
        mixer(core, Hr, OD, x_saved)
        with core.nc.Block() as block:
            @block.sync
            def _(sp):
                sp.dma_start(core.X[:, 0:core.NT * D], xsave).then_inc(x_back, 16)
        norm_stats(core, "lnC2", 1e-12)
        kan(core, Hr, OD, x_back)


def experts1(core, W, ahead, XS, YS):
    nc, aps = core.nc, core.aps
    on = ExitStack()
    with on:
        sb = lambda name, shape, dt=F32: core.sbuf("e1_" + name, shape, dt, on=on)
        w1, w2, b1, b2 = W
        x = [sb(f"x{n}", [CAP, D]) for n in range(2)]
        xT = sb("xT", [P, CAP])
        h1, g = sb("h1", [CAP, F]), sb("gelu", [CAP, F])
        gT = sb("gelu_T", [P, FC, CAP])
        y = [sb(f"y{n}", [CAP, D]) for n in range(2)]
        psX, ps1, psY = (core.psum("e1_ps" + n, [P, 512], on=on) for n in "X1Y")
        psG = core.psum("e1_psG", [P, FC, P], on=on)
        S = start_counts(core, "e1", ["x_loaded", "xT_ps", "xT_ready", "h1_ps", "h1_ready", "gelu_ready", "gT_ps", "gT_ready",
                                      "y_ps", "y_ready", "y_stored"])
        live = lambda i, lag: not isinstance(i, int) or 0 <= i - lag < E
        slots_of = lambda table, e: table[ds(e * CAP, CAP), :]
        of = lambda t, e: t[:, ds(e, 1)].rearrange("p n f -> p (n f)")

        with nc.Block() as block:
            @block.sync
            def _(sp):
                def emit(i, u):
                    if live(i, 0):
                        upto(sp, S["x_loaded"], 16 * i)
                        upto(sp, S["xT_ps"], i - 1)
                        sp.dma_start(x[u][:], slots_of(XS, i)).then_inc(S["x_loaded"], 16)
                    if live(i, 1):
                        j = i - 1
                        upto(sp, S["y_ready"], j + 1)
                        upto(sp, S["y_stored"], 16 * j)
                        sp.dma_start(slots_of(YS, j), y[(u + 1) % 2][:]).then_inc(S["y_stored"], 16)
                rolled(sp, E, 1, 2, emit, ring=2)
                upto(sp, S["y_stored"], 16 * E)

            @block.tensor
            def _(pe):
                mm = nc.tensor.matmul
                pe.wait_ge(ahead.loaded, ahead.loads)

                def emit(i, u):
                    if live(i, 0):
                        upto(pe, S["x_loaded"], 16 * (i + 1))
                        upto(pe, S["xT_ready"], i)
                        nc.tensor.transpose(psX[:, 0:CAP], x[u][:], core.ident[0:CAP, 0:CAP]).then_inc(S["xT_ps"], 1)
                    if live(i, 1):
                        j = i - 1
                        upto(pe, S["gelu_ready"], j + 1)
                        upto(pe, S["gT_ready"], j)
                        for c in range(FC):
                            last = nc.tensor.transpose(psG[:, c, 0:CAP], g[:, c * P:(c + 1) * P], core.ident[0:CAP, 0:CAP])
                        last.then_inc(S["gT_ps"], 1)
                    if live(i, 0):
                        upto(pe, S["xT_ready"], i + 1)
                        upto(pe, S["h1_ready"], i)
                        mm(ps1[0:CAP, :], xT[:], of(w1, i), start=True, stop=True).then_inc(S["h1_ps"], 1)
                    if live(i, 1):
                        upto(pe, S["gT_ready"], j + 1)
                        upto(pe, S["y_ready"], j)
                        for c in range(FC):
                            last = mm(psY[0:CAP, 0:D], gT[:, c, :], w2[:, ds(j, 1), c, :].rearrange("p n d -> p (n d)"), start=(c == 0), stop=(c == FC - 1))
                        last.then_inc(S["y_ps"], 1)
                rolled(pe, E, 1, 2, emit, ring=2)

            @block.scalar
            def _(act):
                def emit(i, u):
                    if live(i, 1):
                        j = i - 1
                        upto(act, S["gT_ps"], j + 1)
                        upto(act, S["y_ps"], j)
                        nc.scalar.activation(gT[:], psG[:, :, 0:CAP], ACT.Copy).then_inc(S["gT_ready"], 1)
                    if live(i, 0):
                        upto(act, S["h1_ready"], i + 1)
                        upto(act, S["gT_ps"], i)
                        nc.scalar.activation(g[:], h1[:], ACT.Gelu_apprx_tanh).then_inc(S["gelu_ready"], 1)
                rolled(act, E, 1, 2, emit, ring=2)

            @block.vector
            def _(dve):
                dve.wait_ge(ahead.loaded, ahead.loads)

                def emit(i, u):
                    if live(i, 0):
                        upto(dve, S["xT_ps"], i + 1)
                        upto(dve, S["h1_ps"], i)
                        nc.vector.tensor_copy(xT[:], psX[:, 0:CAP]).then_inc(S["xT_ready"], 1)
                        upto(dve, S["h1_ps"], i + 1)
                        upto(dve, S["gelu_ready"], i)
                        nc.vector.tensor_tensor(h1[:], ps1[0:CAP, :], of(b1, i)[0:CAP], ALU.add).then_inc(S["h1_ready"], 1)
                    if live(i, 1):
                        j = i - 1
                        upto(dve, S["y_ps"], j + 1)
                        upto(dve, S["y_stored"], 16 * (j - 1))
                        nc.vector.tensor_tensor(y[(u + 1) % 2][:], psY[0:CAP, 0:D], of(b2, j)[0:CAP], ALU.add).then_inc(S["y_ready"], 1)
                rolled(dve, E, 1, 2, emit, ring=2)


def ffn1(core):
    nc, aps, NT = core.nc, core.aps, core.NT
    rows = E * CAP
    XS = nc.dram_tensor("slot_inputs1", [rows, D], F32, kind="Internal").ap()
    YS = nc.dram_tensor("slot_outputs1", [(rows // P + 1) * P, D], F32, kind="Internal").ap()
    on = ExitStack()
    with on:
        slots, weights = [core.sbuf("slots1", [P, NT], U32, on=on)], [core.sbuf("weights1", [P, NT], on=on)]
        w1, w2, b1, b2 = (core.sbuf(f"e1_{n}", [P, E, w], on=on) for n, w in (("w1", F), ("w2", F), ("b1", F), ("b2", D)))
        ahead = Ahead(core, "e1", [(w1[:], aps["L1_ffn_w1"].rearrange("e d f -> d e f")),
                                   (w2[:].rearrange("p e (c d) -> p (e c) d", d=D), aps["L1_ffn_w2"].rearrange("e (c f) d -> f (e c) d", f=P)),
                                   (b1[:], aps["L1_ffn_b1"].partition_broadcast(P)), (b2[:], aps["L1_ffn_b2"].partition_broadcast(P))],
                      [(XS, rows // P), (YS, rows // P + 1)], on=on)
        w2 = w2[:].rearrange("p e (c d) -> p e c d", d=D)
        scratch = ExitStack()
        with scratch:
            Hr = core.sbuf("h_rows2", [P, NT * D], on=scratch)
            L = core.sbuf("logits1", [P, NT * E], on=scratch)
            norm_stats(core, "lnD")
            modulated(core, 1, Hr, L, 6)
            moe_route(core, 1, L, slots, weights)
            scatter_rows(core, "sc1", Hr, slots, XS, rows, ahead)
        experts1(core, (w1, w2, b1, b2), ahead, XS, YS[0:rows, :])
        gather_and_add(core, "ga1", 1, slots, weights, YS, stats=False)


def store_x(core):
    with core.nc.Block() as block:
        s_stored = core.sem("out_stored")

        @block.sync
        def _(sp):
            sp.dma_start(core.aps["out_tiles"].rearrange("n p d -> p n d"), core.X[:, 0:core.NT * D].rearrange("p (n d) -> p n d", d=D))\
                .then_inc(s_stored, 16)
            sp.wait_ge(s_stored, 16)


def adaln_two_layers(nc, aps, B):
    core = Core(nc, aps, B)
    with core.stack:
        load_and_modulate(core)
        norm_stats(core, "lnA")
        attention(core)
        ffn0(core)
        core.next_stage()
        layer1_attention(core)
        core.next_stage()
        ffn1(core)
        store_x(core)


def shape_constants():
    out = {"ident": np.eye(P, dtype=np.float32)}
    inv_freq = (1.0 / (np.float32(10000.0) ** (np.arange(0, DH, 2, dtype=np.float32) / np.float32(DH)))).astype(np.float32)
    freqs = np.arange(T, dtype=np.float32)[:, None] * inv_freq[None, :]
    emb = np.concatenate([freqs, freqs], -1)
    out["rope_cos"] = np.tile(np.cos(emb).astype(np.float32).T, (H, 1))
    out["rope_sin"] = np.tile(np.sin(emb).astype(np.float32).T, (H, 1))
    rot = np.zeros((D, D), np.float32)
    for m in range(D):
        half = DH // 2
        rot[m + half if m % DH < half else m - half, m] = -1 if m % DH < half else 1
    out["rope_rot"] = rot
    out["selector"] = np.tile(np.eye(BC, dtype=np.float32), (PARTS, 1))
    out["rev_rank"] = np.tile(np.arange(E, 0, -1, dtype=np.float32), (P, 1))
    out["tri"] = np.triu(np.ones((P, P), np.float32))
    return out


def kernel(**inputs):
    import concourse.bacc as bacc
    from concourse.bass_utils import run_bass_kernel_spmd

    arrays = {name: np.ascontiguousarray(a) for name, a in inputs.items()}
    x = arrays.pop("L0_attn_x")
    B = x.shape[0]
    arrays["x_tiles"] = x.reshape(B * TC, P, D)
    arrays.update({name: np.ascontiguousarray(a) for name, a in shape_constants().items()})
    nc = bacc.Bacc("TRN2", target_bir_lowering=False, num_devices=1)
    aps = {name: nc.dram_tensor(name, a.shape, mybir.dt.from_np(a.dtype), kind="ExternalInput").ap() for name, a in arrays.items()}
    aps["out_tiles"] = nc.dram_tensor("out_tiles", [B * TC, P, D], F32, kind="ExternalOutput").ap()
    adaln_two_layers(nc, aps, B)
    r = run_bass_kernel_spmd(nc, [arrays], core_ids=[0])
    return np.asarray(r.results[0]["out_tiles"]).reshape(x.shape)
```
